# Optimizing a Trainium2 kernel written in Bass

```python
import numpy as np
import jax
import jax.numpy as jnp

def _softmax(x, axis=-1):
    return jax.nn.softmax(x, axis=axis)

def _gelu(x):
    return jax.nn.gelu(x, approximate=True)

def _silu(x):
    return jax.nn.silu(x)

def _sigmoid(x):
    return jax.nn.sigmoid(x)

def _layernorm(x, axis=-1, eps=1e-05):
    m = jnp.mean(x, axis=axis, keepdims=True)
    v = jnp.var(x, axis=axis, keepdims=True)
    return (x - m) / jnp.sqrt(v + eps)

def _scatter_add(tgt, idx, src, axis=0):
    return tgt.at[idx].add(src)

def _segment_sum(src, seg, n):
    return jax.ops.segment_sum(src, seg, n)
kernel_name = 'mk_decoder_preln_d4_seqx_r8_2713af'

def setup_inputs(seed: int=0):
    np.random.seed(seed)
    _w = jnp.asarray

    def _rec_inputs():
        import jax
        import jax.numpy as jnp
        _rk = jax.random.key(seed)
        x = 7.22e-05 + 1 * jax.random.normal(jax.random.fold_in(_rk, 1), (16, 128, 256), jnp.float32)
        _lenS = 128 - jax.random.randint(jax.random.fold_in(_rk, 7), (16,), 0, max(1, 128 // 4) + 1, jnp.int32)
        _lenS2 = 128 - jax.random.randint(jax.random.fold_in(_rk, 8), (16,), 0, max(1, 128 // 4) + 1, jnp.int32)
        _ctx_2048P = jax.random.normal(jax.random.fold_in(_rk, 11), (16, 16, 256), jnp.float32)
        _ctx_2048c = jax.random.dirichlet(jax.random.fold_in(_rk, 511), 0.3 * jnp.ones((16,), jnp.float32), (16, 128))
        _ctx_2048t = jnp.einsum('bsk,bkd->bsd', _ctx_2048c, _ctx_2048P)
        _ctx_2048t = _ctx_2048t * jax.lax.rsqrt(jnp.mean(jnp.square(_ctx_2048t)) + 1e-12) * 0.953939
        ctx_2048 = 4.13588e-05 + 0.999923 * (_ctx_2048t + 0.3 * jax.random.normal(jax.random.fold_in(_rk, 611), (16, 128, 256), jnp.float32))
        _validS = jnp.arange(128)[None, :] < _lenS[:, None]
        _validS2 = jnp.arange(128)[None, :] < _lenS2[:, None]
        _causal = jnp.tril(jnp.ones((128, 128), dtype=bool))
        mask_1x1x2048x2048_if1 = jnp.where(jnp.ones((1, 1, 256, 256), dtype=bool), 1, 0).astype(jnp.int32)
        mask_BxS2_bk0 = jnp.logical_not(jnp.broadcast_to(_validS2[:, :], (16, 128)))
        return (x, ctx_2048, mask_1x1x2048x2048_if1, mask_BxS2_bk0)
    x, ctx_2048, mask_1x1x2048x2048_if1, mask_BxS2_bk0 = _rec_inputs()

    def _L0_attn_setup():
        import jax, jax.numpy as jnp
        import numpy as np
        B, N, H = (2, 512, 256)
        NH, HD = (16, 128)
        BLK = 32
        EPS = 1e-06

        def _lightning_attn(x, slope_rate, w_qkv, w_gate, w_out, norm_w):
            b, n, _ = x.shape
            h, d = (NH, HD)
            nb = n // BLK
            qkv = jax.nn.silu(jnp.einsum('bnf,of->bno', x, w_qkv))
            qkv = qkv.reshape(b, n, h, 3 * d)
            q, k, v = jnp.split(qkv, 3, axis=-1)
            q = q.transpose(0, 2, 1, 3)
            k = k.transpose(0, 2, 1, 3)
            v = v.transpose(0, 2, 1, 3)
            s = slope_rate.astype(jnp.float32)
            arr = jnp.arange(1, BLK + 1, dtype=jnp.float32)
            q_decay = jnp.exp(-s * arr[:, None])
            k_decay = jnp.exp(-s * (BLK - arr)[:, None])
            idx = arr[:, None] - arr[None, :]
            diag_decay = jnp.where(idx >= 0, jnp.exp(-s * idx), 0.0)
            block_decay = jnp.exp(-s * BLK)
            qb = q.reshape(b, h, nb, BLK, d).transpose(2, 0, 1, 3, 4)
            kb = k.reshape(b, h, nb, BLK, d).transpose(2, 0, 1, 3, 4)
            vb = v.reshape(b, h, nb, BLK, d).transpose(2, 0, 1, 3, 4)

            def step(kv, blk):
                qi, ki, vi = blk
                o_inter = jnp.einsum('bhmd,bhde->bhme', qi * q_decay, kv)
                qk = jnp.einsum('bhmd,bhnd->bhmn', qi, ki) * diag_decay
                o_intra = jnp.einsum('bhmn,bhne->bhme', qk, vi)
                kv_new = block_decay * kv + jnp.einsum('bhmd,bhme->bhde', ki * k_decay, vi)
                return (kv_new, o_inter + o_intra)
            kv0 = jnp.zeros((b, h, d, d), dtype=jnp.float32)
            _, out = jax.lax.scan(step, kv0, (qb, kb, vb))
            out = out.transpose(1, 2, 0, 3, 4).reshape(b, h, n, d)
            out = out.transpose(0, 2, 1, 3).reshape(b, n, h * d)
            var = jnp.mean(out * out, axis=-1, keepdims=True)
            out = norm_w * (out * jax.lax.rsqrt(var + EPS))
            gate = jax.nn.sigmoid(jnp.einsum('bnf,of->bno', x, w_gate))
            return jnp.einsum('bno,fo->bnf', gate * out, w_out)
        key = jax.random.key(seed)
        ks = jax.random.split(key, 5)
        scale = 0.02
        x = jax.random.normal(ks[0], (B, N, H), dtype=jnp.float32)
        slopes = (1.0 / 2.0 ** (8.0 * np.arange(1, NH + 1) / NH)).astype(np.float32)
        slope_rate = jnp.asarray(slopes).reshape(NH, 1, 1)
        w_qkv = jax.random.normal(ks[1], (3 * NH * HD, H), dtype=jnp.float32) * scale
        w_gate = jax.random.normal(ks[2], (NH * HD, H), dtype=jnp.float32) * scale
        w_out = jax.random.normal(ks[3], (H, NH * HD), dtype=jnp.float32) * scale
        norm_w = jnp.ones((NH * HD,), dtype=jnp.float32)
        return {'hidden_states': x, 'slope_rate': slope_rate, 'w_qkv': w_qkv, 'w_gate': w_gate, 'w_out': w_out, 'norm_w': norm_w}
    _L0_attn_all = _L0_attn_setup()
    _L0_attn_in = {k: v for k, v in _L0_attn_all.items() if k in ('slope_rate', 'w_qkv', 'w_gate', 'w_out', 'norm_w')}
    del _L0_attn_all

    def _L0_xattn_setup():
        import jax, jax.numpy as jnp
        import numpy as np
        import math
        CHANNELS = 128
        N_HEADS = 16
        K_CHANNELS = CHANNELS // N_HEADS
        ROPE_D = int(K_CHANNELS * 0.5)
        B, T = (4, 256)

        def apply_rope(x, d, base=10000.0):
            t = x.shape[2]
            theta = 1.0 / base ** (jnp.arange(0, d, 2, dtype=jnp.float32) / d)
            idx_theta = jnp.arange(t, dtype=jnp.float32)[:, None] * theta[None, :]
            idx_theta2 = jnp.concatenate([idx_theta, idx_theta], axis=-1)
            cos = jnp.cos(idx_theta2)[None, None, :, :]
            sin = jnp.sin(idx_theta2)[None, None, :, :]
            x_rope, x_pass = (x[..., :d], x[..., d:])
            d2 = d // 2
            neg_half = jnp.concatenate([-x_rope[..., d2:], x_rope[..., :d2]], axis=-1)
            x_rope = x_rope * cos + neg_half * sin
            return jnp.concatenate([x_rope, x_pass], axis=-1)
        key = jax.random.key(seed)
        ks = jax.random.split(key, 12)
        xavier = math.sqrt(6.0 / (CHANNELS + CHANNELS))
        inp = {'x': jax.random.normal(ks[0], (B, CHANNELS, T), dtype=jnp.float32), 'c': jax.random.normal(ks[1], (B, CHANNELS, T), dtype=jnp.float32), 'attn_mask': jnp.ones((1, 1, T, T), dtype=jnp.int32), 'wq': jax.random.uniform(ks[2], (CHANNELS, CHANNELS), jnp.float32, -xavier, xavier), 'bq': jnp.zeros((CHANNELS,), jnp.float32), 'wk': jax.random.uniform(ks[3], (CHANNELS, CHANNELS), jnp.float32, -xavier, xavier), 'bk': jnp.zeros((CHANNELS,), jnp.float32), 'wv': jax.random.uniform(ks[4], (CHANNELS, CHANNELS), jnp.float32, -xavier, xavier), 'bv': jnp.zeros((CHANNELS,), jnp.float32), 'wo': jax.random.normal(ks[5], (CHANNELS, CHANNELS), jnp.float32) * (1.0 / math.sqrt(CHANNELS)), 'bo': jnp.zeros((CHANNELS,), jnp.float32)}
        return inp
    _L0_xattn_all = _L0_xattn_setup()
    _L0_xattn_in = {k: v for k, v in _L0_xattn_all.items() if k in ('wq', 'bq', 'wk', 'bk', 'wv', 'bv', 'wo', 'bo')}
    del _L0_xattn_all

    def _L0_ffn_setup():
        import jax, jax.numpy as jnp
        import numpy as np
        HIDDEN = 256
        N_EXPERTS = 8
        N_SHARED = 2
        TOP_K = 2
        MOE_FF = 176
        SHARED_FF = N_SHARED * MOE_FF
        SCALE = 2.5
        BATCH, SEQ = (2, 128)
        key = jax.random.key(seed)
        ks = jax.random.split(key, 8)
        s = 0.02
        return {'hidden_states': jax.random.normal(ks[0], (BATCH, SEQ, HIDDEN), jnp.float32), 'gate_w': jax.random.normal(ks[1], (N_EXPERTS, HIDDEN), jnp.float32) * s, 'shared_wg': jax.random.normal(ks[2], (SHARED_FF, HIDDEN), jnp.float32) * s, 'shared_wu': jax.random.normal(ks[3], (SHARED_FF, HIDDEN), jnp.float32) * s, 'shared_wd': jax.random.normal(ks[4], (HIDDEN, SHARED_FF), jnp.float32) * s, 'exp_wg': jax.random.normal(ks[5], (N_EXPERTS, MOE_FF, HIDDEN), jnp.float32) * s, 'exp_wu': jax.random.normal(ks[6], (N_EXPERTS, MOE_FF, HIDDEN), jnp.float32) * s, 'exp_wd': jax.random.normal(ks[7], (N_EXPERTS, HIDDEN, MOE_FF), jnp.float32) * s}
    _L0_ffn_all = _L0_ffn_setup()
    _L0_ffn_in = {k: v for k, v in _L0_ffn_all.items() if k in ('gate_w', 'shared_wg', 'shared_wu', 'shared_wd', 'exp_wg', 'exp_wu', 'exp_wd')}
    del _L0_ffn_all

    def _L1_attn_setup():
        import jax, jax.numpy as jnp
        import numpy as np
        H = 8
        R = 2
        D = 128
        DEG = 2
        GATE_OFFSET = 6.906768

        def _power_attention(q, k, v, log_g):
            B, T, hq, d = q.shape
            scale = 1.0 / d ** 0.5
            k = jnp.repeat(k, R, axis=2)
            v = jnp.repeat(v, R, axis=2)
            logG = jnp.cumsum(log_g, axis=1)
            logG = jnp.repeat(logG, R, axis=2)
            logG = jnp.transpose(logG, (0, 2, 1))
            qk = jnp.einsum('bthd,bshd->bhts', q, k) * scale
            a = qk ** DEG
            gate = logG[:, :, :, None] - logG[:, :, None, :]
            causal = jnp.tril(jnp.ones((T, T), dtype=bool))
            a = jnp.where(causal, a * jnp.exp(gate), 0.0)
            norm = jnp.sum(a, axis=-1) + 1e-06
            y = jnp.einsum('bhts,bshd->bthd', a, v)
            y = y / jnp.transpose(norm, (0, 2, 1))[..., None]
            return y
        key = jax.random.key(seed)
        ks = jax.random.split(key, 7)
        B, T, C = (1, 256, 256)
        q_dim = H * R * D
        kv_dim = H * D
        s = 0.02
        return {'hidden_states': jax.random.normal(ks[0], (B, T, C), dtype=jnp.float32), 'Wq': jax.random.normal(ks[1], (C, q_dim), dtype=jnp.float32) * s, 'Wk': jax.random.normal(ks[2], (C, kv_dim), dtype=jnp.float32) * s, 'Wv': jax.random.normal(ks[3], (C, kv_dim), dtype=jnp.float32) * s, 'Wg': jax.random.normal(ks[4], (C, H), dtype=jnp.float32) * s, 'Wc': jax.random.normal(ks[5], (q_dim, C), dtype=jnp.float32) * s, 'bc': jnp.zeros((C,), dtype=jnp.float32)}
    _L1_attn_all = _L1_attn_setup()
    _L1_attn_in = {k: v for k, v in _L1_attn_all.items() if k in ('Wq', 'Wk', 'Wv', 'Wg', 'Wc', 'bc')}
    del _L1_attn_all

    def _L1_xattn_setup():
        import jax, jax.numpy as jnp
        import numpy as np
        HIDDEN = 256
        NUM_HEADS = 16
        NUM_KV_HEADS = 4
        HEAD_DIM = 128
        ROPE_THETA = 10000.0
        EPS = 1e-06

        def rms_norm(x, w, eps=EPS):
            var = jnp.mean(jnp.square(x), axis=-1, keepdims=True)
            return x * jax.lax.rsqrt(var + eps) * w

        def rope_cache(L, head_dim, theta, dtype):
            inv_freq = 1.0 / theta ** (jnp.arange(0, head_dim, 2, dtype=jnp.float32) / head_dim)
            t = jnp.arange(L, dtype=jnp.float32)
            freqs = jnp.outer(t, inv_freq)
            emb = jnp.concatenate([freqs, freqs], -1)
            cos = jnp.cos(emb).astype(dtype)[None, :, None, :]
            sin = jnp.sin(emb).astype(dtype)[None, :, None, :]
            return (cos, sin)

        def rotate_half(x):
            x1, x2 = jnp.split(x, 2, axis=-1)
            return jnp.concatenate([-x2, x1], axis=-1)
        key = jax.random.key(seed)
        ks = jax.random.split(key, 10)
        B, L, T = (2, 256, 64)
        q_out = NUM_HEADS * HEAD_DIM
        kv_out = NUM_KV_HEADS * HEAD_DIM
        s = lambda fan_in: 1.0 / np.sqrt(fan_in)
        return {'x': jax.random.normal(ks[0], (B, L, HIDDEN), jnp.float32), 'h_ctx_kv': jax.random.normal(ks[1], (B, T, HIDDEN), jnp.float32), 'wq': jax.random.normal(ks[2], (HIDDEN, q_out), jnp.float32) * s(HIDDEN), 'wk': jax.random.normal(ks[3], (HIDDEN, kv_out), jnp.float32) * s(HIDDEN), 'wv': jax.random.normal(ks[4], (HIDDEN, kv_out), jnp.float32) * s(HIDDEN), 'wo': jax.random.normal(ks[5], (q_out, HIDDEN), jnp.float32) * s(q_out), 'wk_ctx': jax.random.normal(ks[6], (HIDDEN, kv_out), jnp.float32) * s(HIDDEN), 'wv_ctx': jax.random.normal(ks[7], (HIDDEN, kv_out), jnp.float32) * s(HIDDEN), 'q_norm_w': jnp.ones((HEAD_DIM,), jnp.float32), 'k_norm_w': jnp.ones((HEAD_DIM,), jnp.float32)}
    _L1_xattn_all = _L1_xattn_setup()
    _L1_xattn_in = {k: v for k, v in _L1_xattn_all.items() if k in ('wq', 'wk', 'wv', 'wo', 'wk_ctx', 'wv_ctx', 'q_norm_w', 'k_norm_w')}
    del _L1_xattn_all

    def _L1_ffn_setup():
        import jax, jax.numpy as jnp
        import numpy as np
        B, L, D = (2, 128, 256)
        E, TOP_K, RANK, DFF = (8, 2, 8, 688)

        def _lora(x, A, Bm, scale):
            return x @ A @ Bm * scale

        def _expert_lora(x, A, Bm, w, scale):
            xA = jnp.einsum('bld,edr->bler', x, A)
            xAB = jnp.einsum('bler,erd->bled', xA, Bm) * scale
            return (xAB * w).sum(axis=2)
        key = jax.random.key(seed)
        ks = jax.random.split(key, 18)
        r = lambda k, s, sc: jax.random.normal(k, s, dtype=jnp.float32) * sc
        inv_d = 1.0 / np.sqrt(D)
        inv_f = 1.0 / np.sqrt(DFF)
        return {'x': r(ks[0], (B, L, D), 1.0), 'W_router': r(ks[1], (D, E), inv_d), 'W_gate': r(ks[2], (D, DFF), inv_d), 'W_up': r(ks[3], (D, DFF), inv_d), 'W_down': r(ks[4], (DFF, D), inv_f), 'sA_gate': r(ks[5], (D, RANK), inv_d), 'sB_gate': r(ks[6], (RANK, DFF), 0.02), 'sA_up': r(ks[7], (D, RANK), inv_d), 'sB_up': r(ks[8], (RANK, DFF), 0.02), 'sA_down': r(ks[9], (DFF, RANK), inv_f), 'sB_down': r(ks[10], (RANK, D), 0.02), 'A_gate': r(ks[11], (E, D, RANK), inv_d), 'B_gate': r(ks[12], (E, RANK, DFF), 0.02), 'A_up': r(ks[13], (E, D, RANK), inv_d), 'B_up': r(ks[14], (E, RANK, DFF), 0.02), 'A_down': r(ks[15], (E, DFF, RANK), inv_f), 'B_down': r(ks[16], (E, RANK, D), 0.02), 'expert_bias': jnp.zeros((E,), dtype=jnp.float32)}
    _L1_ffn_all = _L1_ffn_setup()
    _L1_ffn_in = {k: v for k, v in _L1_ffn_all.items() if k in ('W_router', 'W_gate', 'W_up', 'W_down', 'sA_gate', 'sB_gate', 'sA_up', 'sB_up', 'sA_down', 'sB_down', 'A_gate', 'B_gate', 'A_up', 'B_up', 'A_down', 'B_down', 'expert_bias')}
    del _L1_ffn_all

    def _L2_attn_setup():
        import jax, jax.numpy as jnp
        import numpy as np
        B, S, M = (1, 256, 256)
        H, HKV, D = (32, 8, 64)
        SW = 128
        WAVELENGTH = 150000.0
        SCALE = D ** (-0.25)
        NEG = -1000000000.0

        def _cos_sin(seq_len, dtype):
            half = D // 2
            inv_freq = 1.0 / WAVELENGTH ** (jnp.arange(half, dtype=jnp.float32) * 2.0 / D)
            t = jnp.arange(seq_len, dtype=jnp.float32)
            freqs = t[:, None] * inv_freq[None, :]
            return (jnp.cos(freqs)[None, :, None, :].astype(dtype), jnp.sin(freqs)[None, :, None, :].astype(dtype))

        def _interleaved_rope(x, cos, sin):
            x_even = x[..., ::2]
            x_odd = x[..., 1::2]
            first = x_even * cos - x_odd * sin
            second = x_odd * cos + x_even * sin
            return jnp.stack([first, second], axis=-1).reshape(x.shape)
        key = jax.random.key(seed)
        ks = jax.random.split(key, 8)
        return {'hidden_states': jax.random.normal(ks[0], (B, S, M), jnp.float32), 'Wq': jax.random.normal(ks[1], (M, H, D), jnp.float32) * 0.02, 'bq': jnp.zeros((H, D), jnp.float32), 'Wk': jax.random.normal(ks[2], (M, HKV, D), jnp.float32) * 0.02, 'bk': jnp.zeros((HKV, D), jnp.float32), 'Wv': jax.random.normal(ks[3], (M, HKV, D), jnp.float32) * 0.02, 'bv': jnp.zeros((HKV, D), jnp.float32), 'Wo': jax.random.normal(ks[4], (H, D, M), jnp.float32) * 0.02, 'bo': jnp.zeros((M,), jnp.float32), 'sinks': jax.random.normal(ks[5], (H,), jnp.float32)}
    _L2_attn_all = _L2_attn_setup()
    _L2_attn_in = {k: v for k, v in _L2_attn_all.items() if k in ('Wq', 'bq', 'Wk', 'bk', 'Wv', 'bv', 'Wo', 'bo', 'sinks')}
    del _L2_attn_all

    def _L2_xattn_setup():
        import jax, jax.numpy as jnp
        import numpy as np
        key = jax.random.key(seed)
        k1, k2, k3 = jax.random.split(key, 3)
        B, S, D, M = (8, 256, 256, 128)
        hidden_states = jax.random.normal(k1, (B, S, D), dtype=jnp.float32)
        memory_tokens = jax.random.normal(k2, (B, M, D), dtype=jnp.float32)
        memory_mask = jax.random.randint(k3, (B, M), 0, 2).astype(jnp.bool_)
        return {'hidden_states': hidden_states, 'memory_tokens': memory_tokens, 'memory_mask': memory_mask}
    _L2_xattn_all = _L2_xattn_setup()
    _L2_xattn_in = {k: v for k, v in _L2_xattn_all.items() if k in ()}
    del _L2_xattn_all

    def _L2_ffn_setup():
        import jax, jax.numpy as jnp
        import numpy as np
        B, S, D, R, E = (4, 256, 256, 64, 8)
        SCALING = 64.0 / 16.0
        key = jax.random.key(seed)
        k1, k2, k3, k4 = jax.random.split(key, 4)
        x = jax.random.normal(k1, (B, S, D), dtype=jnp.float32)
        A = jax.random.normal(k2, (E, R, D), dtype=jnp.float32) * 0.02
        Bw = jax.random.normal(k3, (E, D, R), dtype=jnp.float32) * 0.02
        Wg = jax.random.normal(k4, (E, D), dtype=jnp.float32) * 0.02
        return {'x': x, 'A': A, 'Bw': Bw, 'Wg': Wg}
    _L2_ffn_all = _L2_ffn_setup()
    _L2_ffn_in = {k: v for k, v in _L2_ffn_all.items() if k in ('A', 'Bw', 'Wg')}
    del _L2_ffn_all

    def _L3_attn_setup():
        import jax, jax.numpy as jnp
        import numpy as np
        H = 256
        Q_RANK = 32
        SCALE = float(np.sqrt(Q_RANK))
        key = jax.random.key(seed)
        k_x, k_s, k_a, k_o, k_b = jax.random.split(key, 5)
        B, L = (4, 512)
        x = jax.random.normal(k_x, (B, L, H), dtype=jnp.float32)
        Ws = jax.random.normal(k_s, (H, Q_RANK), dtype=jnp.float32) / np.sqrt(H)
        Wa = jax.random.normal(k_a, (H, Q_RANK), dtype=jnp.float32) / np.sqrt(H)
        Wo = jax.random.normal(k_o, (H, H), dtype=jnp.float32) / np.sqrt(H)
        bo = jax.random.normal(k_b, (H,), dtype=jnp.float32) * 0.01
        return {'x': x, 'Ws': Ws, 'Wa': Wa, 'Wo': Wo, 'bo': bo}
    _L3_attn_all = _L3_attn_setup()
    _L3_attn_in = {k: v for k, v in _L3_attn_all.items() if k in ('Ws', 'Wa', 'Wo', 'bo')}
    del _L3_attn_all

    def _L3_xattn_setup():
        import jax, jax.numpy as jnp
        import numpy as np
        BS, S, DK = (8, 64, 256)
        key = jax.random.key(seed)
        kq, kk, kv = jax.random.split(key, 3)
        q = jax.random.normal(kq, (BS, S, DK), dtype=jnp.float32)
        k = jax.random.normal(kk, (BS, S, DK), dtype=jnp.float32)
        v = jax.random.normal(kv, (BS, S, DK), dtype=jnp.float32)
        return {'q': q, 'k': k, 'v': v}
    _L3_xattn_all = _L3_xattn_setup()
    _L3_xattn_in = {k: v for k, v in _L3_xattn_all.items() if k in ()}
    del _L3_xattn_all

    def _L3_ffn_setup():
        import jax, jax.numpy as jnp
        import numpy as np
        H, I, E, TOP_K = (256, 176, 16, 6)
        IS = 352
        NORM_TOPK_PROB = False

        def _silu_and_mul(gate_up):
            d = gate_up.shape[-1] // 2
            g, u = (gate_up[..., :d], gate_up[..., d:])
            return jax.nn.silu(g) * u
        key = jax.random.key(seed)
        ks = jax.random.split(key, 6)
        s = 0.02
        return {'x': jax.random.normal(ks[0], (1, 256, H), jnp.float32), 'gate_w': jax.random.normal(ks[1], (E, H), jnp.float32) * s, 'w1': jax.random.normal(ks[2], (E, 2 * I, H), jnp.float32) * s, 'w2': jax.random.normal(ks[3], (E, H, I), jnp.float32) * s, 'shared_w1': jax.random.normal(ks[4], (2 * IS, H), jnp.float32) * s, 'shared_w2': jax.random.normal(ks[5], (H, IS), jnp.float32) * s}
    _L3_ffn_all = _L3_ffn_setup()
    _L3_ffn_in = {k: v for k, v in _L3_ffn_all.items() if k in ('gate_w', 'w1', 'w2', 'shared_w1', 'shared_w2')}
    del _L3_ffn_all
    return {'x': x, 'ctx_2048': ctx_2048, 'mask_1x1x2048x2048_if1': mask_1x1x2048x2048_if1, 'mask_BxS2_bk0': mask_BxS2_bk0, 'L0_attn_slope_rate': _L0_attn_in['slope_rate'], 'L0_attn_w_qkv': _L0_attn_in['w_qkv'], 'L0_attn_w_gate': _L0_attn_in['w_gate'], 'L0_attn_w_out': _L0_attn_in['w_out'], 'L0_attn_norm_w': _L0_attn_in['norm_w'], 'L0_xattn_wq': _L0_xattn_in['wq'], 'L0_xattn_bq': _L0_xattn_in['bq'], 'L0_xattn_wk': _L0_xattn_in['wk'], 'L0_xattn_bk': _L0_xattn_in['bk'], 'L0_xattn_wv': _L0_xattn_in['wv'], 'L0_xattn_bv': _L0_xattn_in['bv'], 'L0_xattn_wo': _L0_xattn_in['wo'], 'L0_xattn_bo': _L0_xattn_in['bo'], 'L0_ffn_gate_w': _L0_ffn_in['gate_w'], 'L0_ffn_shared_wg': _L0_ffn_in['shared_wg'], 'L0_ffn_shared_wu': _L0_ffn_in['shared_wu'], 'L0_ffn_shared_wd': _L0_ffn_in['shared_wd'], 'L0_ffn_exp_wg': _L0_ffn_in['exp_wg'], 'L0_ffn_exp_wu': _L0_ffn_in['exp_wu'], 'L0_ffn_exp_wd': _L0_ffn_in['exp_wd'], 'L1_attn_Wq': _L1_attn_in['Wq'], 'L1_attn_Wk': _L1_attn_in['Wk'], 'L1_attn_Wv': _L1_attn_in['Wv'], 'L1_attn_Wg': _L1_attn_in['Wg'], 'L1_attn_Wc': _L1_attn_in['Wc'], 'L1_attn_bc': _L1_attn_in['bc'], 'L1_xattn_wq': _L1_xattn_in['wq'], 'L1_xattn_wk': _L1_xattn_in['wk'], 'L1_xattn_wv': _L1_xattn_in['wv'], 'L1_xattn_wo': _L1_xattn_in['wo'], 'L1_xattn_wk_ctx': _L1_xattn_in['wk_ctx'], 'L1_xattn_wv_ctx': _L1_xattn_in['wv_ctx'], 'L1_xattn_q_norm_w': _L1_xattn_in['q_norm_w'], 'L1_xattn_k_norm_w': _L1_xattn_in['k_norm_w'], 'L1_ffn_W_router': _L1_ffn_in['W_router'], 'L1_ffn_W_gate': _L1_ffn_in['W_gate'], 'L1_ffn_W_up': _L1_ffn_in['W_up'], 'L1_ffn_W_down': _L1_ffn_in['W_down'], 'L1_ffn_sA_gate': _L1_ffn_in['sA_gate'], 'L1_ffn_sB_gate': _L1_ffn_in['sB_gate'], 'L1_ffn_sA_up': _L1_ffn_in['sA_up'], 'L1_ffn_sB_up': _L1_ffn_in['sB_up'], 'L1_ffn_sA_down': _L1_ffn_in['sA_down'], 'L1_ffn_sB_down': _L1_ffn_in['sB_down'], 'L1_ffn_A_gate': _L1_ffn_in['A_gate'], 'L1_ffn_B_gate': _L1_ffn_in['B_gate'], 'L1_ffn_A_up': _L1_ffn_in['A_up'], 'L1_ffn_B_up': _L1_ffn_in['B_up'], 'L1_ffn_A_down': _L1_ffn_in['A_down'], 'L1_ffn_B_down': _L1_ffn_in['B_down'], 'L1_ffn_expert_bias': _L1_ffn_in['expert_bias'], 'L2_attn_Wq': _L2_attn_in['Wq'], 'L2_attn_bq': _L2_attn_in['bq'], 'L2_attn_Wk': _L2_attn_in['Wk'], 'L2_attn_bk': _L2_attn_in['bk'], 'L2_attn_Wv': _L2_attn_in['Wv'], 'L2_attn_bv': _L2_attn_in['bv'], 'L2_attn_Wo': _L2_attn_in['Wo'], 'L2_attn_bo': _L2_attn_in['bo'], 'L2_attn_sinks': _L2_attn_in['sinks'], 'L2_ffn_A': _L2_ffn_in['A'], 'L2_ffn_Bw': _L2_ffn_in['Bw'], 'L2_ffn_Wg': _L2_ffn_in['Wg'], 'L3_attn_Ws': _L3_attn_in['Ws'], 'L3_attn_Wa': _L3_attn_in['Wa'], 'L3_attn_Wo': _L3_attn_in['Wo'], 'L3_attn_bo': _L3_attn_in['bo'], 'L3_ffn_gate_w': _L3_ffn_in['gate_w'], 'L3_ffn_w1': _L3_ffn_in['w1'], 'L3_ffn_w2': _L3_ffn_in['w2'], 'L3_ffn_shared_w1': _L3_ffn_in['shared_w1'], 'L3_ffn_shared_w2': _L3_ffn_in['shared_w2']}

def reference(x, ctx_2048, mask_1x1x2048x2048_if1, mask_BxS2_bk0, L0_attn_slope_rate, L0_attn_w_qkv, L0_attn_w_gate, L0_attn_w_out, L0_attn_norm_w, L0_xattn_wq, L0_xattn_bq, L0_xattn_wk, L0_xattn_bk, L0_xattn_wv, L0_xattn_bv, L0_xattn_wo, L0_xattn_bo, L0_ffn_gate_w, L0_ffn_shared_wg, L0_ffn_shared_wu, L0_ffn_shared_wd, L0_ffn_exp_wg, L0_ffn_exp_wu, L0_ffn_exp_wd, L1_attn_Wq, L1_attn_Wk, L1_attn_Wv, L1_attn_Wg, L1_attn_Wc, L1_attn_bc, L1_xattn_wq, L1_xattn_wk, L1_xattn_wv, L1_xattn_wo, L1_xattn_wk_ctx, L1_xattn_wv_ctx, L1_xattn_q_norm_w, L1_xattn_k_norm_w, L1_ffn_W_router, L1_ffn_W_gate, L1_ffn_W_up, L1_ffn_W_down, L1_ffn_sA_gate, L1_ffn_sB_gate, L1_ffn_sA_up, L1_ffn_sB_up, L1_ffn_sA_down, L1_ffn_sB_down, L1_ffn_A_gate, L1_ffn_B_gate, L1_ffn_A_up, L1_ffn_B_up, L1_ffn_A_down, L1_ffn_B_down, L1_ffn_expert_bias, L2_attn_Wq, L2_attn_bq, L2_attn_Wk, L2_attn_bk, L2_attn_Wv, L2_attn_bv, L2_attn_Wo, L2_attn_bo, L2_attn_sinks, L2_ffn_A, L2_ffn_Bw, L2_ffn_Wg, L3_attn_Ws, L3_attn_Wa, L3_attn_Wo, L3_attn_bo, L3_ffn_gate_w, L3_ffn_w1, L3_ffn_w2, L3_ffn_shared_w1, L3_ffn_shared_w2):
    import jax
    import jax.numpy as jnp

    def _L0_attn_ref(hidden_states, slope_rate, w_qkv, w_gate, w_out, norm_w):
        import jax, jax.numpy as jnp
        import numpy as np
        B, N, H = (2, 512, 256)
        NH, HD = (16, 128)
        BLK = 32
        EPS = 1e-06

        def _lightning_attn(x, slope_rate, w_qkv, w_gate, w_out, norm_w):
            b, n, _ = x.shape
            h, d = (NH, HD)
            nb = n // BLK
            qkv = jax.nn.silu(jnp.einsum('bnf,of->bno', x, w_qkv))
            qkv = qkv.reshape(b, n, h, 3 * d)
            q, k, v = jnp.split(qkv, 3, axis=-1)
            q = q.transpose(0, 2, 1, 3)
            k = k.transpose(0, 2, 1, 3)
            v = v.transpose(0, 2, 1, 3)
            s = slope_rate.astype(jnp.float32)
            arr = jnp.arange(1, BLK + 1, dtype=jnp.float32)
            q_decay = jnp.exp(-s * arr[:, None])
            k_decay = jnp.exp(-s * (BLK - arr)[:, None])
            idx = arr[:, None] - arr[None, :]
            diag_decay = jnp.where(idx >= 0, jnp.exp(-s * idx), 0.0)
            block_decay = jnp.exp(-s * BLK)
            qb = q.reshape(b, h, nb, BLK, d).transpose(2, 0, 1, 3, 4)
            kb = k.reshape(b, h, nb, BLK, d).transpose(2, 0, 1, 3, 4)
            vb = v.reshape(b, h, nb, BLK, d).transpose(2, 0, 1, 3, 4)

            def step(kv, blk):
                qi, ki, vi = blk
                o_inter = jnp.einsum('bhmd,bhde->bhme', qi * q_decay, kv)
                qk = jnp.einsum('bhmd,bhnd->bhmn', qi, ki) * diag_decay
                o_intra = jnp.einsum('bhmn,bhne->bhme', qk, vi)
                kv_new = block_decay * kv + jnp.einsum('bhmd,bhme->bhde', ki * k_decay, vi)
                return (kv_new, o_inter + o_intra)
            kv0 = jnp.zeros((b, h, d, d), dtype=jnp.float32)
            _, out = jax.lax.scan(step, kv0, (qb, kb, vb))
            out = out.transpose(1, 2, 0, 3, 4).reshape(b, h, n, d)
            out = out.transpose(0, 2, 1, 3).reshape(b, n, h * d)
            var = jnp.mean(out * out, axis=-1, keepdims=True)
            out = norm_w * (out * jax.lax.rsqrt(var + EPS))
            gate = jax.nn.sigmoid(jnp.einsum('bnf,of->bno', x, w_gate))
            return jnp.einsum('bno,fo->bnf', gate * out, w_out)
        return _lightning_attn(hidden_states, slope_rate, w_qkv, w_gate, w_out, norm_w)

    def _L0_xattn_ref(x, c, attn_mask, wq, bq, wk, bk, wv, bv, wo, bo):
        import jax, jax.numpy as jnp
        import numpy as np
        import math
        CHANNELS = 128
        N_HEADS = 16
        K_CHANNELS = CHANNELS // N_HEADS
        ROPE_D = int(K_CHANNELS * 0.5)
        B, T = (4, 256)

        def apply_rope(x, d, base=10000.0):
            t = x.shape[2]
            theta = 1.0 / base ** (jnp.arange(0, d, 2, dtype=jnp.float32) / d)
            idx_theta = jnp.arange(t, dtype=jnp.float32)[:, None] * theta[None, :]
            idx_theta2 = jnp.concatenate([idx_theta, idx_theta], axis=-1)
            cos = jnp.cos(idx_theta2)[None, None, :, :]
            sin = jnp.sin(idx_theta2)[None, None, :, :]
            x_rope, x_pass = (x[..., :d], x[..., d:])
            d2 = d // 2
            neg_half = jnp.concatenate([-x_rope[..., d2:], x_rope[..., :d2]], axis=-1)
            x_rope = x_rope * cos + neg_half * sin
            return jnp.concatenate([x_rope, x_pass], axis=-1)
        b, _, t_t = x.shape
        t_s = c.shape[2]
        q = jnp.einsum('oi,bit->bot', wq, x) + bq[None, :, None]
        k = jnp.einsum('oi,bit->bot', wk, c) + bk[None, :, None]
        v = jnp.einsum('oi,bit->bot', wv, c) + bv[None, :, None]

        def split_heads(z, t):
            return z.reshape(b, N_HEADS, K_CHANNELS, t).transpose(0, 1, 3, 2)
        q = split_heads(q, t_t)
        k = split_heads(k, t_s)
        v = split_heads(v, t_s)
        q = apply_rope(q, ROPE_D)
        k = apply_rope(k, ROPE_D)
        scores = jnp.einsum('bhqc,bhkc->bhqk', q, k) / math.sqrt(K_CHANNELS)
        scores = jnp.where(attn_mask == 0, jnp.float32(-10000.0), scores)
        p_attn = jax.nn.softmax(scores, axis=-1)
        out = jnp.einsum('bhqk,bhkc->bhqc', p_attn, v)
        out = out.transpose(0, 1, 3, 2).reshape(b, CHANNELS, t_t)
        out = jnp.einsum('oi,bit->bot', wo, out) + bo[None, :, None]
        return out

    def _L0_ffn_ref(hidden_states, gate_w, shared_wg, shared_wu, shared_wd, exp_wg, exp_wu, exp_wd):
        import jax, jax.numpy as jnp
        import numpy as np
        HIDDEN = 256
        N_EXPERTS = 8
        N_SHARED = 2
        TOP_K = 2
        MOE_FF = 176
        SHARED_FF = N_SHARED * MOE_FF
        SCALE = 2.5
        BATCH, SEQ = (2, 128)
        B, S, D = hidden_states.shape
        T = B * S
        xf = hidden_states.reshape(T, D)
        scores = jax.nn.sigmoid(xf @ gate_w.T)
        topk_w, topk_idx = jax.lax.top_k(scores, TOP_K)
        topk_w = topk_w / (topk_w.sum(axis=-1, keepdims=True) + 1e-20)
        topk_w = topk_w * SCALE
        shared_out = jax.nn.silu(xf @ shared_wg.T) * (xf @ shared_wu.T) @ shared_wd.T
        h = jax.nn.silu(jnp.einsum('td,efd->etf', xf, exp_wg)) * jnp.einsum('td,efd->etf', xf, exp_wu)
        all_out = jnp.einsum('etf,edf->etd', h, exp_wd)
        picked = all_out[topk_idx, jnp.arange(T)[:, None]]
        routed_out = (topk_w[..., None] * picked).sum(axis=1)
        return (shared_out + routed_out).reshape(B, S, D)

    def _L1_attn_ref(hidden_states, Wq, Wk, Wv, Wg, Wc, bc):
        import jax, jax.numpy as jnp
        import numpy as np
        H = 8
        R = 2
        D = 128
        DEG = 2
        GATE_OFFSET = 6.906768

        def _power_attention(q, k, v, log_g):
            B, T, hq, d = q.shape
            scale = 1.0 / d ** 0.5
            k = jnp.repeat(k, R, axis=2)
            v = jnp.repeat(v, R, axis=2)
            logG = jnp.cumsum(log_g, axis=1)
            logG = jnp.repeat(logG, R, axis=2)
            logG = jnp.transpose(logG, (0, 2, 1))
            qk = jnp.einsum('bthd,bshd->bhts', q, k) * scale
            a = qk ** DEG
            gate = logG[:, :, :, None] - logG[:, :, None, :]
            causal = jnp.tril(jnp.ones((T, T), dtype=bool))
            a = jnp.where(causal, a * jnp.exp(gate), 0.0)
            norm = jnp.sum(a, axis=-1) + 1e-06
            y = jnp.einsum('bhts,bshd->bthd', a, v)
            y = y / jnp.transpose(norm, (0, 2, 1))[..., None]
            return y
        B, T, C = hidden_states.shape
        q = (hidden_states @ Wq).reshape(B, T, H * R, D)
        k = (hidden_states @ Wk).reshape(B, T, H, D)
        v = (hidden_states @ Wv).reshape(B, T, H, D)
        g = hidden_states @ Wg
        log_g = jax.nn.log_sigmoid(GATE_OFFSET + g.astype(jnp.float32))
        y = _power_attention(q, k, v, log_g)
        y = y.reshape(B, T, H * R * D)
        return y @ Wc + bc

    def _L1_xattn_ref(x, h_ctx_kv, wq, wk, wv, wo, wk_ctx, wv_ctx, q_norm_w, k_norm_w):
        import jax, jax.numpy as jnp
        import numpy as np
        HIDDEN = 256
        NUM_HEADS = 16
        NUM_KV_HEADS = 4
        HEAD_DIM = 128
        ROPE_THETA = 10000.0
        EPS = 1e-06

        def rms_norm(x, w, eps=EPS):
            var = jnp.mean(jnp.square(x), axis=-1, keepdims=True)
            return x * jax.lax.rsqrt(var + eps) * w

        def rope_cache(L, head_dim, theta, dtype):
            inv_freq = 1.0 / theta ** (jnp.arange(0, head_dim, 2, dtype=jnp.float32) / head_dim)
            t = jnp.arange(L, dtype=jnp.float32)
            freqs = jnp.outer(t, inv_freq)
            emb = jnp.concatenate([freqs, freqs], -1)
            cos = jnp.cos(emb).astype(dtype)[None, :, None, :]
            sin = jnp.sin(emb).astype(dtype)[None, :, None, :]
            return (cos, sin)

        def rotate_half(x):
            x1, x2 = jnp.split(x, 2, axis=-1)
            return jnp.concatenate([-x2, x1], axis=-1)
        B, L, _ = x.shape
        T = h_ctx_kv.shape[1]
        rep = NUM_HEADS // NUM_KV_HEADS
        q = (x @ wq).reshape(B, L, NUM_HEADS, HEAD_DIM)
        k = (x @ wk).reshape(B, L, NUM_KV_HEADS, HEAD_DIM)
        v = (x @ wv).reshape(B, L, NUM_KV_HEADS, HEAD_DIM)
        q = rms_norm(q, q_norm_w)
        k = rms_norm(k, k_norm_w)
        k_ctx = (h_ctx_kv @ wk_ctx).reshape(B, T, NUM_KV_HEADS, HEAD_DIM)
        v_ctx = (h_ctx_kv @ wv_ctx).reshape(B, T, NUM_KV_HEADS, HEAD_DIM)
        k_ctx = rms_norm(k_ctx, k_norm_w)
        cos, sin = rope_cache(L, HEAD_DIM, ROPE_THETA, x.dtype)
        q = q * cos + rotate_half(q) * sin
        k = k * cos + rotate_half(k) * sin
        k_full = jnp.concatenate([k_ctx, k], axis=1)
        v_full = jnp.concatenate([v_ctx, v], axis=1)
        k_full = jnp.repeat(k_full, rep, axis=2)
        v_full = jnpp_repeat = jnp.repeat(v_full, rep, axis=2)
        i = jnp.arange(L)[:, None]
        j = jnp.arange(L)[None, :]
        causal = jnp.where(j > i, -jnp.inf, 0.0).astype(x.dtype)
        mask = jnp.concatenate([jnp.zeros((L, T), x.dtype), causal], axis=1)
        scale = 1.0 / np.sqrt(HEAD_DIM)
        scores = jnp.einsum('blhd,bmhd->bhlm', q, k_full) * scale + mask
        probs = jax.nn.softmax(scores, axis=-1)
        out = jnp.einsum('bhlm,bmhd->blhd', probs, v_full)
        out = out.reshape(B, L, NUM_HEADS * HEAD_DIM)
        return out @ wo

    def _L1_ffn_ref(x, W_router, W_gate, W_up, W_down, sA_gate, sB_gate, sA_up, sB_up, sA_down, sB_down, A_gate, B_gate, A_up, B_up, A_down, B_down, expert_bias):
        import jax, jax.numpy as jnp
        import numpy as np
        B, L, D = (2, 128, 256)
        E, TOP_K, RANK, DFF = (8, 2, 8, 688)

        def _lora(x, A, Bm, scale):
            return x @ A @ Bm * scale

        def _expert_lora(x, A, Bm, w, scale):
            xA = jnp.einsum('bld,edr->bler', x, A)
            xAB = jnp.einsum('bler,erd->bled', xA, Bm) * scale
            return (xAB * w).sum(axis=2)
        scale = 1.0 / RANK
        logits = x @ W_router
        scores = jax.nn.sigmoid(logits)
        biased = scores + expert_bias
        _, topk_idx = jax.lax.top_k(biased, TOP_K)
        topk_scores = jnp.take_along_axis(scores, topk_idx, axis=-1)
        topk_w = topk_scores / (topk_scores.sum(-1, keepdims=True) + 1e-08)
        one_hot = jax.nn.one_hot(topk_idx, E, dtype=x.dtype)
        expert_weights = (one_hot * topk_w[..., None]).sum(axis=2)
        w = expert_weights[..., None]
        gate = x @ W_gate + _lora(x, sA_gate, sB_gate, scale) + _expert_lora(x, A_gate, B_gate, w, scale)
        up = x @ W_up + _lora(x, sA_up, sB_up, scale) + _expert_lora(x, A_up, B_up, w, scale)
        hidden = jax.nn.silu(gate) * up
        out = hidden @ W_down + _lora(hidden, sA_down, sB_down, scale) + _expert_lora(hidden, A_down, B_down, w, scale)
        return out

    def _L2_attn_ref(hidden_states, Wq, bq, Wk, bk, Wv, bv, Wo, bo, sinks):
        import jax, jax.numpy as jnp
        import numpy as np
        B, S, M = (1, 256, 256)
        H, HKV, D = (32, 8, 64)
        SW = 128
        WAVELENGTH = 150000.0
        SCALE = D ** (-0.25)
        NEG = -1000000000.0

        def _cos_sin(seq_len, dtype):
            half = D // 2
            inv_freq = 1.0 / WAVELENGTH ** (jnp.arange(half, dtype=jnp.float32) * 2.0 / D)
            t = jnp.arange(seq_len, dtype=jnp.float32)
            freqs = t[:, None] * inv_freq[None, :]
            return (jnp.cos(freqs)[None, :, None, :].astype(dtype), jnp.sin(freqs)[None, :, None, :].astype(dtype))

        def _interleaved_rope(x, cos, sin):
            x_even = x[..., ::2]
            x_odd = x[..., 1::2]
            first = x_even * cos - x_odd * sin
            second = x_odd * cos + x_even * sin
            return jnp.stack([first, second], axis=-1).reshape(x.shape)
        b, s, _ = hidden_states.shape
        groups = H // HKV
        q = jnp.einsum('bqm,muh->bquh', hidden_states, Wq) + bq
        k = jnp.einsum('bkm,mvh->bkvh', hidden_states, Wk) + bk
        v = jnp.einsum('bkm,mvh->bkvh', hidden_states, Wv) + bv
        cos, sin = _cos_sin(s, hidden_states.dtype)
        q = _interleaved_rope(q, cos, sin) * SCALE
        k = _interleaved_rope(k, cos, sin) * SCALE
        k = jnp.repeat(k, groups, axis=2)
        v = jnp.repeat(v, groups, axis=2)
        scores = jnp.einsum('bquh,bkuh->buqk', q, k)
        pos = jnp.arange(s)
        sw_mask = jnp.abs(pos[:, None] - pos[None, :]) <= SW
        scores = jnp.where(sw_mask[None, None, :, :], scores, NEG)
        sink_logits = jnp.broadcast_to(sinks[None, :, None, None], (b, H, s, 1))
        combined = jnp.concatenate([scores, sink_logits], axis=-1)
        probs = jax.nn.softmax(combined.astype(jnp.float32), axis=-1)
        attn = probs[..., :-1].astype(hidden_states.dtype)
        out = jnp.einsum('buqk,bkuh->bquh', attn, v)
        return jnp.einsum('bquh,uhm->bqm', out, Wo) + bo

    def _L2_xattn_ref(hidden_states, memory_tokens, memory_mask):
        import jax, jax.numpy as jnp
        import numpy as np
        B, S, D = hidden_states.shape
        scale = 1.0 / jnp.sqrt(jnp.asarray(D, hidden_states.dtype))
        scores = jnp.einsum('bsd,bmd->bsm', hidden_states, memory_tokens) * scale
        neg_inf = jnp.asarray(-1e+30, scores.dtype)
        scores = jnp.where(memory_mask[:, None, :], scores, neg_inf)
        attn = jax.nn.softmax(scores, axis=-1)
        readout = jnp.einsum('bsm,bmd->bsd', attn, memory_tokens)
        valid_b = jnp.any(memory_mask, axis=-1)
        out = jnp.where(valid_b[:, None, None], readout, jnp.zeros_like(readout))
        return out

    def _L2_ffn_ref(x, A, Bw, Wg):
        import jax, jax.numpy as jnp
        import numpy as np
        B, S, D, R, E = (4, 256, 256, 64, 8)
        SCALING = 64.0 / 16.0
        bsz, seq_len, dim = x.shape
        xf = x.reshape(-1, dim)
        logits = jnp.einsum('nd,ed->ne', xf, Wg)
        prob = jax.nn.softmax(logits, axis=-1)
        gate = jnp.argmax(prob, axis=-1)
        prob_sel = jnp.take_along_axis(prob, gate[:, None], axis=1)
        mask = jax.nn.one_hot(gate, E, dtype=xf.dtype)
        h = jnp.einsum('nd,erd->ner', xf, A)
        h = h * mask[:, :, None]
        y = jnp.einsum('ner,eor->no', h, Bw)
        y = y * SCALING * prob_sel
        return y.reshape(bsz, seq_len, -1)

    def _L3_attn_ref(x, Ws, Wa, Wo, bo):
        import jax, jax.numpy as jnp
        import numpy as np
        H = 256
        Q_RANK = 32
        SCALE = float(np.sqrt(Q_RANK))
        B, L, _ = x.shape
        state = jnp.einsum('blh,hr->blr', x, Ws)
        action = jnp.einsum('blh,hr->blr', x, Wa)
        q_values = jnp.einsum('bir,bjr->bij', state, action) / SCALE
        causal = jnp.tril(jnp.ones((L, L), dtype=bool))
        q_values = jnp.where(causal, q_values, -jnp.inf)
        weights = jax.nn.softmax(q_values, axis=-1)
        out = jnp.einsum('bij,bjh->bih', weights, x)
        return jnp.einsum('bih,ho->bio', out, Wo.T) + bo

    def _L3_xattn_ref(q, k, v):
        import jax, jax.numpy as jnp
        import numpy as np
        BS, S, DK = (8, 64, 256)
        dk = q.shape[-1]
        scale = 1.0 / jnp.sqrt(jnp.asarray(dk, dtype=q.dtype))
        scaled = jnp.einsum('bsd,bse->bde', q, k) * scale
        attn = jax.nn.softmax(scaled, axis=1)
        out = jnp.einsum('bde,bse->bsd', attn, v)
        return out

    def _L3_ffn_ref(x, gate_w, w1, w2, shared_w1, shared_w2):
        import jax, jax.numpy as jnp
        import numpy as np
        H, I, E, TOP_K = (256, 176, 16, 6)
        IS = 352
        NORM_TOPK_PROB = False

        def _silu_and_mul(gate_up):
            d = gate_up.shape[-1] // 2
            g, u = (gate_up[..., :d], gate_up[..., d:])
            return jax.nn.silu(g) * u
        B, S, Hd = x.shape
        xf = x.reshape(-1, Hd)
        T = xf.shape[0]
        shared_out = _silu_and_mul(xf @ shared_w1.T) @ shared_w2.T
        logits = xf @ gate_w.T
        probs = jax.nn.softmax(logits.astype(jnp.float32), axis=-1)
        routing_weights, selected = jax.lax.top_k(probs, TOP_K)
        if NORM_TOPK_PROB:
            routing_weights = routing_weights / routing_weights.sum(-1, keepdims=True)
        combine = jnp.zeros((T, E), jnp.float32).at[jnp.arange(T)[:, None], selected].add(routing_weights).astype(x.dtype)
        gate_up = jnp.einsum('th,eoh->teo', xf, w1)
        act = _silu_and_mul(gate_up)
        moe_out = jnp.einsum('te,tei,ehi->th', combine, act, w2)
        return (moe_out + shared_out).reshape(B, S, Hd)
    x = x + _L0_attn_ref(_layernorm(x, axis=-1), L0_attn_slope_rate, L0_attn_w_qkv, L0_attn_w_gate, L0_attn_w_out, L0_attn_norm_w)
    x = x + _L0_xattn_ref(_layernorm(x, axis=-1), ctx_2048, mask_1x1x2048x2048_if1, L0_xattn_wq, L0_xattn_bq, L0_xattn_wk, L0_xattn_bk, L0_xattn_wv, L0_xattn_bv, L0_xattn_wo, L0_xattn_bo)
    x = x + _L0_ffn_ref(_layernorm(x, axis=-1), L0_ffn_gate_w, L0_ffn_shared_wg, L0_ffn_shared_wu, L0_ffn_shared_wd, L0_ffn_exp_wg, L0_ffn_exp_wu, L0_ffn_exp_wd)
    x = x + _L1_attn_ref(_layernorm(x, axis=-1), L1_attn_Wq, L1_attn_Wk, L1_attn_Wv, L1_attn_Wg, L1_attn_Wc, L1_attn_bc)
    x = x + _L1_xattn_ref(_layernorm(x, axis=-1), ctx_2048, L1_xattn_wq, L1_xattn_wk, L1_xattn_wv, L1_xattn_wo, L1_xattn_wk_ctx, L1_xattn_wv_ctx, L1_xattn_q_norm_w, L1_xattn_k_norm_w)
    x = x + _L1_ffn_ref(_layernorm(x, axis=-1), L1_ffn_W_router, L1_ffn_W_gate, L1_ffn_W_up, L1_ffn_W_down, L1_ffn_sA_gate, L1_ffn_sB_gate, L1_ffn_sA_up, L1_ffn_sB_up, L1_ffn_sA_down, L1_ffn_sB_down, L1_ffn_A_gate, L1_ffn_B_gate, L1_ffn_A_up, L1_ffn_B_up, L1_ffn_A_down, L1_ffn_B_down, L1_ffn_expert_bias)
    x = x + _L2_attn_ref(_layernorm(x, axis=-1), L2_attn_Wq, L2_attn_bq, L2_attn_Wk, L2_attn_bk, L2_attn_Wv, L2_attn_bv, L2_attn_Wo, L2_attn_bo, L2_attn_sinks)
    x = x + _L2_xattn_ref(_layernorm(x, axis=-1), ctx_2048, mask_BxS2_bk0)
    x = x + _L2_ffn_ref(_layernorm(x, axis=-1), L2_ffn_A, L2_ffn_Bw, L2_ffn_Wg)
    x = x + _L3_attn_ref(_layernorm(x, axis=-1), L3_attn_Ws, L3_attn_Wa, L3_attn_Wo, L3_attn_bo)
    x = x + _L3_xattn_ref(_layernorm(x, axis=-1), ctx_2048, ctx_2048)
    x = x + _L3_ffn_ref(_layernorm(x, axis=-1), L3_ffn_gate_w, L3_ffn_w1, L3_ffn_w2, L3_ffn_shared_w1, L3_ffn_shared_w2)
    return x

_drawn_inputs = setup_inputs


def setup_inputs(seed=0):
    import zlib

    import numpy as np

    out = dict(_drawn_inputs(seed))
    spreads = {'L0_attn_norm_w': (1.0, 0.2),
     'L0_xattn_bq': (0.0, 0.589),
     'L0_xattn_bk': (0.0, 0.8),
     'L0_xattn_bv': (0.0, 0.8),
     'L0_xattn_bo': (0.0, 0.8),
     'L1_attn_bc': (0.0, 0.1),
     'L1_xattn_q_norm_w': (1.0, 0.6),
     'L1_xattn_k_norm_w': (1.0, 0.6),
     'L1_ffn_expert_bias': (0.0, 0.8),
     'L2_attn_bq': (0.0, 0.8),
     'L2_attn_bk': (0.0, 2.0),
     'L2_attn_bv': (0.0, 0.1),
     'L2_attn_bo': (0.0, 0.1)}
    factors = {'L0_ffn_gate_w': 4.502,
     'L0_ffn_shared_wg': 4.527,
     'L0_ffn_shared_wu': 4.284,
     'L0_ffn_shared_wd': 4.627,
     'L0_ffn_exp_wg': 3.865,
     'L0_ffn_exp_wu': 3.904,
     'L0_ffn_exp_wd': 3.934,
     'L1_attn_Wg': 22.755,
     'L1_ffn_W_router': 8.0,
     'L1_ffn_sA_gate': 8.0,
     'L1_ffn_sB_gate': 8.0,
     'L1_ffn_sA_up': 8.0,
     'L1_ffn_sB_up': 8.0,
     'L1_ffn_sA_down': 8.0,
     'L1_ffn_sB_down': 8.0,
     'L1_ffn_A_gate': 8.0,
     'L1_ffn_B_gate': 8.0,
     'L1_ffn_A_up': 8.0,
     'L1_ffn_B_up': 8.0,
     'L1_ffn_A_down': 8.0,
     'L1_ffn_B_down': 8.0,
     'L2_attn_Wq': 8.0,
     'L2_attn_Wk': 8.0,
     'L2_attn_sinks': 55.525,
     'L2_ffn_Wg': 3.162,
     'L3_attn_bo': 3.403,
     'L3_ffn_gate_w': 8.0,
     'L3_ffn_w1': 8.0,
     'L3_ffn_w2': 8.0,
     'L3_ffn_shared_w1': 7.315,
     'L3_ffn_shared_w2': 7.138}
    for name, (base, spread) in spreads.items():
        noise = np.random.default_rng([zlib.crc32(name.encode()), seed]).standard_normal(out[name].shape)
        drawn = base * np.exp(spread * noise) if base else spread * noise
        out[name] = jnp.asarray(drawn.astype(out[name].dtype))
    for name, factor in factors.items():
        out[name] = (out[name] * factor).astype(out[name].dtype)
    return out
```

```python
from contextlib import ExitStack, contextmanager

import concourse.bass as bass
import numpy as np
from concourse import mybir

F32 = mybir.dt.float32
I32 = mybir.dt.int32
U8 = mybir.dt.uint8
ALU = mybir.AluOpType
ACT = mybir.ActivationFunctionType
AX = mybir.AxisListType.X

P = 128
B = 16
D = 256
KD = D // P
G = 4
GROUPS = B // G
N = G * P
LN_EPS = 1e-5


def at(turn, per, count):
    return count if turn is None else turn * per + count


class Core:

    def __init__(self, nc, ctx, dram):
        self.nc, self.dram, self.ctx = nc, dram, ctx
        self.of_sublayer = []
        self.x = self.sb("x_tokens", [P, B, D])
        self.xnT = self.sb("xn_features", [P, KD, B, P])
        self.const = self.sb("const_sb", [P, dram["const"].shape[1]])
        self.arena = self.sb("arena", [P, ARENA])
        self.bank = [ctx.enter_context(nc.psum_tensor(f"bank{i}", [P, 512], F32)) for i in range(8)]
        self.ctx_sb = self.sb("ctx_tokens", [P, B, D])
        self.ctxT = self.sb("ctx_features", [P, KD, B, P])
        self.x_loaded = self.sem("x_loaded")
        self.const_loaded = self.sem("const_loaded")
        self.ctx_loaded = self.sem("ctx_loaded")
        self.passed = self.sem("passed")
        self.weights_loaded = {}
        self.ident = self.constant("ident")

    def sb(self, name, shape, dt=F32, ctx=None):
        return (ctx or self.ctx).enter_context(self.nc.sbuf_tensor(name, shape, dt))

    def sem(self, name, ctx=None):
        sem = (ctx or self.ctx).enter_context(self.nc.semaphore(name))
        if ctx is not None:
            self.of_sublayer.append(sem)
        return sem

    @contextmanager
    def block(self):
        with self.nc.Block() as block:
            yield block
        for sem in self.of_sublayer:
            self.nc.sync.sem_clear(sem)
        self.of_sublayer = []
        self.nc.all_engine_barrier()

    def constant(self, name):
        lo, hi = CONST_AT[name]
        return self.const[:, lo:hi]

    def held(self, eng):
        eng.sem_inc(self.passed, 1)

    def weights(self, name):
        base = WEIGHT_BASE.get(name, 0)
        out = {}
        for part, lo, hi in WEIGHT_PARTS[name]:
            out[part] = self.arena[:, base + lo:base + hi]
        return out

    def load(self, eng, name):
        if f"w_{name}" not in self.dram: return
        if name not in self.weights_loaded:
            self.weights_loaded[name] = self.sem(f"weights_loaded_{name}")
        base, width = WEIGHT_BASE[name], self.dram[f"w_{name}"].shape[1]
        eng.dma_start(self.arena[:, base:base + width], self.dram[f"w_{name}"]).then_inc(self.weights_loaded[name], 16)

    def work(self, name):
        lo, hi = WORK[name]
        taken = [lo]

        def carve(*shape):
            size = int(np.prod(shape))
            a = self.arena[:, taken[0]:taken[0] + size]
            taken[0] += size
            assert taken[0] <= hi, (name, taken[0], hi)
            if len(shape) == 2:
                return a.rearrange("p (a b) -> p a b", a=shape[0])
            if len(shape) == 3:
                return a.rearrange("p (a b c) -> p a b c", a=shape[0], b=shape[1])
            return a

        return carve


ARENA = 35200
WEIGHT_BASE = {"L0a": 0, "L0x": 34544, "L0f": 0, "L1a": 12640, "L1x": 0, "L1f": 12640, "L2a": 19900,
               "L2f": 12480, "L3a": 15064, "L3f": 15968, "L3sel": 13100}
WORK = {"L0a": (20512, 34544), "L0x": (21000, 34544), "L0f": (25200, 34544), "L1a": (25200, 35200),
        "L1x": (12560, 35200), "L1f": (0, 12640), "L2a": (0, 19900), "L2x": (0, 12480), "L2f": (0, 12480),
        "L3a": (0, 12480), "L3x": (0, 13100), "L3f": (0, 13100)}


def normalise(core, name, block, s, tokens=None):
    nc = core.nc
    mv, rstd, half, xn, stats = s["mv"], s["rstd"], s["half"], s["xn"], s["stats"]
    stats_done, mv_done, eps_done, rstd_done = s["stats_done"], s["mv_done"], s["eps_done"], s["rstd_done"]
    xn_done, turned, xnT_done = s["xn_done"], s["turned"], s["xnT_done"]

    def vector(dve):
        nc.vector.memset(half, -0.5)
        dve.wait_ge(core.x_loaded, 16)
        for b in range(B):
            nc.vector.bn_stats(stats[:, b, :], core.x[:, b, :]).then_inc(stats_done, 1)
        for b in range(B):
            dve.wait_ge(stats_done, b + 1)
            last = nc.vector.bn_aggr(mv[:, b, :], stats[:, b, :])
        last.then_inc(mv_done, 1)
        dve.wait_ge(mv_done, 1)
        nc.vector.tensor_scalar(rstd, mv[:, :, 1], LN_EPS, None, ALU.add).then_inc(eps_done, 1)
        dve.wait_ge(rstd_done, 1)
        for b in range(B):
            if tokens is None and b >= 4:
                dve.wait_ge(turned, (b - 4) // 2 + 1)
            out = xn[:, b % 4, :] if tokens is None else tokens[:, b, :]
            nc.vector.tensor_scalar(out, core.x[:, b, :], mv[:, b, 0:1], rstd[:, b:b + 1],
                                    ALU.subtract, ALU.mult).then_inc(xn_done, 1)

    def gpsimd(pool):
        pool.wait_ge(eps_done, 1)
        nc.gpsimd.tensor_tensor(rstd, rstd, half, ALU.pow).then_inc(rstd_done, 1)

    def tensor(pe):
        pe.wait_ge(core.const_loaded, 16)
        for i in range(B // 2):
            pe.wait_ge(xn_done, 2 * i + 2)
            if i >= 2:
                pe.wait_ge(xnT_done, i - 1)
            for k in range(KD):
                for b in (2 * i, 2 * i + 1):
                    last = nc.tensor.transpose(
                        core.bank[i % 2][:, k * 256 + (b % 2) * P:k * 256 + (b % 2) * P + P],
                        xn[:, b % 4, k * P:(k + 1) * P], core.ident)
            last.then_inc(turned, 1)

    def scalar(act):
        for i in range(B // 2):
            act.wait_ge(turned, i + 1)
            nc.scalar.activation(core.xnT[:, :, 2 * i:2 * i + 2, :],
                                 core.bank[i % 2][:, :].rearrange("p (k b t) -> p k b t", k=KD, b=2),
                                 ACT.Copy).then_inc(xnT_done, 1)

    return vector, gpsimd, tensor, scalar


def norm_state(core, name, carve, ctx, turn_to_features=True):
    s = {n: core.sem(f"{name}_{n}", ctx) for n in
         ("stats_done", "mv_done", "eps_done", "rstd_done", "xn_done", "turned", "xnT_done")}
    s["stats"] = carve(B, 6)
    s["mv"] = carve(B, 2)
    s["rstd"] = carve(B)
    s["half"] = carve(B)
    s["xn"] = carve(4, D) if turn_to_features else None
    return s


def lightning_attention(core):
    nc, H, EPS = core.nc, 16, 1e-6
    w = core.weights("L0a")
    wqkv = w["qkv"].rearrange("p (k h c n) -> p k h c n", k=KD, h=H, c=3)
    wgate = w["gate"].rearrange("p (k h n) -> p k h n", k=KD, h=H)
    wout = w["out"].rearrange("p (h n) -> p h n", h=H)
    norm_w = w["norm"]
    slope = w["slope"]
    with ExitStack() as ctx:
        sem = lambda name: core.sem(f"L0a_{name}", ctx)
        carve = core.work("L0a")
        s = norm_state(core, "L0a", carve, ctx)
        decay = carve(H, P)
        xcur = carve(KD, N)
        qT, kT, v, gate, ow, sq, z = (carve(2, N) for _ in range(7))
        attn = carve(N)
        sumsq = carve(N)
        zeros = carve(N)
        msq = carve(G)
        half = s["half"][:, 0:G]
        q_bank, k_bank, v_bank, g_bank, s_bank, o_bank = core.bank[0:6]
        y_bank = core.bank[6:8]

        slope_neg, decay_exp, decay_done = sem("slope_neg"), sem("decay_exp"), sem("decay_done")
        xcur_done, xcur_used = sem("xcur_done"), sem("xcur_used")
        q_made, k_made, v_made, g_made = sem("q_made"), sem("k_made"), sem("v_made"), sem("g_made")
        qT_done, kT_done, v_done, gate_done = sem("qT_done"), sem("kT_done"), sem("v_done"), sem("gate_done")
        scores_made, attn_done, o_made = sem("scores_made"), sem("attn_done"), sem("o_made")
        ow_done, sq_done, sumsq_done, z_done = sem("ow_done"), sem("sq_done"), sem("sumsq_done"), sem("z_done")
        ssq_made, msq_done, rms_done, y_made, y_added = (
            sem("ssq_made"), sem("msq_done"), sem("rms_done"), sem("y_made"), sem("y_added"))
        block = ctx.enter_context(core.block())
        n_vector, n_gpsimd, n_tensor, n_scalar = normalise(core, "L0a", block, s)

        @block.gpsimd
        def _(pool):
            pool.wait_ge(core.x_loaded, 16)
            nc.gpsimd.memset(zeros, 0.0)
            n_gpsimd(pool)
            with pool.Fori(0, GROUPS) as t:
                pool.wait_ge(xcur_used, at(t, 1, 1))
                pool.wait_ge(s["xnT_done"], B // 2)
                nc.gpsimd.tensor_copy(xcur.rearrange("p k (b t) -> p k b t", b=G),
                                      core.xnT[:, :, bass.ds(t * G, G), :]).then_inc(xcur_done, 1)
                for h in range(H):
                    pool.wait_ge(sq_done, at(t, H, h + 1))
                    if h == 0:
                        nc.gpsimd.tensor_tensor(sumsq, sq[:, 0, :], zeros, ALU.add).then_inc(sumsq_done, 1)
                    else:
                        pool.wait_ge(sumsq_done, at(t, H, h))
                        nc.gpsimd.tensor_tensor(sumsq, sumsq, sq[:, h % 2, :], ALU.add).then_inc(sumsq_done, 1)
                pool.wait_ge(msq_done, at(t, 1, 1))
                nc.gpsimd.tensor_tensor(msq, msq, half, ALU.pow).then_inc(rms_done, 1)

        @block.tensor
        def _(pe):
            pe.wait_ge(core.const_loaded, 16)
            n_tensor(pe)
            pe.sem_inc(xcur_used, 1)
            pe.wait_ge(core.weights_loaded["L0a"], 16)
            pe.wait_ge(s["xnT_done"], B // 2)
            with pe.Fori(0, GROUPS) as t:
                pe.wait_ge(xcur_done, at(t, 1, 1))
                for step in range(H + 2):
                    if step < H:
                        h = step
                        if h:
                            pe.wait_ge(qT_done, at(t, H, h))
                        for k in range(KD):
                            last = nc.tensor.matmul(q_bank[:, :], wqkv[:, k, h, 0, :], xcur[:, k, :],
                                                    start=(k == 0), stop=(k == KD - 1))
                        last.then_inc(q_made, 1)
                        if h:
                            pe.wait_ge(kT_done, at(t, H, h))
                        for k in range(KD):
                            last = nc.tensor.matmul(k_bank[:, :], wqkv[:, k, h, 1, :], xcur[:, k, :],
                                                    start=(k == 0), stop=(k == KD - 1))
                        last.then_inc(k_made, 1)
                    if 1 <= step <= H:
                        h = step - 1
                        pe.wait_ge(kT_done, at(t, H, h + 1))
                        pe.wait_ge(qT_done, at(t, H, h + 1))
                        if h:
                            pe.wait_ge(attn_done, at(t, H, h))
                        else:
                            pe.wait_ge(y_added, at(t, 1, 1))
                        for j in range(G):
                            last = nc.tensor.matmul(s_bank[:, j * P:(j + 1) * P], kT[:, h % 2, j * P:(j + 1) * P],
                                                    qT[:, h % 2, j * P:(j + 1) * P], start=True, stop=True)
                        last.then_inc(scores_made, 1)
                    if step < H:
                        h = step
                        if h:
                            pe.wait_ge(v_done, at(t, H, h))
                        for j in range(G):
                            for k in range(KD):
                                last = nc.tensor.matmul(v_bank[:, j * P:(j + 1) * P], xcur[:, k, j * P:(j + 1) * P],
                                                        wqkv[:, k, h, 2, :], start=(k == 0), stop=(k == KD - 1))
                        last.then_inc(v_made, 1)
                        if h:
                            pe.wait_ge(gate_done, at(t, H, h))
                        for k in range(KD):
                            last = nc.tensor.matmul(g_bank[:, :], wgate[:, k, h, :], xcur[:, k, :],
                                                    start=(k == 0), stop=(k == KD - 1))
                        last.then_inc(g_made, 1)
                        if h == H - 1:
                            pe.wait_ge(g_made, at(t, H, H))
                            pe.sem_inc(xcur_used, 1)
                    if 1 <= step <= H:
                        h = step - 1
                        pe.wait_ge(attn_done, at(t, H, h + 1))
                        pe.wait_ge(v_done, at(t, H, h + 1))
                        if h:
                            pe.wait_ge(sq_done, at(t, H, h))
                        for j in range(G):
                            last = nc.tensor.matmul(o_bank[:, j * P:(j + 1) * P], v[:, h % 2, j * P:(j + 1) * P],
                                                    attn[:, j * P:(j + 1) * P], start=True, stop=True)
                        last.then_inc(o_made, 1)
                    if step >= 2:
                        h = step - 2
                        pe.wait_ge(z_done, at(t, H, h + 1))
                        for j in range(G):
                            last = nc.tensor.matmul(y_bank[j // 2][:, (j % 2) * D:(j % 2 + 1) * D],
                                                    z[:, h % 2, j * P:(j + 1) * P], wout[:, h, :],
                                                    start=(h == 0 and j % 2 == 0), stop=(h == H - 1),
                                                    skip_group_check=True)
                last.then_inc(y_made, 1)
                pe.wait_ge(sumsq_done, at(t, H, H))
                for j in range(G):
                    last = nc.tensor.matmul(s_bank[:, j:j + 1], sumsq[:, j * P:(j + 1) * P],
                                            core.constant("ones")[:, 0:1], start=True, stop=True)
                last.then_inc(ssq_made, 1)

        @block.scalar
        def _(act):
            n_scalar(act)
            act.wait_ge(core.weights_loaded["L0a"], 16)
            nc.scalar.mul(slope, slope, -1.0).then_inc(slope_neg, 1)
            act.wait_ge(slope_neg, 1)
            for h in range(H):
                last = nc.scalar.activation(decay[:, h, :], core.constant("dist"), ACT.Exp, scale=slope[:, h:h + 1])
            last.then_inc(decay_exp, 1)
            with act.Fori(0, GROUPS) as t:
                for step in range(H + 1):
                    if step < H:
                        h = step
                        act.wait_ge(q_made, at(t, H, h + 1))
                        nc.scalar.activation(qT[:, h % 2, :], q_bank[:, :], ACT.Silu).then_inc(qT_done, 1)
                        act.wait_ge(k_made, at(t, H, h + 1))
                        nc.scalar.activation(kT[:, h % 2, :], k_bank[:, :], ACT.Silu).then_inc(kT_done, 1)
                        act.wait_ge(v_made, at(t, H, h + 1))
                        nc.scalar.activation(v[:, h % 2, :], v_bank[:, :], ACT.Silu).then_inc(v_done, 1)
                        act.wait_ge(g_made, at(t, H, h + 1))
                        if h >= 2:
                            act.wait_ge(z_done, at(t, H, h - 1))
                        nc.scalar.activation(gate[:, h % 2, :], g_bank[:, :], ACT.Tanh, scale=0.5).then_inc(gate_done, 1)
                    if step >= 1:
                        h = step - 1
                        act.wait_ge(o_made, at(t, H, h + 1))
                        if h >= 2:
                            act.wait_ge(sumsq_done, at(t, H, h - 1))
                            act.wait_ge(z_done, at(t, H, h - 1))
                        nc.scalar.activation(ow[:, h % 2, :], o_bank[:, :], ACT.Copy, scale=norm_w[:, h:h + 1]).then_inc(ow_done, 1)
                        nc.scalar.activation(sq[:, h % 2, :], o_bank[:, :], ACT.Square).then_inc(sq_done, 1)

        @block.vector
        def _(dve):
            dve.wait_ge(core.x_loaded, 16)
            n_vector(dve)
            dve.wait_ge(core.const_loaded, 16)
            dve.wait_ge(decay_exp, 1)
            nc.vector.tensor_tensor(decay, decay, core.constant("causalT").unsqueeze(1).to_broadcast([P, H, P]),
                                    ALU.mult).then_inc(decay_done, 1)
            dve.wait_ge(decay_done, 1)
            dve.sem_inc(y_added, 1)
            with dve.Fori(0, GROUPS) as t:
                for h in range(H):
                    dve.wait_ge(scores_made, at(t, H, h + 1))
                    nc.vector.tensor_tensor(attn.rearrange("p (j t) -> p j t", j=G),
                                            s_bank[:, :].rearrange("p (j t) -> p j t", j=G),
                                            decay[:, h, :].unsqueeze(1).to_broadcast([P, G, P]),
                                            ALU.mult).then_inc(attn_done, 1)
                    dve.wait_ge(ow_done, at(t, H, h + 1))
                    dve.wait_ge(gate_done, at(t, H, h + 1))
                    nc.vector.scalar_tensor_tensor(out=z[:, h % 2, :], in0=gate[:, h % 2, :], scalar=1.0,
                                                   in1=ow[:, h % 2, :], op0=ALU.add, op1=ALU.mult).then_inc(z_done, 1)
                dve.wait_ge(ssq_made, at(t, 1, 1))
                nc.vector.tensor_scalar(msq, s_bank[:, 0:G], 4.0 / (H * P), 4.0 * EPS, ALU.mult, ALU.add).then_inc(msq_done, 1)
                dve.wait_ge(rms_done, at(t, 1, 1))
                dve.wait_ge(y_made, at(t, 1, 1))
                for j in range(G):
                    xj = core.x[:, bass.ds(t * G + j, 1), :].squeeze(1)
                    last = nc.vector.scalar_tensor_tensor(out=xj, in0=y_bank[j // 2][:, (j % 2) * D:(j % 2 + 1) * D],
                                                          scalar=msq[:, j:j + 1], in1=xj, op0=ALU.mult, op1=ALU.add)
                last.then_inc(y_added, 1)


def channel_cross_attention(core):
    nc, H, C = core.nc, 16, 8
    SCALE = 1.0 / float(np.sqrt(np.float32(C)))
    w = core.weights("L0x")
    with ExitStack() as ctx:
        sem = lambda name: core.sem(f"L0x_{name}", ctx)
        carve = core.work("L0x")
        s = norm_state(core, "L0x", carve, ctx, turn_to_features=False)
        q_all = core.xnT.rearrange("p k b t -> p (k b t)").rearrange("p (b d) -> p b d", b=B)
        v_all = core.ctxT.rearrange("p k b t -> p (k b t)").rearrange("p (b d) -> p b d", b=B)
        k_all = carve(B, D)
        q_cur, v_cur = carve(2, D), carve(2, D)
        k_one = carve(2, 4, D)
        sm, probs, pT = carve(2, 2 * D), carve(2, 2 * D), carve(2, 2 * D)
        biased, sin_part = pT, sm
        mask_in = carve(2 * D)
        keep, fill = carve(2 * D), carve(2 * D)
        peak, peak_neg = carve(2, 2), carve(2, 2)
        total = carve(2, 2, H)
        on, oT = carve(2, D), carve(2, D)
        bank = core.bank
        s_bank, t_bank, o_bank, f_bank, y_bank = bank[0:2], bank[2:4], bank[4:6], bank[6], bank[7]

        mask_loaded, fill_done, keep_done = sem("mask_loaded"), sem("fill_done"), sem("keep_done")
        proj_made, biased_done, turn_made = sem("proj_made"), sem("biased_done"), sem("turn_made")
        cos_done, sin_done, roped = sem("cos_done"), sem("sin_done"), sem("roped")
        v_made, v_done = sem("v_made"), sem("v_done")
        staged, staged_used = sem("staged"), sem("staged_used")
        scores_made, masked, filled, peak_done = sem("scores_made"), sem("masked"), sem("filled"), sem("peak_done")
        exp_done, p_turned, pT_done, o_made = sem("exp_done"), sem("p_turned"), sem("pT_done"), sem("o_made")
        total_inv, on_done, on_turned, oT_done = sem("total_inv"), sem("on_done"), sem("on_turned"), sem("oT_done")
        y_made, y_added = sem("y_made"), sem("y_added")
        block = ctx.enter_context(core.block())
        n_vector, n_gpsimd, _, _ = normalise(core, "L0x", block, s, tokens=q_all)
        UNITS = 2 * H

        @block.sync
        def _(sp):
            sp.dma_start(mask_in.bitcast(I32), core.dram["attn_mask"]).then_inc(mask_loaded, 16)
            core.load(sp, "L0f")

        @block.gpsimd
        def _(pool):
            n_gpsimd(pool)
            pool.wait_ge(roped, B)
            with pool.Fori(0, B // 2) as t:
                for i in range(2):
                    pool.wait_ge(staged_used, at(t, 2, i + 1))
                    pool.wait_ge(v_done, B // 2)
                    nc.gpsimd.tensor_copy(q_cur[:, i, :], q_all[:, bass.ds(2 * t + i, 1), :].squeeze(1))
                    nc.gpsimd.tensor_copy(v_cur[:, i, :], v_all[:, bass.ds(2 * t + i, 1), :].squeeze(1))
                    nc.gpsimd.tensor_tensor(k_one[:, i, :, :], k_all[:, bass.ds(2 * t + i, 1), :].to_broadcast([P, 4, D]),
                                            core.constant("headmask").unsqueeze(2).to_broadcast([P, 4, D]),
                                            ALU.mult).then_inc(staged, 1)

        @block.tensor
        def _(pe):
            pe.wait_ge(core.weights_loaded["L0x"], 16)
            pe.wait_ge(core.const_loaded, 16)
            pe.wait_ge(core.ctx_loaded, 16)
            for i in range(B + 1):
                if i < B:
                    src, wt, b = (q_all, w["q"], 2 * i) if i < B // 2 else (core.ctx_sb, w["k"], 2 * i - B)
                    if i < B // 2:
                        pe.wait_ge(s["xn_done"], b + 2)
                    if i >= 2:
                        pe.wait_ge(biased_done, i - 1)
                    nc.tensor.matmul(bank[i % 2][:, :], wt, src[:, b:b + 2, :].rearrange("p b d -> p (b d)"),
                                     start=True, stop=True).then_inc(proj_made, 1)
                if i >= 1:
                    pe.wait_ge(biased_done, i)
                    if i >= 3:
                        pe.wait_ge(sin_done, i - 2)
                    nc.tensor.matmul(bank[2 + (i - 1) % 2][:, :], core.constant("turn0"), biased[:, (i - 1) % 2, :],
                                     start=True, stop=True).then_inc(turn_made, 1)
            for i in range(B // 2):
                if i >= 2:
                    pe.wait_ge(v_done, i - 1)
                for j in range(4):
                    b, half = 2 * i + j // 2, j % 2
                    last = nc.tensor.matmul(bank[4 + i % 2][:, j * P:(j + 1) * P],
                                            core.ctx_sb[:, b, half * P:(half + 1) * P], w["v"], start=True, stop=True)
                last.then_inc(v_made, 1)
            pe.sem_inc(staged_used, 2)
            with pe.Fori(0, B // 2) as t:
                for step in range(UNITS + 8):
                    if step < UNITS:
                        u, h, i = step, step % H, step // H
                        g, n = h // 4, h % 4
                        if h == 0:
                            pe.wait_ge(staged, at(t, 2, i + 1))
                        if u >= 2:
                            pe.wait_ge(masked, at(t, UNITS, u - 1))
                        for half in range(2):
                            last = nc.tensor.matmul(s_bank[u % 2][:, half * D:(half + 1) * D],
                                                    q_cur[32 * g:32 * g + 32, i, half * P:(half + 1) * P],
                                                    k_one[32 * g:32 * g + 32, i, n, :], start=True, stop=True)
                        last.then_inc(scores_made, 1)
                    if 2 <= step < UNITS + 2:
                        u = step - 2
                        pe.wait_ge(exp_done, at(t, UNITS, u + 1))
                        if u >= 2:
                            pe.wait_ge(pT_done, at(t, UNITS, u - 1))
                        for kh in range(2):
                            for qh in range(2):
                                last = nc.tensor.transpose(t_bank[u % 2][:, kh * D + qh * P:kh * D + (qh + 1) * P],
                                                           probs[:, u % 2, qh * D + kh * P:qh * D + (kh + 1) * P], core.ident)
                        last.then_inc(p_turned, 1)
                    if 3 <= step < UNITS + 3:
                        u = step - 3
                        h, i = u % H, u // H
                        pe.wait_ge(pT_done, at(t, UNITS, u + 1))
                        if u == 0:
                            pe.wait_ge(on_done, at(t, 2, 1))
                        if u == H:
                            pe.wait_ge(on_done, at(t, 2, 2))
                        for qh in range(2):
                            for kh in range(2):
                                last = nc.tensor.matmul(o_bank[i][:, qh * P + h * C:qh * P + (h + 1) * C],
                                                        pT[:, u % 2, kh * D + qh * P:kh * D + (qh + 1) * P],
                                                        v_cur[:, i, kh * P + h * C:kh * P + (h + 1) * C],
                                                        start=(kh == 0), stop=(kh == 1))
                        if h == H - 1:
                            last.then_inc(o_made, 1)
                            pe.wait_ge(o_made, at(t, 2, i + 1))
                            pe.sem_inc(staged_used, 1)
                    for i in range(2):
                        if step == H * (i + 1) + 4:
                            pe.wait_ge(on_done, at(t, 2, i + 3))
                            for half in range(2):
                                last = nc.tensor.transpose(f_bank[:, half * P:(half + 1) * P],
                                                           on[:, i, half * P:(half + 1) * P], core.ident)
                            last.then_inc(on_turned, 1)
                        if step == H * (i + 1) + 6:
                            pe.wait_ge(oT_done, at(t, 2, i + 1))
                            pe.wait_ge(y_added, at(t, 2, i + 1))
                            nc.tensor.matmul(y_bank[:, 0:D], w["o"], oT[:, i, :], start=True, stop=True).then_inc(y_made, 1)

        @block.scalar
        def _(act):
            act.wait_ge(core.weights_loaded["L0x"], 16)
            for i in range(B):
                act.wait_ge(proj_made, i + 1)
                if i >= 2:
                    act.wait_ge(cos_done, i - 1)
                    act.wait_ge(turn_made, i - 1)
                bias = w["bq"] if i < B // 2 else w["bk"]
                nc.scalar.activation(biased[:, i % 2, :], bank[i % 2][:, :], ACT.Identity, bias=bias).then_inc(biased_done, 1)
            with act.Fori(0, B // 2) as t:
                for step in range(UNITS + 7):
                    if 2 <= step < UNITS + 2:
                        u = step - 2
                        act.wait_ge(p_turned, at(t, UNITS, u + 1))
                        nc.scalar.copy(pT[:, u % 2, :], t_bank[u % 2][:, :]).then_inc(pT_done, 1)
                    if step < UNITS:
                        u, h, i = step, step % H, step // H
                        act.wait_ge(peak_done, at(t, UNITS, u + 1))
                        if u >= 2:
                            act.wait_ge(p_turned, at(t, UNITS, u - 1))
                        for half in range(2):
                            last = nc.scalar.activation(probs[:, u % 2, half * D:(half + 1) * D],
                                                        sm[:, u % 2, half * D:(half + 1) * D], ACT.Exp,
                                                        bias=peak_neg[:, u % 2, half:half + 1], scale=SCALE,
                                                        accum_out=total[:, i, half, h:h + 1])
                        last.then_inc(exp_done, 1)
                    for i in range(2):
                        if step == H * (i + 1) + 5:
                            act.wait_ge(on_turned, at(t, 2, i + 1))
                            nc.scalar.copy(oT[:, i, :], f_bank[:, 0:D]).then_inc(oT_done, 1)

        @block.vector
        def _(dve):
            dve.wait_ge(mask_loaded, 16)
            nc.vector.tensor_scalar(fill, mask_in.bitcast(I32), 0.0, -10000.0 / SCALE, ALU.is_equal, ALU.mult).then_inc(fill_done, 1)
            nc.vector.tensor_scalar(keep, mask_in.bitcast(I32), 0.0, None, ALU.not_equal).then_inc(keep_done, 1)
            dve.wait_ge(keep_done, 1)
            dve.wait_ge(fill_done, 1)
            n_vector(dve)
            cos = core.constant("cos0").unsqueeze(1).to_broadcast([P, 2, D])
            sin = core.constant("sin0").unsqueeze(1).to_broadcast([P, 2, D])
            pair = lambda a: a.rearrange("p (b d) -> p b d", b=2)
            for i in range(B):
                dst, b = (q_all, 2 * i) if i < B // 2 else (k_all, 2 * i - B)
                dve.wait_ge(biased_done, i + 1)
                nc.vector.tensor_tensor(dst[:, b:b + 2, :], pair(biased[:, i % 2, :]), cos, ALU.mult).then_inc(cos_done, 1)
                dve.wait_ge(turn_made, i + 1)
                if i >= 2:
                    dve.wait_ge(roped, i - 1)
                nc.vector.tensor_tensor(pair(sin_part[:, i % 2, :]), pair(bank[2 + i % 2][:, :]), sin, ALU.mult).then_inc(sin_done, 1)
                dve.wait_ge(sin_done, i + 1)
                dve.wait_ge(cos_done, i + 1)
                nc.vector.tensor_tensor(dst[:, b:b + 2, :], dst[:, b:b + 2, :], pair(sin_part[:, i % 2, :]), ALU.add).then_inc(roped, 1)
            bv = w["bv"].unsqueeze(1).to_broadcast([P, 4, P])
            for i in range(B // 2):
                dve.wait_ge(v_made, i + 1)
                nc.vector.tensor_tensor(v_all[:, 2 * i:2 * i + 2, :].rearrange("p b (h c) -> p (b h) c", h=2),
                                        bank[4 + i % 2][:, :].rearrange("p (a c) -> p a c", a=4), bv, ALU.add).then_inc(v_done, 1)
            dve.wait_ge(v_done, B // 2)
            dve.wait_ge(roped, B)
            dve.sem_inc(on_done, 2)
            dve.sem_inc(y_added, 1)

            def normalise_heads(t, i):
                dve.wait_ge(o_made, at(t, 2, i + 1))
                nc.vector.reciprocal(total[:, i, :, :], total[:, i, :, :]).then_inc(total_inv, 1)
                dve.wait_ge(total_inv, at(t, 2, i + 1))
                nc.vector.tensor_tensor(on[:, i, :].rearrange("p (a c) -> p a c", c=C),
                                        o_bank[i][:, 0:D].rearrange("p (a c) -> p a c", c=C),
                                        total[:, i, :, :].rearrange("p a h -> p (a h)").unsqueeze(2).to_broadcast([P, 2 * H, C]),
                                        ALU.mult).then_inc(on_done, 1)

            def add_to_x(t, i):
                dve.wait_ge(y_made, at(t, 2, i + 1))
                xb = core.x[:, bass.ds(2 * t + i, 1), :].squeeze(1)
                nc.vector.scalar_tensor_tensor(out=xb, in0=y_bank[:, 0:D], scalar=w["bo"], in1=xb,
                                               op0=ALU.add, op1=ALU.add).then_inc(y_added, 1)

            with dve.Fori(0, B // 2) as t:
                for step in range(UNITS + 8):
                    if step < UNITS:
                        u = step
                        dve.wait_ge(scores_made, at(t, UNITS, u + 1))
                        if u >= 2:
                            dve.wait_ge(exp_done, at(t, UNITS, u - 1))
                        nc.vector.tensor_tensor(sm[:, u % 2, :], s_bank[u % 2][:, :], keep, ALU.mult).then_inc(masked, 1)
                        dve.wait_ge(masked, at(t, UNITS, u + 1))
                        core.held(dve)
                        for half in range(2):
                            part = sm[:, u % 2, half * D:(half + 1) * D]
                            last = nc.vector.tensor_tensor_reduce(out=part, in0=part, in1=fill[:, half * D:(half + 1) * D],
                                                                  scale=1.0, scalar=-3e38, op0=ALU.add, op1=ALU.max,
                                                                  accum_out=peak[:, u % 2, half:half + 1])
                        last.then_inc(filled, 1)
                        dve.wait_ge(filled, at(t, UNITS, u + 1))
                        nc.vector.tensor_scalar(peak_neg[:, u % 2, :], peak[:, u % 2, :], -SCALE, None, ALU.mult).then_inc(peak_done, 1)
                    for i in range(2):
                        if step == H * (i + 1) + 3:
                            normalise_heads(t, i)
                        if step == H * (i + 1) + 7:
                            add_to_x(t, i)


def router(core, name, E, top, kind, s, gate, carve, scratch, ctx, bias=None, scale=1.0, floor=0.0, ones=0):
    nc = core.nc
    logits_bank, turn_bank = core.bank[2], core.bank[3:5]
    R = E + ones
    score, chosen_by, rank, total = carve(B, E), carve(B, E), carve(B, E), carve(B)
    share = carve(B, R)
    shareT = carve(B * P)
    ahead = scratch[:, 0:B * E * E].rearrange("p (b e f) -> p b e f", b=B, e=E)
    tied = scratch[:, B * E * E:2 * B * E * E].rearrange("p (b e f) -> p b e f", b=B, e=E)
    lower = carve(E, E)
    sem = lambda n: core.sem(f"{name}_{n}", ctx)
    logits_made, scored, step_done, share_done, share_turned, shareT_done = (
        sem("logits_made"), sem("scored"), sem("route_step"), sem("share_done"), sem("share_turned"), sem("shareT_done"))
    logits = logits_bank[:, 0:B * E].rearrange("p (b e) -> p b e", b=B)

    def tensor(pe):
        pe.wait_ge(core.weights_loaded[name], 16)
        pe.wait_ge(s["xnT_done"], B // 2)
        for b in range(B):
            for k in range(KD):
                last = nc.tensor.matmul(logits_bank[:, b * E:(b + 1) * E], core.xnT[:, k, b, :],
                                        gate[:, k * E:(k + 1) * E], start=(k == 0), stop=(k == KD - 1))
        last.then_inc(logits_made, 1)
        pe.wait_ge(share_done, 1)
        for i in range(B // 4):
            if i >= 2:
                pe.wait_ge(shareT_done, i - 1)
            for b in range(4 * i, 4 * i + 4):
                last = nc.tensor.matmul(turn_bank[i % 2][0:R, (b % 4) * P:(b % 4 + 1) * P], share[:, b, :],
                                        core.ident, start=True, stop=True)
            last.then_inc(share_turned, 1)

    def scalar(act):
        if kind == "sigmoid":
            act.wait_ge(logits_made, 1)
            nc.scalar.activation(score, logits, ACT.Sigmoid).then_inc(scored, 1)
        else:
            act.wait_ge(step_done, 2)
            nc.scalar.activation(score, score, ACT.Exp).then_inc(scored, 1)
        for i in range(B // 4):
            act.wait_ge(share_turned, i + 1)
            nc.scalar.copy(shareT[0:R, i * N:(i + 1) * N], turn_bank[i % 2][0:R, :]).then_inc(shareT_done, 1)

    def vector(dve):
        done = [0]

        def step(instruction):
            done[0] += 1
            instruction.then_inc(step_done, 1)
            dve.wait_ge(step_done, done[0])

        each = lambda a: a.unsqueeze(2).to_broadcast([P, B, E])
        if kind == "softmax":
            dve.wait_ge(logits_made, 1)
            step(nc.vector.tensor_reduce(total, logits, AX, ALU.max))
            step(nc.vector.tensor_tensor(score, logits, each(total), ALU.subtract))
            dve.wait_ge(scored, 1)
            step(nc.vector.tensor_reduce(total, score, AX, ALU.add))
            step(nc.vector.reciprocal(total, total))
            step(nc.vector.tensor_tensor(score, score, each(total), ALU.mult))
        dve.wait_ge(scored, 1)
        by = score
        if bias is not None:
            step(nc.vector.tensor_tensor(chosen_by, score, bias.unsqueeze(1).to_broadcast([P, B, E]), ALU.add))
            by = chosen_by
        other = by.unsqueeze(2).to_broadcast([P, B, E, E])
        own = by.unsqueeze(3).to_broadcast([P, B, E, E])
        for e in range(E):
            if e:
                nc.vector.memset(lower[:, e, 0:e], 1.0)
            last = nc.vector.memset(lower[:, e, e:E], 0.0)
        step(last)
        step(nc.vector.tensor_tensor(ahead, other, own, ALU.is_gt))
        step(nc.vector.tensor_tensor(tied, other, own, ALU.is_equal))
        step(nc.vector.tensor_tensor(tied, tied, lower.unsqueeze(1).to_broadcast([P, B, E, E]), ALU.mult))
        step(nc.vector.tensor_tensor(ahead, ahead, tied, ALU.add))
        step(nc.vector.tensor_reduce(rank, ahead, AX, ALU.add))
        step(nc.vector.tensor_scalar(rank, rank, float(top), None, ALU.is_lt))
        if kind == "sigmoid":
            step(nc.vector.tensor_tensor(score, score, rank, ALU.mult))
            step(nc.vector.tensor_reduce(total, score, AX, ALU.add))
            step(nc.vector.tensor_scalar(total, total, floor, None, ALU.add))
            step(nc.vector.reciprocal(total, total))
            step(nc.vector.tensor_tensor(score, score, each(total), ALU.mult))
            step(nc.vector.tensor_scalar(share[:, :, 0:E], score, scale, None, ALU.mult))
        else:
            step(nc.vector.scalar_tensor_tensor(out=share[:, :, 0:E], in0=score, scalar=scale, in1=rank,
                                                op0=ALU.mult, op1=ALU.mult))
        nc.vector.memset(share[:, :, E:R] if ones else lower[:, 0, :], scale if ones else 0.0).then_inc(share_done, 1)

    return shareT, shareT_done, (vector, tensor, scalar)


def experts(core, name, E, top, kind, chunks, routed, gated=True, **how):
    nc = core.nc
    w = core.weights(name)
    F = chunks * P
    wg = w["gate"].rearrange("p (k f) -> p k f", k=KD)
    wu = w["up"].rearrange("p (k f) -> p k f", k=KD) if gated else None
    wd = w["down"].rearrange("p (c d) -> p c d", c=chunks)
    select = (w["select"] if "select" in w else core.weights("L3sel")["select"])[0:E, :]
    with ExitStack() as ctx:
        sem = lambda n: core.sem(f"{name}_{n}", ctx)
        carve = core.work(name)
        s = norm_state(core, name, carve, ctx)
        scratch = carve(2 * B * E * E) if E == 16 else carve(max(2 * B * E * E, 3 * 2 * N))
        first, partly, h = (scratch[:, 2 * i * N:2 * (i + 1) * N].rearrange("p (a n) -> p a n", a=2) for i in range(3))
        shareT, shareT_done, (r_vector, r_tensor, r_scalar) = router(
            core, name, E, top, kind, s, w["router"], carve, scratch, ctx, **how)
        g_bank, u_bank, c_bank, y_bank = core.bank[0:2], core.bank[2:4], core.bank[4:6], core.bank[6:8]
        g_made, u_made, c_made = sem("g_made"), sem("u_made"), sem("c_made")
        first_done, partly_done, h_done = sem("first_done"), sem("partly_done"), sem("h_done")
        y_made, y_added = sem("y_made"), sem("y_added")
        block = ctx.enter_context(core.block())
        n_vector, n_gpsimd, n_tensor, n_scalar = normalise(core, name, block, s)
        parts = ([(wg, g_bank, g_made), (wu, u_bank, u_made)] if gated else [(wg, g_bank, g_made)])

        @block.sync
        def _(sp):
            for what in LOADS[name]:
                core.load(sp, what)

        @block.gpsimd
        def _(pool):
            n_gpsimd(pool)

        @block.tensor
        def _(pe):
            n_tensor(pe)
            r_tensor(pe)
            if "select" not in w:
                pe.wait_ge(core.weights_loaded["L3sel"], 16)
            pe.wait_ge(shareT_done, B // 4)
            with pe.Fori(0, GROUPS) as t:
                for step in range(chunks + 1):
                    if step < chunks:
                        c = step
                        if c >= 2:
                            pe.wait_ge(h_done, at(t, chunks, c - 1))
                        elif c == 0:
                            pe.wait_ge(y_added, at(t, 1, 1))
                        for wt, bank, made in parts:
                            for k in range(KD):
                                last = nc.tensor.matmul(
                                    bank[c % 2][:, :], wt[:, k, c * P:(c + 1) * P],
                                    core.xnT[:, k, bass.ds(t * G, G), :], start=(k == 0), stop=(k == KD - 1))
                            last.then_inc(made, 1)
                        if c < routed:
                            nc.tensor.matmul(c_bank[c % 2][:, :], select[:, c * P:(c + 1) * P],
                                             shareT[0:E, bass.ds(t * N, N)], start=True, stop=True).then_inc(c_made, 1)
                    if step >= 1:
                        c = step - 1
                        pe.wait_ge(h_done, at(t, chunks, c + 1))
                        for j in range(G):
                            last = nc.tensor.matmul(y_bank[j // 2][:, (j % 2) * D:(j % 2 + 1) * D],
                                                    h[:, c % 2, j * P:(j + 1) * P], wd[:, c, :],
                                                    start=(c == 0 and j % 2 == 0), stop=(c == chunks - 1),
                                                    skip_group_check=True)
                last.then_inc(y_made, 1)

        @block.scalar
        def _(act):
            n_scalar(act)
            r_scalar(act)
            act.wait_ge(shareT_done, B // 4)
            with act.Fori(0, GROUPS) as t:
                for c in range(chunks):
                    act.wait_ge(g_made, at(t, chunks, c + 1))
                    if c >= 2:
                        act.wait_ge(h_done, at(t, chunks, c - 1))
                    nc.scalar.activation(first[:, c % 2, :], g_bank[c % 2][:, :],
                                         ACT.Silu if gated else ACT.Copy).then_inc(first_done, 1)

        @block.vector
        def _(dve):
            n_vector(dve)
            r_vector(dve)
            dve.sem_inc(y_added, 1)
            with dve.Fori(0, GROUPS) as t:
                for c in range(chunks):
                    dve.wait_ge(first_done, at(t, chunks, c + 1))
                    source = first
                    if gated:
                        dve.wait_ge(u_made, at(t, chunks, c + 1))
                        out = partly if c < routed else h
                        last = nc.vector.tensor_tensor(out[:, c % 2, :], u_bank[c % 2][:, :], first[:, c % 2, :], ALU.mult)
                        source = partly
                    if c < routed:
                        dve.wait_ge(c_made, at(t, routed, c + 1))
                        if gated:
                            last.then_inc(partly_done, 1)
                            dve.wait_ge(partly_done, at(t, routed, c + 1))
                        last = nc.vector.tensor_tensor(h[:, c % 2, :], c_bank[c % 2][:, :], source[:, c % 2, :], ALU.mult)
                    last.then_inc(h_done, 1)
                dve.wait_ge(y_made, at(t, 1, 1))
                for j in range(G):
                    xj = core.x[:, bass.ds(t * G + j, 1), :].squeeze(1)
                    last = nc.vector.tensor_tensor(xj, y_bank[j // 2][:, (j % 2) * D:(j % 2 + 1) * D], xj, ALU.add)
                last.then_inc(y_added, 1)


def experts_0(core):
    experts(core, "L0f", 8, 2, "sigmoid", 14, 11, scale=2.5, floor=1e-20)


def experts_2(core):
    experts(core, "L2f", 8, 1, "softmax", 4, 4, gated=False, scale=4.0)


def experts_3(core):
    experts(core, "L3f", 16, 6, "softmax", 25, 22)


LOADS = {"L0f": ["L1a"], "L1f": ["L1f", "L2a"], "L2a": [], "L2x": ["L2f", "L3a", "L3f"], "L2f": [], "L3a": [],
         "L3x": ["L3sel"], "L3f": []}


def power_attention(core):
    nc, HQ, HK, OFFSET, EPS = core.nc, 16, 8, 6.906768, 1e-6
    SCALE = 1.0 / 128 ** 0.5
    w = core.weights("L1a")
    wq = w["q"].rearrange("p (k h n) -> p k h n", k=KD, h=HQ)
    wk = w["k"].rearrange("p (k h n) -> p k h n", k=KD, h=HK)
    wv = w["v"].rearrange("p (k h n) -> p k h n", k=KD, h=HK)
    wc = w["c"].rearrange("p (h n) -> p h n", h=HQ)
    with ExitStack() as ctx:
        sem = lambda n: core.sem(f"L1a_{n}", ctx)
        carve = core.work("L1a")
        s = norm_state(core, "L1a", carve, ctx)
        xcur = s["xn"].rearrange("p a d -> p (a d)").rearrange("p (k n) -> p k n", k=KD)
        qT, kT, v, a, z, decay = (carve(2, N) for _ in range(6))
        sq, spread_log, norm = carve(N), carve(N), carve(N)
        log_g, soft, cum_neg = carve(B, HK), carve(B, HK), carve(B, HK)
        q_bank, kv_bank, w_bank, s_bank, o_bank, n_bank = core.bank[0:6]
        y_bank = core.bank[6:8]
        causalT, ones = core.constant("causalT"), core.constant("ones")
        over_t = lambda m: m.unsqueeze(1).to_broadcast([P, G, P])
        quads = lambda m: m.rearrange("p (j t) -> p j t", j=G)

        g_made, z_done0, exp0_done, soft_done, log_done, cum_made, cum_done = (
            sem("g_made"), sem("gate_step"), sem("exp0_done"), sem("soft_done"), sem("log_done"), sem("cum_made"), sem("cum_done"))
        xcur_done, xcur_used = sem("xcur_done"), sem("xcur_used")
        spread_done, w_made, diff_done, capped, decay_done = (
            sem("spread_done"), sem("w_made"), sem("diff_done"), sem("capped"), sem("decay_done"))
        k_made, v_made, q_made, kT_done, v_done, qT_done = (
            sem("k_made"), sem("v_made"), sem("q_made"), sem("kT_done"), sem("v_done"), sem("qT_done"))
        scores_made, sq_done, a_done, o_made, norm_step, z_done = (
            sem("scores_made"), sem("sq_done"), sem("a_done"), sem("o_made"), sem("norm_step"), sem("z_done"))
        y_made, y_added, added = sem("y_made"), sem("y_added"), sem("added")
        block = ctx.enter_context(core.block())
        n_vector, n_gpsimd, n_tensor, n_scalar = normalise(core, "L1a", block, s)

        @block.sync
        def _(sp):
            core.load(sp, "L1x")

        @block.gpsimd
        def _(pool):
            n_gpsimd(pool)
            pool.wait_ge(log_done, 1)
            with pool.Fori(0, GROUPS) as t:
                pool.wait_ge(xcur_used, at(t, 1, 1))
                core.held(pool)
                nc.gpsimd.tensor_copy(xcur.rearrange("p k (b t) -> p k b t", b=G),
                                      core.xnT[:, :, bass.ds(t * G, G), :]).then_inc(xcur_done, 1)

                def spread_logs(i):
                    if i:
                        pool.wait_ge(w_made, at(t, HK, i))
                    nc.gpsimd.tensor_tensor(quads(spread_log), over_t(causalT),
                                            log_g[:, bass.ds(t * G, G), i:i + 1].to_broadcast([P, G, P]),
                                            ALU.mult).then_inc(spread_done, 1)

                for i in range(HK):
                    spread_logs(i)

        @block.tensor
        def _(pe):
            n_tensor(pe)
            pe.sem_inc(xcur_used, 1)
            pe.wait_ge(core.weights_loaded["L1a"], 16)
            pe.wait_ge(s["xnT_done"], B // 2)
            for b in range(B):
                for k in range(KD):
                    last = nc.tensor.matmul(q_bank[:, b * HK:(b + 1) * HK], core.xnT[:, k, b, :],
                                            w["g"][:, k * HK:(k + 1) * HK], start=(k == 0), stop=(k == KD - 1))
            last.then_inc(g_made, 1)
            pe.wait_ge(log_done, 1)
            nc.tensor.matmul(q_bank[:, 0:B * HK], causalT, log_g.rearrange("p b h -> p (b h)"),
                             start=True, stop=True).then_inc(cum_made, 1)
            pe.wait_ge(cum_done, 1)
            with pe.Fori(0, GROUPS) as t:
                pe.wait_ge(xcur_done, at(t, 1, 1))
                for step in range(HQ + 3):
                    i = step // 2
                    if step < HQ and step % 2 == 0:
                        if i:
                            pe.wait_ge(v_done, at(t, HK, i))
                        for k in range(KD):
                            last = nc.tensor.matmul(kv_bank[:, :], wk[:, k, i, :], xcur[:, k, :],
                                                    start=(k == 0), stop=(k == KD - 1))
                        last.then_inc(k_made, 1)
                    if 1 <= step <= HQ:
                        u = step - 1
                        pe.wait_ge(qT_done, at(t, HQ, u + 1))
                        pe.wait_ge(kT_done, at(t, HK, u // 2 + 1))
                        if u:
                            pe.wait_ge(sq_done, at(t, HQ, u))
                        for j in range(G):
                            last = nc.tensor.matmul(s_bank[:, j * P:(j + 1) * P], kT[:, u // 2 % 2, j * P:(j + 1) * P],
                                                    qT[:, u % 2, j * P:(j + 1) * P], start=True, stop=True)
                        last.then_inc(scores_made, 1)
                    if step < HQ:
                        u = step
                        if u:
                            pe.wait_ge(qT_done, at(t, HQ, u))
                        for k in range(KD):
                            last = nc.tensor.matmul(q_bank[:, :], wq[:, k, u, :], xcur[:, k, :],
                                                    start=(k == 0), stop=(k == KD - 1))
                        last.then_inc(q_made, 1)
                    if step < HQ and step % 2 == 0:
                        pe.wait_ge(spread_done, at(t, HK, i + 1))
                        if i:
                            pe.wait_ge(diff_done, at(t, HK, i))
                        nc.tensor.matmul(w_bank[:, :], ones, spread_log, start=True, stop=True).then_inc(w_made, 1)
                        pe.wait_ge(kT_done, at(t, HK, i + 1))
                        for j in range(G):
                            for k in range(KD):
                                last = nc.tensor.matmul(kv_bank[:, j * P:(j + 1) * P], xcur[:, k, j * P:(j + 1) * P],
                                                        wv[:, k, i, :], start=(k == 0), stop=(k == KD - 1))
                        last.then_inc(v_made, 1)
                    if step == HQ - 1:
                        pe.wait_ge(q_made, at(t, HQ, HQ))
                        pe.sem_inc(xcur_used, 1)
                    if step >= 3:
                        u = step - 3
                        pe.wait_ge(z_done, at(t, HQ, u + 1))
                        if u == 0:
                            pe.wait_ge(y_added, at(t, 1, 1))
                        for j in range(G):
                            last = nc.tensor.matmul(y_bank[j // 2][:, (j % 2) * D:(j % 2 + 1) * D],
                                                    z[:, u % 2, j * P:(j + 1) * P], wc[:, u, :],
                                                    start=(u == 0 and j % 2 == 0), stop=(u == HQ - 1),
                                                    skip_group_check=True)
                        if u == HQ - 1:
                            last.then_inc(y_made, 1)
                    if 2 <= step <= HQ + 1:
                        u = step - 2
                        pe.wait_ge(a_done, at(t, HQ, u + 1))
                        pe.wait_ge(v_done, at(t, HK, u // 2 + 1))
                        if u:
                            pe.wait_ge(z_done, at(t, HQ, u))
                        for j in range(G):
                            nc.tensor.matmul(o_bank[:, j * P:(j + 1) * P], v[:, u // 2 % 2, j * P:(j + 1) * P],
                                             a[:, u % 2, j * P:(j + 1) * P], start=True, stop=True)
                        nc.tensor.matmul(n_bank[:, :], ones, a[:, u % 2, :], start=True, stop=True).then_inc(o_made, 1)

        @block.scalar
        def _(act):
            n_scalar(act)
            act.wait_ge(z_done0, 2)
            nc.scalar.activation(soft, soft, ACT.Exp).then_inc(exp0_done, 1)
            act.wait_ge(exp0_done, 1)
            nc.scalar.activation(soft, soft, ACT.Ln, bias=1.0).then_inc(soft_done, 1)
            with act.Fori(0, GROUPS) as t:
                for step in range(HQ + 1):
                    i = step // 2
                    if step < HQ and step % 2 == 0:
                        act.wait_ge(k_made, at(t, HK, i + 1))
                        nc.scalar.copy(kT[:, i % 2, :], kv_bank[:, :]).then_inc(kT_done, 1)
                    if 1 <= step <= HQ:
                        u = step - 1
                        act.wait_ge(scores_made, at(t, HQ, u + 1))
                        if u:
                            act.wait_ge(a_done, at(t, HQ, u))
                        nc.scalar.activation(sq, s_bank[:, :], ACT.Square, scale=SCALE).then_inc(sq_done, 1)
                    if step < HQ:
                        u = step
                        act.wait_ge(q_made, at(t, HQ, u + 1))
                        nc.scalar.copy(qT[:, u % 2, :], q_bank[:, :]).then_inc(qT_done, 1)
                    if step < HQ and step % 2 == 0:
                        act.wait_ge(v_made, at(t, HK, i + 1))
                        nc.scalar.copy(v[:, i % 2, :], kv_bank[:, :]).then_inc(v_done, 1)
                        act.wait_ge(capped, at(t, HK, i + 1))
                        nc.scalar.activation(decay[:, i % 2, :], decay[:, i % 2, :], ACT.Exp).then_inc(decay_done, 1)

        @block.vector
        def _(dve):
            n_vector(dve)
            gates = q_bank[:, 0:B * HK].rearrange("p (b h) -> p b h", b=B)
            dve.wait_ge(g_made, 1)
            nc.vector.tensor_scalar(log_g, gates, OFFSET, None, ALU.add).then_inc(z_done0, 1)
            dve.wait_ge(z_done0, 1)
            nc.vector.scalar_tensor_tensor(out=soft, in0=log_g, scalar=-1.0, in1=log_g,
                                           op0=ALU.mult, op1=ALU.min).then_inc(z_done0, 1)
            dve.wait_ge(z_done0, 2)
            nc.vector.tensor_scalar(log_g, log_g, 0.0, None, ALU.min).then_inc(z_done0, 1)
            dve.wait_ge(z_done0, 3)
            dve.wait_ge(soft_done, 1)
            nc.vector.tensor_tensor(log_g, log_g, soft, ALU.subtract).then_inc(log_done, 1)
            dve.wait_ge(cum_made, 1)
            nc.vector.tensor_scalar(cum_neg, gates, -1.0, None, ALU.mult).then_inc(cum_done, 1)
            dve.wait_ge(cum_done, 1)
            dve.sem_inc(y_added, 1)
            with dve.Fori(0, GROUPS) as t:

                def normalise_head(u):
                    dve.wait_ge(o_made, at(t, HQ, u + 1))
                    nc.vector.tensor_scalar(norm, n_bank[:, :], EPS, None, ALU.add).then_inc(norm_step, 1)
                    dve.wait_ge(norm_step, at(t, 2 * HQ, 2 * u + 1))
                    nc.vector.reciprocal(norm, norm).then_inc(norm_step, 1)
                    dve.wait_ge(norm_step, at(t, 2 * HQ, 2 * u + 2))
                    nc.vector.tensor_tensor(z[:, u % 2, :], o_bank[:, :], norm, ALU.mult).then_inc(z_done, 1)

                for step in range(HQ + 2):
                    if step < HQ and step % 2 == 0:
                        i = step // 2
                        dve.wait_ge(w_made, at(t, HK, i + 1))
                        nc.vector.tensor_tensor(quads(decay[:, i % 2, :]), quads(w_bank[:, :]),
                                                cum_neg[:, bass.ds(t * G, G), i:i + 1].to_broadcast([P, G, P]),
                                                ALU.add).then_inc(diff_done, 1)
                        dve.wait_ge(diff_done, at(t, HK, i + 1))
                        nc.vector.tensor_tensor(quads(decay[:, i % 2, :]), quads(decay[:, i % 2, :]),
                                                over_t(core.constant("causal_cap")), ALU.min).then_inc(capped, 1)
                    if 1 <= step <= HQ:
                        u = step - 1
                        if u % 2 == 0:
                            dve.wait_ge(decay_done, at(t, HK, u // 2 + 1))
                        dve.wait_ge(sq_done, at(t, HQ, u + 1))
                        nc.vector.tensor_tensor(a[:, u % 2, :], sq, decay[:, u // 2 % 2, :], ALU.mult).then_inc(a_done, 1)
                    if step >= 2:
                        normalise_head(step - 2)
                dve.wait_ge(y_made, at(t, 1, 1))
                for j in range(G):
                    xj = core.x[:, bass.ds(t * G + j, 1), :].squeeze(1)
                    nc.vector.tensor_tensor(xj, y_bank[j // 2][:, (j % 2) * D:(j % 2 + 1) * D], xj, ALU.add).then_inc(added, 1)
                dve.wait_ge(added, at(t, G, G))
                xg = core.x[:, bass.ds(t * G, G), :]
                nc.vector.tensor_tensor(xg, xg, w["bc"].unsqueeze(1).to_broadcast([P, G, D]), ALU.add).then_inc(y_added, 1)


def context_features(core, pe, act, made, done, banks):
    nc = core.nc
    if pe is not None:
        pe.wait_ge(core.ctx_loaded, 16)
        for i in range(B // 2):
            if i >= 2:
                pe.wait_ge(done, i - 1)
            for k in range(KD):
                for b in (2 * i, 2 * i + 1):
                    last = nc.tensor.transpose(banks[i % 2][:, k * 256 + (b % 2) * P:k * 256 + (b % 2) * P + P],
                                               core.ctx_sb[:, b, k * P:(k + 1) * P], core.ident)
            last.then_inc(made, 1)
    else:
        for i in range(B // 2):
            act.wait_ge(made, i + 1)
            nc.scalar.activation(core.ctxT[:, :, 2 * i:2 * i + 2, :],
                                 banks[i % 2][:, :].rearrange("p (k b t) -> p k b t", k=KD, b=2),
                                 ACT.Copy).then_inc(done, 1)


def rotary_cross_attention(core):
    nc, EPS, HD = core.nc, 1e-6, 128
    w = core.weights("L1x")
    proj = {n: w[n].rearrange("p (k n) -> p k n", k=KD) for n in ("q", "k", "v", "kc", "vc")}
    wo = w["o"].rearrange("p (h n) -> p h n", h=16)
    KINDS = ["k", "kc", "q0", "v", "vc", "q1", "q2", "q3"]
    NP, NU = 2 * len(KINDS), 16
    ROPES = [n for n in range(NP) if KINDS[n % 8][0] != "v"]
    VALUES = [n for n in range(NP) if KINDS[n % 8][0] == "v"]
    NR, NV = len(ROPES), len(VALUES)
    LEAD, LAG_T, LAG_O, LAG_Y, LAG_X = 8, 2, 3, 4, 3
    STEPS = LEAD + NU + LAG_Y
    ready = {}
    for r, n in enumerate(ROPES):
        ready[(n // 8, KINDS[n % 8])] = r + 1
    with ExitStack() as ctx:
        sem = lambda n: core.sem(f"L1x_{n}", ctx)
        carve = core.work("L1x")
        s = norm_state(core, "L1x", carve, ctx)
        xcur = carve(KD, 2 * P)
        ccur = carve(KD, 2 * P)
        raw, cos_part, sin_part, turned_in = carve(2, 512), carve(2, 512), carve(2, 512), carve(2, 512)
        square = carve(512)
        sums = carve(2, 24)
        qT, kT, v = carve(2, 16, P), carve(2, 4, 2 * P), carve(2, 2, 512)
        sm, probs, pT, oT = s["xn"].rearrange("p (a b) d -> p a (b d)", a=2), carve(2, 512), carve(2, 512), carve(2, 256)
        peak, peak_neg, total = carve(2, 2), carve(2, 2), carve(2, 2)
        minus_one = carve(2)
        visible = carve(2, P)
        tables = {c: (carve(HD), carve(HD)) for c in "qk"}
        half = s["half"]
        p_bank, x_bank, s_bank, t_bank, o_bank, y_bank = (
            core.bank[0:2], core.bank[2], core.bank[3], core.bank[4], core.bank[5], core.bank[6:8])

        ctx_turned, ctxT_done = sem("ctx_turned"), sem("ctxT_done")
        tables_done, staged, staged_used = sem("tables_done"), sem("staged"), sem("staged_used")
        piece_made, raw_done, square_done, sums_done, factor_done = (
            sem("piece_made"), sem("raw_done"), sem("square_done"), sem("sums_done"), sem("factor_done"))
        reduced, parts_done, roped, rope_turned, rope_done, v_done = (
            sem("reduced"), sem("parts_done"), sem("roped"), sem("rope_turned"), sem("rope_done"), sem("v_done"))
        added = sem("pool_added")
        scores_made, masked, peak_done, exp_done, total_inv, p_done = (
            sem("scores_made"), sem("masked"), sem("peak_done"), sem("exp_done"), sem("total_inv"), sem("p_done"))
        p_turned, pT_done, o_made, oT_done, y_made, y_added = (
            sem("p_turned"), sem("pT_done"), sem("o_made"), sem("oT_done"), sem("y_made"), sem("y_added"))
        block = ctx.enter_context(core.block())
        n_vector, n_gpsimd, n_tensor, n_scalar = normalise(core, "L1x", block, s)
        heads = lambda a: a.rearrange("p (h d) -> p h d", h=4)
        over = lambda a: a.unsqueeze(1).to_broadcast([P, 4, a.shape[1]])

        @block.gpsimd
        def _(pool):
            nc.gpsimd.memset(minus_one, -1.0)
            n_gpsimd(pool)
            pool.wait_ge(ctxT_done, B // 2)
            with pool.Fori(0, B // 2) as t:
                pool.wait_ge(staged_used, at(t, 1, 1))
                core.held(pool)
                pool.wait_ge(s["xnT_done"], B // 2)
                nc.gpsimd.tensor_copy(xcur.rearrange("p k (b t) -> p k b t", b=2), core.xnT[:, :, bass.ds(t * 2, 2), :])
                nc.gpsimd.tensor_copy(ccur.rearrange("p k (b t) -> p k b t", b=2),
                                      core.ctxT[:, :, bass.ds(t * 2, 2), :]).then_inc(staged, 1)
                for step in range(LEAD + NU):
                    if step in ROPES:
                        r, i, kind, n = ROPES.index(step), step // 8, KINDS[step % 8], step
                        col = {"k": 0, "kc": 4}.get(kind, 8 + 4 * int(kind[1]) if kind[0] == "q" else 0)
                        factor = sums[:, i, col:col + 4]
                        pool.wait_ge(sums_done, at(t, NR, r + 1))
                        nc.gpsimd.tensor_tensor(factor, factor, half[:, 0:4], ALU.pow).then_inc(factor_done, 1)
                        pool.wait_ge(parts_done, at(t, NR, r + 1))
                        if r >= 2:
                            pool.wait_ge(rope_turned, at(t, NR, r - 1))
                        out, by = heads(turned_in[:, r % 2, :]), factor.unsqueeze(2).to_broadcast([P, 4, HD])
                        if kind == "kc":
                            pool.wait_ge(factor_done, at(t, NR, r + 1))
                            nc.gpsimd.tensor_tensor(out, heads(cos_part[:, r % 2, :]), by, ALU.mult).then_inc(roped, 1)
                        else:
                            last = nc.gpsimd.tensor_tensor(turned_in[:, r % 2, :], cos_part[:, r % 2, :],
                                                           sin_part[:, r % 2, :], ALU.add)
                            if kind == "k":
                                last.then_inc(added, 1)
                                pool.wait_ge(added, at(t, 2, i + 1))
                                pool.wait_ge(factor_done, at(t, NR, r + 1))
                                last = nc.gpsimd.tensor_tensor(out, out, by, ALU.mult)
                            last.then_inc(roped, 1)
                    if step >= LEAD:
                        u = step - LEAD
                        pool.wait_ge(exp_done, at(t, NU, u + 1))
                        nc.gpsimd.tensor_tensor(total[:, u % 2, :], total[:, u % 2, :], minus_one, ALU.pow).then_inc(total_inv, 1)
                        pool.wait_ge(total_inv, at(t, NU, u + 1))
                        p2 = probs[:, u % 2, :].rearrange("p (h d) -> p h d", h=2)
                        nc.gpsimd.tensor_tensor(p2, p2, total[:, u % 2, :].unsqueeze(2).to_broadcast([P, 2, 256]),
                                                ALU.mult).then_inc(p_done, 1)

        @block.tensor
        def _(pe):
            n_tensor(pe)
            context_features(core, pe, None, ctx_turned, ctxT_done, core.bank[2:4])
            pe.wait_ge(s["xnT_done"], B // 2)
            pe.wait_ge(ctxT_done, B // 2)
            pe.sem_inc(staged_used, 1)
            pe.wait_ge(core.weights_loaded["L1x"], 16)
            with pe.Fori(0, B // 2) as t:
                pe.wait_ge(staged, at(t, 1, 1))
                for step in range(STEPS):
                    if step < NP:
                        n, i, kind = step, step // 8, KINDS[step % 8]
                        src = ccur if kind[-1] == "c" else xcur
                        rhs = proj["q"][:, :, 512 * int(kind[1]):512 * int(kind[1]) + 512] if kind[0] == "q" else proj[kind]
                        if n >= 2:
                            pe.wait_ge(raw_done, at(t, NR, sum(m < n - 1 for m in ROPES)))
                            if any(m < n - 1 for m in VALUES):
                                pe.wait_ge(v_done, at(t, NV, sum(m < n - 1 for m in VALUES)))
                        for k in range(KD):
                            last = nc.tensor.matmul(p_bank[n % 2][:, :], src[:, k, i * P:(i + 1) * P], rhs[:, k, :],
                                                    start=(k == 0), stop=(k == KD - 1))
                        last.then_inc(piece_made, 1)
                        if n == NP - 1:
                            pe.wait_ge(piece_made, at(t, NP, NP))
                            pe.sem_inc(staged_used, 1)
                    if step - LAG_X in ROPES:
                        r = ROPES.index(step - LAG_X)
                        pe.wait_ge(roped, at(t, NR, r + 1))
                        if r:
                            pe.wait_ge(rope_done, at(t, NR, r))
                        for h in range(4):
                            last = nc.tensor.transpose(x_bank[:, h * P:(h + 1) * P],
                                                       turned_in[:, r % 2, h * P:(h + 1) * P], core.ident)
                        last.then_inc(rope_turned, 1)
                    if LEAD <= step < LEAD + NU:
                        u = step - LEAD
                        i, m = u // 8, u % 8
                        need = max(ready[(i, "k")], ready[(i, "kc")], ready[(i, f"q{m // 2}")])
                        pe.wait_ge(rope_done, at(t, NR, need))
                        if u:
                            pe.wait_ge(masked, at(t, NU, u))
                        for hh in range(2):
                            last = nc.tensor.matmul(s_bank[:, hh * 256:(hh + 1) * 256], qT[:, i, 2 * m + hh, :],
                                                    kT[:, i, m // 2, :], start=True, stop=True)
                        last.then_inc(scores_made, 1)
                    if LEAD + LAG_T <= step < LEAD + LAG_T + NU:
                        u = step - LEAD - LAG_T
                        pe.wait_ge(p_done, at(t, NU, u + 1))
                        if u:
                            pe.wait_ge(pT_done, at(t, NU, u))
                        for c in range(4):
                            last = nc.tensor.transpose(t_bank[:, c * P:(c + 1) * P], probs[:, u % 2, c * P:(c + 1) * P], core.ident)
                        last.then_inc(p_turned, 1)
                    if LEAD + LAG_O <= step < LEAD + LAG_O + NU:
                        u = step - LEAD - LAG_O
                        i, m = u // 8, u % 8
                        pe.wait_ge(pT_done, at(t, NU, u + 1))
                        pe.wait_ge(v_done, at(t, NV, 2 * i + 2))
                        if u:
                            pe.wait_ge(oT_done, at(t, NU, u))
                        for hh in range(2):
                            for c in range(2):
                                kv = m // 2
                                last = nc.tensor.matmul(o_bank[:, hh * P:(hh + 1) * P],
                                                        v[:, i, c, kv * HD:(kv + 1) * HD],
                                                        pT[:, u % 2, (2 * hh + c) * P:(2 * hh + c + 1) * P],
                                                        start=(c == 0), stop=(c == 1))
                        last.then_inc(o_made, 1)
                    if LEAD + LAG_Y <= step:
                        u = step - LEAD - LAG_Y
                        i, m = u // 8, u % 8
                        pe.wait_ge(oT_done, at(t, NU, u + 1))
                        if m == 0:
                            pe.wait_ge(y_added, at(t, 2, i + 1))
                        for hh in range(2):
                            last = nc.tensor.matmul(y_bank[i][:, 0:D], oT[:, u % 2, hh * P:(hh + 1) * P],
                                                    wo[:, 2 * m + hh, :], start=(m == 0 and hh == 0), stop=(m == 7 and hh == 1))
                        if m == 7:
                            last.then_inc(y_made, 1)

        @block.scalar
        def _(act):
            n_scalar(act)
            context_features(core, None, act, ctx_turned, ctxT_done, core.bank[2:4])
            with act.Fori(0, B // 2) as t:
                for step in range(LEAD + NU + LAG_O):
                    if step in ROPES:
                        n, r = step, ROPES.index(step)
                        act.wait_ge(piece_made, at(t, NP, n + 1))
                        if r >= 2:
                            act.wait_ge(parts_done, at(t, NR, r - 1))
                        nc.scalar.copy(raw[:, r % 2, :], p_bank[n % 2][:, :]).then_inc(raw_done, 1)
                        act.wait_ge(raw_done, at(t, NR, r + 1))
                        if r:
                            act.wait_ge(reduced, at(t, NR, r))
                        nc.scalar.activation(square, raw[:, r % 2, :], ACT.Square).then_inc(square_done, 1)
                    if step in VALUES:
                        n, i = step, step // 8
                        act.wait_ge(piece_made, at(t, NP, n + 1))
                        nc.scalar.copy(v[:, i, 0 if KINDS[n % 8] == "vc" else 1, :], p_bank[n % 2][:, :]).then_inc(v_done, 1)
                    if LEAD + LAG_T <= step < LEAD + LAG_T + NU:
                        u = step - LEAD - LAG_T
                        act.wait_ge(p_turned, at(t, NU, u + 1))
                        nc.scalar.copy(pT[:, u % 2, :], t_bank[:, :]).then_inc(pT_done, 1)
                    if LEAD <= step < LEAD + NU:
                        u = step - LEAD
                        i, m = u // 8, u % 8
                        act.wait_ge(peak_done, at(t, NU, u + 1))
                        if u >= 2:
                            act.wait_ge(p_turned, at(t, NU, u - 1))
                        for hh in range(2):
                            h = 2 * m + hh
                            last = nc.scalar.activation(probs[:, u % 2, hh * 256:(hh + 1) * 256], sm[:, u % 2, hh * 256:(hh + 1) * 256],
                                                        ACT.Exp, bias=peak_neg[:, u % 2, hh:hh + 1],
                                                        scale=sums[:, i, 8 + h:9 + h], accum_out=total[:, u % 2, hh:hh + 1])
                        last.then_inc(exp_done, 1)
                    if LEAD + LAG_O <= step:
                        u = step - LEAD - LAG_O
                        act.wait_ge(o_made, at(t, NU, u + 1))
                        nc.scalar.copy(oT[:, u % 2, :], o_bank[:, 0:256]).then_inc(oT_done, 1)

        @block.vector
        def _(dve):
            n_vector(dve)
            dve.wait_ge(core.weights_loaded["L1x"], 16)
            cos, sin = core.constant("cos1"), core.constant("sin1")
            for c, wn in (("q", w["qn"]), ("k", w["kn"])):
                cw, sw = tables[c]
                for lo in (0, 64):
                    nc.vector.tensor_tensor(cw[:, lo:lo + 64], cos, wn[:, lo:lo + 64], ALU.mult)
                nc.vector.scalar_tensor_tensor(out=sw[:, 0:64], in0=sin, scalar=-1.0, in1=wn[:, 64:128], op0=ALU.mult, op1=ALU.mult)
                nc.vector.tensor_tensor(sw[:, 64:128], sin, wn[:, 0:64], ALU.mult)
            nc.vector.memset(visible[:, 0, :], 0.0)
            nc.vector.tensor_copy(visible[:, 1, :], core.constant("causal_bias")).then_inc(tables_done, 1)
            dve.wait_ge(tables_done, 1)
            dve.sem_inc(y_added, 2)
            with dve.Fori(0, B // 2) as t:

                def add_to_x(i):
                    dve.wait_ge(y_made, at(t, 2, i + 1))
                    xb = core.x[:, bass.ds(2 * t + i, 1), :].squeeze(1)
                    nc.vector.tensor_tensor(xb, y_bank[i][:, 0:D], xb, ALU.add).then_inc(y_added, 1)

                for step in range(LEAD + NU):
                    if LEAD <= step:
                        u = step - LEAD
                        i, m = u // 8, u % 8
                        dve.wait_ge(scores_made, at(t, NU, u + 1))
                        if u >= 2:
                            dve.wait_ge(exp_done, at(t, NU, u - 1))
                        dve.wait_ge(factor_done, at(t, NR, ready[(i, f"q{m // 2}")]))
                        core.held(dve)
                        for hh in range(2):
                            last = nc.vector.tensor_tensor_reduce(
                                out=sm[:, u % 2, hh * 256:(hh + 1) * 256], in0=s_bank[:, hh * 256:(hh + 1) * 256],
                                in1=visible.rearrange("p a b -> p (a b)"), scale=1.0, scalar=-3e38, op0=ALU.add, op1=ALU.max,
                                accum_out=peak[:, u % 2, hh:hh + 1])
                        last.then_inc(masked, 1)
                        dve.wait_ge(masked, at(t, NU, u + 1))
                        nc.vector.scalar_tensor_tensor(out=peak_neg[:, u % 2, :], in0=peak[:, u % 2, :], scalar=-1.0,
                                                       in1=sums[:, i, 8 + 2 * m:10 + 2 * m], op0=ALU.mult,
                                                       op1=ALU.mult).then_inc(peak_done, 1)
                    if step in ROPES:
                        r, i, kind = ROPES.index(step), step // 8, KINDS[step % 8]
                        col = {"k": 0, "kc": 4}.get(kind, 8 + 4 * int(kind[1]) if kind[0] == "q" else 0)
                        into = sums[:, i, col:col + 4]
                        cw, sw = tables[kind[0]]
                        dve.wait_ge(raw_done, at(t, NR, r + 1))
                        if r >= 2:
                            dve.wait_ge(roped, at(t, NR, r - 1))
                        part, src = heads(cos_part[:, r % 2, :]), heads(raw[:, r % 2, :])
                        if kind == "kc":
                            last = nc.vector.tensor_tensor(part, src, over(w["kn"]), ALU.mult)
                        else:
                            nc.vector.tensor_tensor(part, src, over(cw), ALU.mult)
                            part = heads(sin_part[:, r % 2, :])
                            nc.vector.tensor_tensor(part[:, :, 0:64], src[:, :, 64:128], over(sw[:, 0:64]), ALU.mult)
                            last = nc.vector.tensor_tensor(part[:, :, 64:128], src[:, :, 0:64], over(sw[:, 64:128]), ALU.mult)
                        last.then_inc(parts_done, 1)
                        dve.wait_ge(square_done, at(t, NR, r + 1))
                        nc.vector.tensor_reduce(into, heads(square), AX, ALU.add).then_inc(reduced, 1)
                        dve.wait_ge(reduced, at(t, NR, r + 1))
                        if kind[0] == "k":
                            nc.vector.tensor_scalar(into, into, 1.0 / HD, EPS, ALU.mult, ALU.add).then_inc(sums_done, 1)
                        else:
                            nc.vector.tensor_scalar(into, into, HD * EPS, None, ALU.add).then_inc(sums_done, 1)
                    if step - LAG_X in ROPES:
                        n = step - LAG_X
                        r, i, kind = ROPES.index(n), n // 8, KINDS[n % 8]
                        dve.wait_ge(rope_turned, at(t, NR, r + 1))
                        if kind[0] == "q":
                            out = qT[:, i, 4 * int(kind[1]):4 * int(kind[1]) + 4, :]
                        else:
                            own = 0 if kind == "kc" else P
                            out = kT[:, i, :, own:own + P]
                        nc.vector.tensor_copy(out, heads(x_bank[:, :])).then_inc(rope_done, 1)
                    if step == LEAD + 8 + LAG_Y:
                        add_to_x(0)
                add_to_x(1)


def sink_attention(core):
    nc, HD = core.nc, 64
    w = core.weights("L2a")
    proj = {n: w[n].rearrange("p (k n) -> p k n", k=KD) for n in "qkv"}
    wo = w["o"].rearrange("p (m n) -> p m n", m=16)
    KINDS = ["k", "v", "q0", "q1", "q2", "q3"]
    NK = len(KINDS)
    NP, NU = 2 * NK, 8
    ROPES = [n for n in range(NP) if KINDS[n % NK] != "v"]
    NR = len(ROPES)
    LAG_X = 3
    SLOT = [6, 7, 9, 10, 12, 13, 14, 15, 16, 17, 18, 19]
    LAG_T, LAG_O, LAG_Y = 2, 3, 4
    STEPS = 20
    with ExitStack() as ctx:
        sem = lambda n: core.sem(f"L2a_{n}", ctx)
        carve = core.work("L2a")
        s = norm_state(core, "L2a", carve, ctx)
        xcur = s["xn"].rearrange("p a d -> p (a d)").rearrange("p (k t) -> p k t", k=KD)[:, :, 0:2 * P]
        xcur = carve(KD, 2 * P)
        raw, cos_part, sin_part, turned_in = (carve(2, 512) for _ in range(4))
        qT, kT, v = carve(2, 16, P), carve(2, 4, P), carve(2, 512)
        sm, pT, oT = carve(2, 2, 512), carve(2, 512), carve(2, 512)
        peak, sinks, sink_part, total = carve(2, 8), carve(32), carve(2, 8), carve(2, 8)
        minus_one = carve(8)
        p_bank, x_bank, s_bank, t_bank, o_bank, y_bank = (
            core.bank[0], core.bank[1], core.bank[2:4], core.bank[4:6], core.bank[6], core.bank[7])

        staged, staged_used, sinks_done = sem("staged"), sem("staged_used"), sem("sinks_done")
        piece_made, piece_done, parts_done, roped = sem("piece_made"), sem("piece_done"), sem("parts_done"), sem("roped")
        rope_turned, rope_done = sem("rope_turned"), sem("rope_done")
        scores_made, peaks, peak_done, moved = sem("scores_made"), sem("peaks"), sem("peak_done"), sem("moved")
        exp_done, summed, total_done, total_inv, p_done = (
            sem("exp_done"), sem("summed"), sem("total_done"), sem("total_inv"), sem("p_done"))
        p_turned, pT_done, o_made, oT_done, y_made, y_read, y_added = (
            sem("p_turned"), sem("pT_done"), sem("o_made"), sem("oT_done"), sem("y_made"), sem("y_read"), sem("y_added"))
        block = ctx.enter_context(core.block())
        n_vector, n_gpsimd, n_tensor, n_scalar = normalise(core, "L2a", block, s)
        fours = lambda a: a.rearrange("p (m d) -> p m d", m=4)

        @block.sync
        def _(sp):
            for what in LOADS["L2a"]:
                core.load(sp, what)

        @block.gpsimd
        def _(pool):
            nc.gpsimd.memset(minus_one, -1.0)
            n_gpsimd(pool)
            with pool.Fori(0, B // 2) as t:
                pool.wait_ge(staged_used, at(t, 1, 1))
                core.held(pool)
                pool.wait_ge(s["xnT_done"], B // 2)
                nc.gpsimd.tensor_copy(xcur.rearrange("p k (b t) -> p k b t", b=2),
                                      core.xnT[:, :, bass.ds(t * 2, 2), :]).then_inc(staged, 1)
                for step in range(STEPS):
                    if step in ROPES:
                        r = ROPES.index(step)
                        pool.wait_ge(parts_done, at(t, NR, r + 1))
                        if r >= 2:
                            pool.wait_ge(rope_turned, at(t, NR, r - 1))
                        nc.gpsimd.tensor_tensor(turned_in[:, r % 2, :], cos_part[:, r % 2, :], sin_part[:, r % 2, :],
                                                ALU.add).then_inc(roped, 1)
                    if step in SLOT[:NU]:
                        u = SLOT.index(step)
                        pool.wait_ge(total_done, at(t, NU, u + 1))
                        nc.gpsimd.tensor_tensor(total[:, u % 2, :], total[:, u % 2, :], minus_one, ALU.pow).then_inc(total_inv, 1)
                        pool.wait_ge(total_inv, at(t, NU, u + 1))
                        p8 = sm[:, u % 2, :, :].rearrange("p e (m d) -> p (e m) d", m=4)
                        nc.gpsimd.tensor_tensor(p8, p8, total[:, u % 2, :].unsqueeze(2).to_broadcast([P, 8, P]),
                                                ALU.mult).then_inc(p_done, 1)

        @block.tensor
        def _(pe):
            n_tensor(pe)
            pe.wait_ge(s["xnT_done"], B // 2)
            pe.sem_inc(staged_used, 1)
            pe.wait_ge(core.weights_loaded["L2a"], 16)
            with pe.Fori(0, B // 2) as t:
                pe.wait_ge(staged, at(t, 1, 1))
                for step in range(STEPS):
                    if step < NP:
                        n, i, kind = step, step // NK, KINDS[step % NK]
                        rhs = proj["q"][:, :, 512 * int(kind[1]):512 * int(kind[1]) + 512] if kind[0] == "q" else proj[kind]
                        if n:
                            pe.wait_ge(piece_done, at(t, NP, n))
                        for k in range(KD):
                            last = nc.tensor.matmul(p_bank[:, :], xcur[:, k, i * P:(i + 1) * P], rhs[:, k, :],
                                                    start=(k == 0), stop=(k == KD - 1))
                        last.then_inc(piece_made, 1)
                        if n == NP - 1:
                            pe.wait_ge(piece_made, at(t, NP, NP))
                            pe.sem_inc(staged_used, 1)
                    if step - LAG_X in ROPES:
                        r = ROPES.index(step - LAG_X)
                        pe.wait_ge(roped, at(t, NR, r + 1))
                        if r:
                            pe.wait_ge(rope_done, at(t, NR, r))
                        for h in range(4):
                            last = nc.tensor.transpose(x_bank[:, h * P:(h + 1) * P],
                                                       turned_in[:, r % 2, h * P:(h + 1) * P], core.ident)
                        last.then_inc(rope_turned, 1)
                    if step in SLOT[:NU]:
                        u = SLOT.index(step)
                        i, a = u // 4, u % 4
                        pe.wait_ge(rope_done, at(t, NR, ROPES.index(NK * i + 2 + a) + 1))
                        if u:
                            pe.wait_ge(moved, at(t, NU, u))
                        for m in range(4):
                            for e in range(2):
                                last = nc.tensor.matmul(s_bank[e][:, m * P:(m + 1) * P],
                                                        qT[e * HD:(e + 1) * HD, i, 4 * a + m, :],
                                                        kT[e * HD:(e + 1) * HD, i, a, :], start=True, stop=True)
                        last.then_inc(scores_made, 1)
                    if step in SLOT[LAG_T:LAG_T + NU]:
                        u = SLOT.index(step) - LAG_T
                        pe.wait_ge(p_done, at(t, NU, u + 1))
                        if u:
                            pe.wait_ge(pT_done, at(t, NU, u))
                        for e in range(2):
                            for m in range(4):
                                last = nc.tensor.transpose(t_bank[e][:, m * P:(m + 1) * P],
                                                           sm[:, u % 2, e, m * P:(m + 1) * P], core.ident)
                        last.then_inc(p_turned, 1)
                    if step in SLOT[LAG_O:LAG_O + NU]:
                        u = SLOT.index(step) - LAG_O
                        i, a = u // 4, u % 4
                        pe.wait_ge(pT_done, at(t, NU, u + 1))
                        if u:
                            pe.wait_ge(oT_done, at(t, NU, u))
                        for e in range(2):
                            kv = 2 * a + e
                            last = nc.tensor.matmul(o_bank[e * HD:(e + 1) * HD, :], v[:, i, kv * HD:(kv + 1) * HD],
                                                    pT[:, e, :], start=True, stop=True)
                        last.then_inc(o_made, 1)
                    if step in SLOT[LAG_Y:]:
                        u = SLOT.index(step) - LAG_Y
                        i, a = u // 4, u % 4
                        pe.wait_ge(oT_done, at(t, NU, u + 1))
                        if a == 0:
                            pe.wait_ge(y_read, at(t, 2, i + 1))
                        for m in range(4):
                            last = nc.tensor.matmul(y_bank[:, 0:D], oT[:, u % 2, m * P:(m + 1) * P], wo[:, 4 * a + m, :],
                                                    start=(a == 0 and m == 0), stop=(a == 3 and m == 3))
                        if a == 3:
                            last.then_inc(y_made, 1)

        @block.scalar
        def _(act):
            n_scalar(act)
            with act.Fori(0, B // 2) as t:
                for step in range(STEPS):
                    if step in SLOT[LAG_T:LAG_T + NU]:
                        u = SLOT.index(step) - LAG_T
                        act.wait_ge(p_turned, at(t, NU, u + 1))
                        if u:
                            act.wait_ge(o_made, at(t, NU, u))
                        for e in range(2):
                            last = nc.scalar.copy(pT[:, e, :], t_bank[e][:, :])
                        last.then_inc(pT_done, 1)
                    if step - LAG_X in ROPES:
                        n = step - LAG_X
                        r, i, kind = ROPES.index(n), n // NK, KINDS[n % NK]
                        act.wait_ge(rope_turned, at(t, NR, r + 1))
                        out = qT[:, i, 4 * int(kind[1]):4 * int(kind[1]) + 4, :] if kind[0] == "q" else kT[:, i, :, :]
                        nc.scalar.copy(out, fours(x_bank[:, :])).then_inc(rope_done, 1)
                    if step in SLOT[:NU]:
                        u = SLOT.index(step)
                        act.wait_ge(moved, at(t, NU, u + 1))
                        nc.scalar.activation(sink_part[:, u % 2, :], sink_part[:, u % 2, :], ACT.Exp, scale=0.125)
                        nc.scalar.activation(sm[:, u % 2, :, :], sm[:, u % 2, :, :], ACT.Exp, scale=0.125).then_inc(exp_done, 1)
                    if step in SLOT[LAG_O:LAG_O + NU]:
                        u = SLOT.index(step) - LAG_O
                        act.wait_ge(o_made, at(t, NU, u + 1))
                        nc.scalar.copy(oT[:, u % 2, :], o_bank[:, :]).then_inc(oT_done, 1)

        @block.vector
        def _(dve):
            n_vector(dve)
            dve.wait_ge(core.weights_loaded["L2a"], 16)
            nc.vector.tensor_scalar(sinks, w["sinks"], 8.0, None, ALU.mult).then_inc(sinks_done, 1)
            dve.wait_ge(sinks_done, 1)
            dve.sem_inc(y_read, 1)
            eights = lambda a: a.rearrange("p (h d) -> p h d", h=8)
            with dve.Fori(0, B // 2) as t:

                def add_to_x(i):
                    dve.wait_ge(y_made, at(t, 2, i + 1))
                    xb = core.x[:, bass.ds(2 * t + i, 1), :].squeeze(1)
                    nc.vector.tensor_tensor(xb, y_bank[:, 0:D], xb, ALU.add).then_inc(y_read, 1)
                    dve.wait_ge(y_read, at(t, 2, i + 2))
                    nc.vector.tensor_tensor(xb, xb, w["bo"], ALU.add).then_inc(y_added, 1)

                for step in range(STEPS):
                    if step < NP:
                        n, i, kind = step, step // NK, KINDS[step % NK]
                        dve.wait_ge(piece_made, at(t, NP, n + 1))
                        if kind == "v":
                            nc.vector.tensor_tensor(v[:, i, :], p_bank[:, :], w["bv"], ALU.add).then_inc(piece_done, 1)
                        else:
                            r = ROPES.index(n)
                            bias = w["bk"] if kind == "k" else w["bq"][:, 512 * int(kind[1]):512 * int(kind[1]) + 512]
                            nc.vector.tensor_tensor(raw[:, r % 2, :], p_bank[:, :], bias, ALU.add).then_inc(piece_done, 1)
                            dve.wait_ge(piece_done, at(t, NP, n + 1))
                            if r >= 2:
                                dve.wait_ge(roped, at(t, NR, r - 1))
                            cos = core.constant("cos2").unsqueeze(1)
                            sin = core.constant("sin2").unsqueeze(1)
                            halves = raw[:, r % 2, :].rearrange("p (a d) -> p a d", a=16)
                            nc.vector.tensor_tensor(cos_part[:, r % 2, :].rearrange("p (a d) -> p a d", a=16), halves,
                                                    cos.to_broadcast([P, 16, 32]), ALU.mult)
                            out, src = eights(sin_part[:, r % 2, :]), eights(raw[:, r % 2, :])
                            nc.vector.scalar_tensor_tensor(out=out[:, :, 0:32], in0=src[:, :, 32:64], scalar=-1.0,
                                                           in1=sin.to_broadcast([P, 8, 32]), op0=ALU.mult, op1=ALU.mult)
                            nc.vector.tensor_tensor(out[:, :, 32:64], src[:, :, 0:32], sin.to_broadcast([P, 8, 32]),
                                                    ALU.mult).then_inc(parts_done, 1)
                    if step in SLOT[:NU]:
                        u = SLOT.index(step)
                        a = u % 4
                        dve.wait_ge(scores_made, at(t, NU, u + 1))
                        for e in range(2):
                            last = nc.vector.tensor_reduce(peak[:, u % 2, 4 * e:4 * e + 4], fours(s_bank[e][:, :]), AX, ALU.max)
                        last.then_inc(peaks, 1)
                        dve.wait_ge(peaks, at(t, NU, u + 1))
                        sink = sinks[:, 8 * a:8 * a + 8]
                        nc.vector.tensor_tensor(peak[:, u % 2, :], peak[:, u % 2, :], sink, ALU.max).then_inc(peak_done, 1)
                        dve.wait_ge(peak_done, at(t, NU, u + 1))
                        if u >= 2:
                            dve.wait_ge(p_turned, at(t, NU, u - 1))
                        nc.vector.tensor_tensor(sink_part[:, u % 2, :], sink, peak[:, u % 2, :], ALU.subtract)
                        for e in range(2):
                            last = nc.vector.tensor_tensor(fours(sm[:, u % 2, e, :]), fours(s_bank[e][:, :]),
                                                           peak[:, u % 2, 4 * e:4 * e + 4].unsqueeze(2).to_broadcast([P, 4, P]),
                                                           ALU.subtract)
                        last.then_inc(moved, 1)
                        dve.wait_ge(exp_done, at(t, NU, u + 1))
                        nc.vector.tensor_reduce(total[:, u % 2, :], sm[:, u % 2, :, :].rearrange("p e (m d) -> p (e m) d", m=4),
                                                AX, ALU.add).then_inc(summed, 1)
                        dve.wait_ge(summed, at(t, NU, u + 1))
                        nc.vector.tensor_tensor(total[:, u % 2, :], total[:, u % 2, :], sink_part[:, u % 2, :],
                                                ALU.add).then_inc(total_done, 1)
                    if step == SLOT[3 + LAG_Y]:
                        add_to_x(0)
                add_to_x(1)


def lora_experts(core):
    nc, CH, R = core.nc, 6, 72
    w = core.weights("L1f")
    wg, wu = (w[n].rearrange("p (k f) -> p k f", k=KD) for n in ("gate", "up"))
    ag, au = (w[n].rearrange("p (k f) -> p k f", k=KD) for n in ("a_gate", "a_up"))
    wd = w["down"].rearrange("p (c d) -> p c d", c=CH)
    ad = w["a_down"].rearrange("p (c r) -> p c r", c=CH)
    with ExitStack() as ctx:
        sem = lambda n: core.sem(f"L1f_{n}", ctx)
        carve = core.work("L1f")
        s = norm_state(core, "L1f", carve, ctx)
        scratch = carve(2 * B * 64)
        shareT, shareT_done, (r_vector, r_tensor, r_scalar) = router(
            core, "L1f", 8, 2, "sigmoid", s, w["router"], carve, scratch, ctx, bias=w["bias"], scale=0.125,
            floor=1e-8, ones=1)
        factor, low_gate, low_up, low_down = carve(N), carve(N), carve(N), carve(N)
        silu, h = carve(2, N), carve(CH, N)
        g_bank, u_bank, a_bank, b_bank, y_bank = core.bank[0:2], core.bank[2:4], core.bank[4], core.bank[5], core.bank[6:8]
        low_made, factor_made, down_made = sem("low_made"), sem("factor_made"), sem("down_made")
        factor_done, low_done, low_down_done = sem("factor_done"), sem("low_done"), sem("low_down_done")
        g_made, u_made, silu_done, h_done = sem("g_made"), sem("u_made"), sem("silu_done"), sem("h_done")
        y_made, y_added = sem("y_made"), sem("y_added")
        block = ctx.enter_context(core.block())
        n_vector, n_gpsimd, n_tensor, n_scalar = normalise(core, "L1f", block, s)

        @block.sync
        def _(sp):
            for what in LOADS["L1f"]:
                core.load(sp, what)

        @block.gpsimd
        def _(pool):
            n_gpsimd(pool)

        @block.tensor
        def _(pe):
            n_tensor(pe)
            r_tensor(pe)
            pe.wait_ge(shareT_done, B // 4)
            with pe.Fori(0, GROUPS) as t:
                xg = core.xnT[:, :, bass.ds(t * G, G), :]
                pe.wait_ge(y_added, at(t, 1, 1))
                nc.tensor.matmul(g_bank[1][0:R, :], w["select"][0:9, :], shareT[0:9, bass.ds(t * N, N)],
                                 start=True, stop=True).then_inc(factor_made, 1)
                for wa, bank in ((ag, a_bank), (au, b_bank)):
                    for k in range(KD):
                        last = nc.tensor.matmul(bank[0:R, :], wa[:, k, :], core.xnT[:, k, bass.ds(t * G, G), :],
                                                start=(k == 0), stop=(k == KD - 1))
                last.then_inc(low_made, 1)
                for step in range(CH + 1):
                    if step < CH:
                        c = step
                        if c == 1:
                            pe.wait_ge(factor_done, at(t, 1, 1))
                        if c >= 2:
                            pe.wait_ge(h_done, at(t, CH, c - 1))
                        for wt, bank in ((wg, g_bank), (wu, u_bank)):
                            for k in range(KD):
                                nc.tensor.matmul(bank[c % 2][:, :], wt[:, k, c * P:(c + 1) * P],
                                                 core.xnT[:, k, bass.ds(t * G, G), :], start=(k == 0), stop=False)
                        pe.wait_ge(low_done, at(t, 1, 1))
                        nc.tensor.matmul(g_bank[c % 2][:, :], w["b_gate"][0:R, c * P:(c + 1) * P], low_gate[0:R, :],
                                         start=False, stop=True).then_inc(g_made, 1)
                        nc.tensor.matmul(u_bank[c % 2][:, :], w["b_up"][0:R, c * P:(c + 1) * P], low_up[0:R, :],
                                         start=False, stop=True).then_inc(u_made, 1)
                    if step >= 1:
                        c = step - 1
                        pe.wait_ge(h_done, at(t, CH, c + 1))
                        last = nc.tensor.matmul(a_bank[0:R, :], ad[:, c, :], h[:, c, :], start=(c == 0), stop=(c == CH - 1))
                        if c == CH - 1:
                            last.then_inc(down_made, 1)
                        for j in range(G):
                            nc.tensor.matmul(y_bank[j // 2][:, (j % 2) * D:(j % 2 + 1) * D], h[:, c, j * P:(j + 1) * P],
                                             wd[:, c, :], start=(c == 0 and j % 2 == 0), stop=False, skip_group_check=True)
                pe.wait_ge(low_down_done, at(t, 1, 1))
                for j in range(G):
                    last = nc.tensor.matmul(y_bank[j // 2][:, (j % 2) * D:(j % 2 + 1) * D], low_down[0:R, j * P:(j + 1) * P],
                                            w["b_down"][0:R, :], start=False, stop=True, skip_group_check=True)
                last.then_inc(y_made, 1)

        @block.scalar
        def _(act):
            n_scalar(act)
            r_scalar(act)
            act.wait_ge(shareT_done, B // 4)
            with act.Fori(0, GROUPS) as t:
                act.wait_ge(factor_made, at(t, 1, 1))
                nc.scalar.copy(factor[0:R, :], g_bank[1][0:R, :]).then_inc(factor_done, 1)
                for c in range(CH):
                    act.wait_ge(g_made, at(t, CH, c + 1))
                    nc.scalar.activation(silu[:, c % 2, :], g_bank[c % 2][:, :], ACT.Silu).then_inc(silu_done, 1)

        @block.vector
        def _(dve):
            n_vector(dve)
            r_vector(dve)
            dve.sem_inc(y_added, 1)
            with dve.Fori(0, GROUPS) as t:
                dve.wait_ge(factor_done, at(t, 1, 1))
                dve.wait_ge(low_made, at(t, 1, 1))
                nc.vector.tensor_tensor(low_gate[0:R, :], a_bank[0:R, :], factor[0:R, :], ALU.mult)
                nc.vector.tensor_tensor(low_up[0:R, :], b_bank[0:R, :], factor[0:R, :], ALU.mult).then_inc(low_done, 1)
                for c in range(CH):
                    dve.wait_ge(silu_done, at(t, CH, c + 1))
                    dve.wait_ge(u_made, at(t, CH, c + 1))
                    nc.vector.tensor_tensor(h[:, c, :], u_bank[c % 2][:, :], silu[:, c % 2, :], ALU.mult).then_inc(h_done, 1)
                dve.wait_ge(down_made, at(t, 1, 1))
                nc.vector.tensor_tensor(low_down[0:R, :], a_bank[0:R, :], factor[0:R, :], ALU.mult).then_inc(low_down_done, 1)
                dve.wait_ge(y_made, at(t, 1, 1))
                for j in range(G):
                    xj = core.x[:, bass.ds(t * G + j, 1), :].squeeze(1)
                    last = nc.vector.tensor_tensor(xj, y_bank[j // 2][:, (j % 2) * D:(j % 2 + 1) * D], xj, ALU.add)
                last.then_inc(y_added, 1)



def token_attention(core, name):
    nc = core.nc
    own = name == "L3a"
    SCALE = 1.0 / float(np.sqrt(32)) if own else 1.0 / 16
    w = core.weights(name)
    with ExitStack() as ctx:
        sem = lambda n: core.sem(f"{name}_{n}", ctx)
        carve = core.work(name)
        s = norm_state(core, name, carve, ctx)
        xcur = carve(2, KD, N) if not own else carve(2, KD, N)
        sm, pT = carve(2, N), carve(2, N)
        peak, total = carve(2, G), carve(2, G)
        s_bank, v_bank, t_bank, y_bank = core.bank[0:2], core.bank[2:4], core.bank[4:6], core.bank[6:8]
        if own:
            state, action, values = carve(2, N), carve(2, N), carve(2, G * D)
        else:
            mask = carve(B * P // 4)
            keep, fill, valid = carve(B, P), carve(B, P), carve(B)
        mask_loaded, keep_done, staged, staged_used = sem("mask_loaded"), sem("keep_done"), sem("staged"), sem("staged_used")
        sa_made, sa_done, v_made, v_done = sem("sa_made"), sem("sa_done"), sem("v_made"), sem("v_done")
        scores_made, masked, filled, peak_done, moved, exp_done = (
            sem("scores_made"), sem("masked"), sem("filled"), sem("peak_done"), sem("moved"), sem("exp_done"))
        total_step, p_done, p_turned, pT_done, y_made, y_added, b_added = (
            sem("total_step"), sem("p_done"), sem("p_turned"), sem("pT_done"), sem("y_made"), sem("y_added"), sem("b_added"))
        block = ctx.enter_context(core.block())
        n_vector, n_gpsimd, n_tensor, n_scalar = normalise(core, name, block, s)
        quads = lambda a: a.rearrange("p (j d) -> p j d", j=G)
        TURNS = GROUPS // 2

        @block.sync
        def _(sp):
            if not own:
                sp.dma_start(mask.bitcast(U8), core.dram["memory_mask"].to_broadcast([P, B * P])).then_inc(mask_loaded, 16)
            for what in LOADS[name]:
                core.load(sp, what)

        @block.gpsimd
        def _(pool):
            n_gpsimd(pool)
            with pool.Fori(0, TURNS) as t:
                for g in range(2):
                    pool.wait_ge(staged_used, at(t, 2, g + 1))
                    core.held(pool)
                    pool.wait_ge(s["xnT_done"], B // 2)
                    nc.gpsimd.tensor_copy(xcur[:, g, :, :].rearrange("p k (b t) -> p k b t", b=G),
                                          core.xnT[:, :, bass.ds(t * 2 * G + g * G, G), :]).then_inc(staged, 1)

        @block.tensor
        def _(pe):
            n_tensor(pe)
            pe.sem_inc(staged_used, 2)
            if own:
                pe.wait_ge(core.weights_loaded[name], 16)
            with pe.Fori(0, TURNS) as t:
                for g in range(2):
                    pe.wait_ge(staged, at(t, 2, g + 1))
                    pe.wait_ge(y_added, at(t, 2, g + 1))
                    if own:
                        for wn, bank in (("s", t_bank[g]), ("a", y_bank[g])):
                            for k in range(KD):
                                last = nc.tensor.matmul(bank[0:32, :], w[wn][:, k * 32:(k + 1) * 32], xcur[:, g, k, :],
                                                        start=(k == 0), stop=(k == KD - 1))
                        last.then_inc(sa_made, 1)
                for g in range(2):
                    if own:
                        for j in range(G):
                            if j == 2 or (j == 0 and g):
                                pe.wait_ge(v_done, at(t, 4, 2 * g + j // 2))
                            for k in range(KD):
                                last = nc.tensor.matmul(v_bank[j // 2][:, (j % 2) * D:(j % 2 + 1) * D],
                                                        xcur[:, g, k, j * P:(j + 1) * P], w["o"][:, k * D:(k + 1) * D],
                                                        start=(k == 0), stop=(k == KD - 1))
                            if j % 2:
                                last.then_inc(v_made, 1)
                        pe.wait_ge(sa_done, at(t, 2, g + 1))
                    for j in range(G):
                        if own:
                            last = nc.tensor.matmul(s_bank[g][:, j * P:(j + 1) * P], state[0:32, g, j * P:(j + 1) * P],
                                                    action[0:32, g, j * P:(j + 1) * P], start=True, stop=True)
                        else:
                            for k in range(KD):
                                last = nc.tensor.matmul(s_bank[g][:, j * P:(j + 1) * P], xcur[:, g, k, j * P:(j + 1) * P],
                                                        core.ctxT[:, k, bass.ds(t * 2 * G + g * G + j, 1), :].squeeze(1),
                                                        start=(k == 0), stop=(k == KD - 1))
                    last.then_inc(scores_made, 1)
                    pe.wait_ge(scores_made, at(t, 2, g + 1))
                    pe.sem_inc(staged_used, 1)
                for g in range(2):
                    pe.wait_ge(p_done, at(t, 2, g + 1))
                    for j in range(G):
                        last = nc.tensor.transpose(t_bank[g][:, j * P:(j + 1) * P], sm[:, g, j * P:(j + 1) * P], core.ident)
                    last.then_inc(p_turned, 1)
                for g in range(2):
                    pe.wait_ge(pT_done, at(t, 2, g + 1))
                    if own:
                        pe.wait_ge(v_done, at(t, 4, 2 * g + 2))
                    for half in range(2):
                        bank = (y_bank[g], s_bank[g])[half]
                        for jj in range(2):
                            j = 2 * half + jj
                            rhs = (values[:, g, j * D:(j + 1) * D] if own else
                                   core.ctx_sb[:, bass.ds(t * 2 * G + g * G + j, 1), :].squeeze(1))
                            last = nc.tensor.matmul(bank[:, jj * D:(jj + 1) * D], pT[:, g, j * P:(j + 1) * P], rhs,
                                                    start=True, stop=True)
                    last.then_inc(y_made, 1)

        @block.scalar
        def _(act):
            n_scalar(act)
            with act.Fori(0, TURNS) as t:
                if own:
                    for g in range(2):
                        act.wait_ge(sa_made, at(t, 2, g + 1))
                        nc.scalar.copy(state[0:32, g, :], t_bank[g][0:32, :])
                        nc.scalar.copy(action[0:32, g, :], y_bank[g][0:32, :]).then_inc(sa_done, 1)
                    for g in range(2):
                        for half in range(2):
                            act.wait_ge(v_made, at(t, 4, 2 * g + half + 1))
                            nc.scalar.copy(values[:, g, half * 2 * D:(half + 1) * 2 * D], v_bank[half][:, :]).then_inc(v_done, 1)
                for g in range(2):
                    act.wait_ge(moved, at(t, 2, g + 1))
                    nc.scalar.activation(sm[:, g, :], sm[:, g, :], ACT.Exp, scale=SCALE).then_inc(exp_done, 1)
                for g in range(2):
                    act.wait_ge(p_turned, at(t, 2, g + 1))
                    nc.scalar.copy(pT[:, g, :], t_bank[g][:, :]).then_inc(pT_done, 1)

        @block.vector
        def _(dve):
            n_vector(dve)
            if own:
                dve.wait_ge(core.weights_loaded[name], 16)
                bias = core.constant("causal_bias").unsqueeze(1).to_broadcast([P, G, P])
            else:
                dve.wait_ge(mask_loaded, 16)
                m8 = mask.bitcast(U8).rearrange("p (b t) -> p b t", b=B)
                nc.vector.tensor_scalar(keep, m8, 0.0, None, ALU.not_equal).then_inc(keep_done, 1)
                nc.vector.tensor_scalar(fill, m8, 0.0, -1e30 / SCALE, ALU.is_equal, ALU.mult).then_inc(keep_done, 1)
                dve.wait_ge(keep_done, 2)
                nc.vector.tensor_reduce(valid, keep, AX, ALU.max).then_inc(keep_done, 1)
                dve.wait_ge(keep_done, 3)
            dve.sem_inc(y_added, 2)
            with dve.Fori(0, TURNS) as t:
                for g in range(2):
                    group = bass.ds(t * 2 * G + g * G, G)
                    dve.wait_ge(scores_made, at(t, 2, g + 1))
                    if own:
                        nc.vector.tensor_tensor(quads(sm[:, g, :]), quads(s_bank[g][:, :]), bias, ALU.add).then_inc(filled, 1)
                    else:
                        nc.vector.tensor_tensor(quads(sm[:, g, :]), quads(s_bank[g][:, :]), keep[:, group, :], ALU.mult).then_inc(masked, 1)
                        dve.wait_ge(masked, at(t, 2, g + 1))
                        nc.vector.tensor_tensor(quads(sm[:, g, :]), quads(sm[:, g, :]), fill[:, group, :], ALU.add).then_inc(filled, 1)
                    dve.wait_ge(filled, at(t, 2, g + 1))
                    nc.vector.tensor_reduce(peak[:, g, :], quads(sm[:, g, :]), AX, ALU.max).then_inc(peak_done, 1)
                    dve.wait_ge(peak_done, at(t, 2, g + 1))
                    nc.vector.tensor_tensor(quads(sm[:, g, :]), quads(sm[:, g, :]),
                                            peak[:, g, :].unsqueeze(2).to_broadcast([P, G, P]), ALU.subtract).then_inc(moved, 1)
                for g in range(2):
                    group = bass.ds(t * 2 * G + g * G, G)
                    dve.wait_ge(exp_done, at(t, 2, g + 1))
                    nc.vector.tensor_reduce(total[:, g, :], quads(sm[:, g, :]), AX, ALU.add).then_inc(total_step, 1)
                    steps = 2 if own else 3
                    dve.wait_ge(total_step, at(t, 2 * steps, steps * g + 1))
                    nc.vector.reciprocal(total[:, g, :], total[:, g, :]).then_inc(total_step, 1)
                    dve.wait_ge(total_step, at(t, 2 * steps, steps * g + 2))
                    if not own:
                        nc.vector.tensor_tensor(total[:, g, :], total[:, g, :], valid[:, group], ALU.mult).then_inc(total_step, 1)
                        dve.wait_ge(total_step, at(t, 2 * steps, steps * g + 3))
                    nc.vector.tensor_tensor(quads(sm[:, g, :]), quads(sm[:, g, :]),
                                            total[:, g, :].unsqueeze(2).to_broadcast([P, G, P]), ALU.mult).then_inc(p_done, 1)
                for g in range(2):
                    group = bass.ds(t * 2 * G + g * G, G)
                    dve.wait_ge(y_made, at(t, 2, g + 1))
                    for half in range(2):
                        pair = core.x[:, bass.ds(t * 2 * G + g * G + 2 * half, 2), :]
                        bank = (y_bank[g], s_bank[g])[half]
                        last = nc.vector.tensor_tensor(pair, bank[:, :].rearrange("p (j d) -> p j d", j=2), pair, ALU.add)
                    if own:
                        last.then_inc(b_added, 1)
                        dve.wait_ge(b_added, at(t, 2, g + 1))
                        xg = core.x[:, group, :]
                        last = nc.vector.tensor_tensor(xg, xg, w["bo"].unsqueeze(1).to_broadcast([P, G, D]), ALU.add)
                    last.then_inc(y_added, 1)


def context_attention(core):
    token_attention(core, "L2x")


def state_action_attention(core):
    token_attention(core, "L3a")


def column_cross_attention(core):
    nc = core.nc
    SCALE = 1.0 / 16
    T = 8
    with ExitStack() as ctx:
        sem = lambda n: core.sem(f"L3x_{n}", ctx)
        carve = core.work("L3x")
        s = norm_state(core, "L3x", carve, ctx, turn_to_features=False)
        xn = core.xnT.rearrange("p k b t -> p (k b t)").rearrange("p (b d) -> p b d", b=B)
        tokens = carve(T, D)
        features = carve(KD, T * P)
        sm = carve(2, 2 * D)
        peak, total = carve(2, 2), carve(2, 2)
        s_bank, y_bank = core.bank[0:2], core.bank[2:4]
        staged, staged_used, scores_made, peak_done, moved, exp_done = (
            sem("staged"), sem("staged_used"), sem("scores_made"), sem("peak_done"), sem("moved"), sem("exp_done"))
        summed, inverted, p_done, y_made, y_added = sem("summed"), sem("inverted"), sem("p_done"), sem("y_made"), sem("y_added")
        block = ctx.enter_context(core.block())
        n_vector, n_gpsimd, _, _ = normalise(core, "L3x", block, s, tokens=xn)
        halves = lambda a: a.rearrange("p (h d) -> p h d", h=2)

        @block.sync
        def _(sp):
            for what in LOADS["L3x"]:
                core.load(sp, what)

        @block.gpsimd
        def _(pool):
            n_gpsimd(pool)
            with pool.Fori(0, B // T) as t:
                pool.wait_ge(staged_used, at(t, 1, 1))
                core.held(pool)
                pool.wait_ge(s["xn_done"], B)
                nc.gpsimd.tensor_copy(tokens, core.ctx_sb[:, bass.ds(t * T, T), :])
                nc.gpsimd.tensor_copy(features.rearrange("p k (b t) -> p k b t", b=T),
                                      core.ctxT[:, :, bass.ds(t * T, T), :]).then_inc(staged, 1)

        @block.tensor
        def _(pe):
            pe.sem_inc(staged_used, 1)
            with pe.Fori(0, B // T) as t:
                pe.wait_ge(staged, at(t, 1, 1))
                for step in range(T + 2):
                    if step < T:
                        if step >= 2:
                            pe.wait_ge(moved, at(t, T, step - 1))
                        for half in range(2):
                            last = nc.tensor.matmul(s_bank[step % 2][:, half * D:(half + 1) * D],
                                                    tokens[:, step, half * P:(half + 1) * P],
                                                    xn[:, bass.ds(t * T + step, 1), :].squeeze(1), start=True, stop=True)
                        last.then_inc(scores_made, 1)
                    if step >= 2:
                        b = step - 2
                        pe.wait_ge(p_done, at(t, T, b + 1))
                        pe.wait_ge(y_added, at(t, T, b + 1))
                        for half in range(2):
                            last = nc.tensor.matmul(y_bank[b % 2][:, 0:D], features[:, half, b * P:(b + 1) * P],
                                                    sm[:, b % 2, half * D:(half + 1) * D], start=(half == 0), stop=(half == 1))
                        last.then_inc(y_made, 1)
                pe.wait_ge(y_made, at(t, T, T))
                pe.sem_inc(staged_used, 1)

        @block.scalar
        def _(act):
            with act.Fori(0, B // T) as t:
                for b in range(T):
                    act.wait_ge(moved, at(t, T, b + 1))
                    nc.scalar.activation(sm[:, b % 2, :], sm[:, b % 2, :], ACT.Exp, scale=SCALE).then_inc(exp_done, 1)

        @block.vector
        def _(dve):
            n_vector(dve)
            dve.sem_inc(y_added, 2)
            with dve.Fori(0, B // T) as t:
                for step in range(T + 2):
                    if step < T:
                        b = step
                        dve.wait_ge(scores_made, at(t, T, b + 1))
                        nc.vector.tensor_reduce(peak[:, b % 2, :], halves(s_bank[b % 2][:, :]), AX, ALU.max).then_inc(peak_done, 1)
                        dve.wait_ge(peak_done, at(t, T, b + 1))
                        if b >= 2:
                            dve.wait_ge(y_made, at(t, T, b - 1))
                        nc.vector.tensor_tensor(halves(sm[:, b % 2, :]), halves(s_bank[b % 2][:, :]),
                                                peak[:, b % 2, :].unsqueeze(2).to_broadcast([P, 2, D]), ALU.subtract).then_inc(moved, 1)
                    if 1 <= step <= T:
                        b = step - 1
                        dve.wait_ge(exp_done, at(t, T, b + 1))
                        nc.vector.tensor_reduce(total[:, b % 2, :], halves(sm[:, b % 2, :]), AX, ALU.add).then_inc(summed, 1)
                        dve.wait_ge(summed, at(t, T, b + 1))
                        nc.vector.reciprocal(total[:, b % 2, :], total[:, b % 2, :]).then_inc(inverted, 1)
                        dve.wait_ge(inverted, at(t, T, b + 1))
                        nc.vector.tensor_tensor(halves(sm[:, b % 2, :]), halves(sm[:, b % 2, :]),
                                                total[:, b % 2, :].unsqueeze(2).to_broadcast([P, 2, D]), ALU.mult).then_inc(p_done, 1)
                        dve.wait_ge(y_made, at(t, T, b + 1))
                        xb = core.x[:, bass.ds(t * T + b, 1), :].squeeze(1)
                        nc.vector.tensor_tensor(xb, y_bank[b % 2][:, 0:D], xb, ALU.add).then_inc(y_added, 1)


def start(core):
    nc = core.nc
    with nc.Block() as block:
        @block.sync
        def _(sp):
            sp.dma_start(core.x.rearrange("p b d -> p (b d)"), core.dram["x"]).then_inc(core.x_loaded, 16)
            sp.dma_start(core.const[:, :], core.dram["const"]).then_inc(core.const_loaded, 16)
            for name in FIRST_LOADS:
                core.load(sp, name)
            sp.dma_start(core.ctx_sb.rearrange("p b d -> p (b d)"), core.dram["ctx"]).then_inc(core.ctx_loaded, 16)


def finish(core, out):
    nc = core.nc
    with ExitStack() as ctx:
        stored = core.sem("stored", ctx)
        block = ctx.enter_context(nc.Block())

        @block.sync
        def _(sp):
            sp.dma_start(out, core.x.rearrange("p b d -> p (b d)")).then_inc(stored, 16)
            sp.wait_ge(stored, 16)


FIRST_LOADS = ["L0a", "L0x"]
PHASES = [lightning_attention, channel_cross_attention, experts_0,
          power_attention, rotary_cross_attention, lora_experts,
          sink_attention, context_attention, experts_2,
          state_action_attention, column_cross_attention, experts_3]


CONST_AT = {}
WEIGHT_PARTS = {"L0a": [], "L0x": [], "L0f": [], "L1a": [], "L1x": [], "L1f": [], "L2a": [], "L2f": [],
                "L2x": [], "L3a": [], "L3x": [], "L3f": [], "L3sel": []}


def constants():
    i = np.arange(P)
    s, t = i[:, None], i[None, :]

    def rope(half, base, dim):
        return np.outer(i.astype(np.float32),
                        (1.0 / np.float32(base) ** (np.arange(0, dim, 2, dtype=np.float32) / dim)).astype(np.float32)[:half])

    parts = {
        "ident": np.eye(P), "ones": np.ones((P, P)),
        "causalT": (s <= t) * 1.0,
        "causal_bias": np.where(t > s, -1e30, 0.0),
        "causal_cap": np.where(s <= t, 0.0, -1e30),
        "dist": np.maximum(t - s, 0),
    }
    c, pos = i % 8, np.arange(D, dtype=np.float32)
    theta = (1.0 / np.float32(10000.0) ** (np.arange(0, 4, 2, dtype=np.float32) / 4)).astype(np.float32)
    angle = pos[None, :] * theta[c % 2][:, None]
    parts["cos0"] = np.where(c[:, None] < 4, np.cos(angle), 1.0)
    parts["sin0"] = np.where(c[:, None] < 4, np.sin(angle), 0.0)
    turn = np.zeros((P, P))
    for p in range(P):
        if p % 8 < 2:
            turn[p + 2, p] = -1.0
        elif p % 8 < 4:
            turn[p - 2, p] = 1.0
    parts["turn0"] = turn
    parts["headmask"] = np.stack([(i % 32 // 8 == n) * 1.0 for n in range(4)], 1)
    f1 = rope(64, 10000.0, 128)
    parts["cos1"], parts["sin1"] = np.cos(f1), np.sin(f1)
    f2 = i[:, None].astype(np.float32) * (1.0 / np.float32(150000.0) ** (np.arange(32, dtype=np.float32) * 2.0 / 64)).astype(np.float32)
    parts["cos2"], parts["sin2"] = np.cos(f2), np.sin(f2)
    at_col = 0
    for name, a in parts.items():
        CONST_AT[name] = (at_col, at_col + a.shape[1])
        at_col += a.shape[1]
    return np.ascontiguousarray(np.concatenate([a.astype(np.float32) for a in parts.values()], 1))


def rows(w):
    w = np.asarray(w)
    k = -(-w.shape[0] // P)
    w = np.concatenate([w, np.zeros((k * P - w.shape[0], w.shape[1]), w.dtype)]) if k * P > w.shape[0] else w
    return w.reshape(k, P, -1).transpose(1, 0, 2).reshape(P, -1)


def on_top(w):
    w = np.asarray(w)
    return np.concatenate([w, np.zeros((P - w.shape[0], w.shape[1]), w.dtype)])


def spread(v):
    v = np.asarray(v).reshape(1, -1)
    return np.broadcast_to(v, (P, v.shape[1]))


def selector(groups, width, size):
    return (np.arange(width)[None, :] // size == np.arange(groups)[:, None]).astype(np.float32)


def pack(name, parts):
    at_col, WEIGHT_PARTS[name][:] = 0, []
    for part, a in parts.items():
        WEIGHT_PARTS[name].append((part, at_col, at_col + a.shape[1]))
        at_col += a.shape[1]
    return np.ascontiguousarray(np.concatenate(list(parts.values()), 1))


def arrays_of(i):
    T = np.transpose
    i = {k: np.asarray(v) for k, v in i.items()}
    out = {"const": constants()}
    out["x"] = np.ascontiguousarray(i["x"].transpose(1, 0, 2)).reshape(P, B * D)
    out["ctx"] = np.ascontiguousarray(i["ctx_2048"].transpose(1, 0, 2)).reshape(P, B * D)
    out["attn_mask"] = np.ascontiguousarray(i["mask_1x1x2048x2048_if1"].reshape(2, P, D).transpose(1, 0, 2)).reshape(P, 2 * D)
    out["memory_mask"] = np.ascontiguousarray(i["mask_BxS2_bk0"].reshape(1, B * P))
    out["w_L0a"] = pack("L0a", {
        "qkv": rows(T(i["L0_attn_w_qkv"])), "gate": rows(T(i["L0_attn_w_gate"])), "out": rows(T(i["L0_attn_w_out"])),
        "norm": rows(i["L0_attn_norm_w"].reshape(-1, 1)), "slope": spread(i["L0_attn_slope_rate"])})
    col = lambda v: rows(np.asarray(v).reshape(-1, 1))
    out["w_L0x"] = pack("L0x", {
        "q": T(i["L0_xattn_wq"]), "k": T(i["L0_xattn_wk"]), "v": T(i["L0_xattn_wv"]), "o": T(i["L0_xattn_wo"]),
        "bq": col(i["L0_xattn_bq"]), "bk": col(i["L0_xattn_bk"]), "bo": col(i["L0_xattn_bo"]), "bv": spread(i["L0_xattn_bv"])})
    wide = lambda w, f: np.concatenate([w, np.zeros((w.shape[0], f - w.shape[1]), w.dtype)], 1)
    hidden = lambda e, sh, f: rows(wide(np.concatenate([T(e.reshape(-1, D)), T(sh)], 1), f))
    down = lambda e, sh: rows(np.concatenate([e.transpose(0, 2, 1).reshape(-1, D), T(sh)], 0))
    out["w_L0f"] = pack("L0f", {
        "router": rows(T(i["L0_ffn_gate_w"])),
        "gate": hidden(i["L0_ffn_exp_wg"], i["L0_ffn_shared_wg"], 14 * P),
        "up": hidden(i["L0_ffn_exp_wu"], i["L0_ffn_shared_wu"], 14 * P),
        "down": down(i["L0_ffn_exp_wd"], i["L0_ffn_shared_wd"]), "select": on_top(selector(8, 11 * P, 176))})
    w1, s1 = i["L3_ffn_w1"], i["L3_ffn_shared_w1"]
    out["w_L3f"] = pack("L3f", {
        "router": rows(T(i["L3_ffn_gate_w"])),
        "gate": hidden(w1[:, :176], s1[:352], 25 * P), "up": hidden(w1[:, 176:], s1[352:], 25 * P),
        "down": down(i["L3_ffn_w2"], i["L3_ffn_shared_w2"])})
    out["w_L3sel"] = pack("L3sel", {"select": on_top(selector(16, 22 * P, 176))})
    out["w_L2f"] = pack("L2f", {
        "router": rows(T(i["L2_ffn_Wg"])), "gate": rows(T(i["L2_ffn_A"].reshape(-1, D))),
        "down": rows(i["L2_ffn_Bw"].transpose(0, 2, 1).reshape(-1, D)), "select": on_top(selector(8, 4 * P, 64))})
    out["w_L1a"] = pack("L1a", {
        "q": rows(i["L1_attn_Wq"]), "k": rows(i["L1_attn_Wk"]), "v": rows(i["L1_attn_Wv"]), "g": rows(i["L1_attn_Wg"]),
        "c": rows(i["L1_attn_Wc"]), "bc": spread(i["L1_attn_bc"])})
    out["w_L1x"] = pack("L1x", {
        **{n: rows(i["L1_xattn_" + m]) for n, m in (("q", "wq"), ("k", "wk"), ("v", "wv"), ("kc", "wk_ctx"), ("vc", "wv_ctx"), ("o", "wo"))},
        "qn": spread(i["L1_xattn_q_norm_w"]), "kn": spread(i["L1_xattn_k_norm_w"])})
    def paired(q):
        q = q.reshape(*q.shape[:-2], 4, 2, 4, 64)
        q = np.swapaxes(q, -3, -2)
        return evens_first(q).reshape(*q.shape[:-4], 2048)

    def evens_first(q):
        q = q.reshape(*q.shape[:-1], 32, 2)
        return np.swapaxes(q, -1, -2).reshape(*q.shape[:-2], 64)

    kvs = lambda k: evens_first(k).reshape(*k.shape[:-2], 512)
    o = i["L2_attn_Wo"].reshape(4, 2, 4, 64, D).transpose(0, 2, 1, 3, 4).reshape(2048, D)
    out["w_L2a"] = pack("L2a", {
        "q": rows(paired(i["L2_attn_Wq"])), "k": rows(kvs(i["L2_attn_Wk"])), "v": rows(i["L2_attn_Wv"].reshape(D, 512)),
        "o": rows(o), "bq": spread(paired(i["L2_attn_bq"])), "bk": spread(kvs(i["L2_attn_bk"])),
        "bv": spread(i["L2_attn_bv"]), "bo": spread(i["L2_attn_bo"]), "sinks": spread(i["L2_attn_sinks"])})
    f = 6 * P
    rank = lambda a, sh: np.concatenate([a.transpose(1, 0, 2).reshape(a.shape[1], -1), sh], 1)
    back = lambda b, sh: np.concatenate([b.reshape(-1, b.shape[2]), sh], 0)
    g = {n[7:]: v for n, v in i.items() if n.startswith("L1_ffn_")}
    out["w_L1f"] = pack("L1f", {
        "router": rows(g["W_router"]), "bias": spread(g["expert_bias"]),
        "gate": rows(wide(g["W_gate"], f)), "up": rows(wide(g["W_up"], f)), "down": rows(g["W_down"]),
        "a_gate": rows(rank(g["A_gate"], g["sA_gate"])), "a_up": rows(rank(g["A_up"], g["sA_up"])),
        "a_down": rows(rank(g["A_down"], g["sA_down"])),
        "b_gate": on_top(wide(back(g["B_gate"], g["sB_gate"]), f)), "b_up": on_top(wide(back(g["B_up"], g["sB_up"]), f)),
        "b_down": on_top(back(g["B_down"], g["sB_down"])), "select": on_top(selector(9, 72, 8))})
    out["w_L3a"] = pack("L3a", {
        "s": rows(i["L3_attn_Ws"]), "a": rows(i["L3_attn_Wa"]), "o": rows(T(i["L3_attn_Wo"])), "bo": spread(i["L3_attn_bo"])})
    return out


def program(nc, arrays, out, phases):
    dram = {name: nc.dram_tensor(f"in_{name}", a.shape, mybir.dt.from_np(a.dtype), kind="ExternalInput").ap()
            for name, a in arrays.items()}
    with ExitStack() as ctx:
        core = Core(nc, ctx, dram)
        start(core)
        for phase in phases:
            phase(core)
        finish(core, out)


def kernel(**inputs):
    import concourse.bacc as _bacc
    from concourse.bass_utils import run_bass_kernel_spmd as _run

    nc = _bacc.Bacc("TRN2", target_bir_lowering=False, num_devices=1)
    arrays = arrays_of(inputs)
    out = nc.dram_tensor("out_x", (P, B * D), F32, kind="ExternalOutput").ap()
    program(nc, arrays, out, PHASES)
    r = _run(nc, [{f"in_{k}": v for k, v in arrays.items()}], core_ids=[0])
    return r.results[0]["out_x"].reshape(P, B, D).transpose(1, 0, 2)
```

```python
from contextlib import ExitStack, contextmanager

import concourse.bass as bass
import numpy as np
from concourse import mybir

F32 = mybir.dt.float32
I32 = mybir.dt.int32
U8 = mybir.dt.uint8
ALU = mybir.AluOpType
ACT = mybir.ActivationFunctionType
AX = mybir.AxisListType.X

P = 128
B = 16
D = 256
KD = D // P
G = 4
GROUPS = B // G
N = G * P
LN_EPS = 1e-5


def at(turn, per, count):
    return count if turn is None else turn * per + count


class Core:

    def __init__(self, nc, ctx, dram):
        self.nc, self.dram, self.ctx = nc, dram, ctx
        self.of_sublayer = []
        self.x = self.sb("x_tokens", [P, B, D])
        self.xnT = self.sb("xn_features", [P, KD, B, P])
        self.const = self.sb("const_sb", [P, dram["const"].shape[1]])
        self.arena = self.sb("arena", [P, ARENA])
        self.bank = [ctx.enter_context(nc.psum_tensor(f"bank{i}", [P, 512], F32)) for i in range(8)]
        self.ctx_sb = self.sb("ctx_tokens", [P, B, D])
        self.ctxT = self.sb("ctx_features", [P, KD, B, P])
        self.x_loaded = self.sem("x_loaded")
        self.const_loaded = self.sem("const_loaded")
        self.ctx_loaded = self.sem("ctx_loaded")
        self.passed = self.sem("passed")
        self.weights_loaded = {}
        self.ident = self.constant("ident")

    def sb(self, name, shape, dt=F32, ctx=None):
        return (ctx or self.ctx).enter_context(self.nc.sbuf_tensor(name, shape, dt))

    def sem(self, name, ctx=None):
        sem = (ctx or self.ctx).enter_context(self.nc.semaphore(name))
        if ctx is not None:
            self.of_sublayer.append(sem)
        return sem

    @contextmanager
    def block(self):
        with self.nc.Block() as block:
            yield block
        for sem in self.of_sublayer:
            self.nc.sync.sem_clear(sem)
        self.of_sublayer = []
        self.nc.all_engine_barrier()

    def constant(self, name):
        lo, hi = CONST_AT[name]
        return self.const[:, lo:hi]

    def held(self, eng):
        eng.sem_inc(self.passed, 1)

    def weights(self, name):
        base = WEIGHT_BASE.get(name, 0)
        out = {}
        for part, lo, hi in WEIGHT_PARTS[name]:
            out[part] = self.arena[:, base + lo:base + hi]
        return out

    def load(self, eng, name):
        if f"w_{name}" not in self.dram: return
        if name not in self.weights_loaded:
            self.weights_loaded[name] = self.sem(f"weights_loaded_{name}")
        base, width = WEIGHT_BASE[name], self.dram[f"w_{name}"].shape[1]
        eng.dma_start(self.arena[:, base:base + width], self.dram[f"w_{name}"]).then_inc(self.weights_loaded[name], 16)

    def work(self, name):
        lo, hi = WORK[name]
        taken = [lo]

        def carve(*shape):
            size = int(np.prod(shape))
            a = self.arena[:, taken[0]:taken[0] + size]
            taken[0] += size
            assert taken[0] <= hi, (name, taken[0], hi)
            if len(shape) == 2:
                return a.rearrange("p (a b) -> p a b", a=shape[0])
            if len(shape) == 3:
                return a.rearrange("p (a b c) -> p a b c", a=shape[0], b=shape[1])
            return a

        return carve


ARENA = 35200
WEIGHT_BASE = {"L0a": 0, "L0x": 34544, "L0f": 0, "L1a": 12640, "L1x": 0, "L1f": 12640, "L2a": 19900,
               "L2f": 12480, "L3a": 15064, "L3f": 15968, "L3sel": 13100}
WORK = {"L0a": (20512, 34544), "L0x": (12640, 34544), "L0f": (25200, 34544), "L1a": (25200, 35200),
        "L1x": (12560, 35200), "L1f": (0, 12640), "L2a": (0, 19900), "L2x": (0, 12480), "L2f": (0, 12480),
        "L3a": (0, 12480), "L3x": (0, 13100), "L3f": (0, 13100)}


def normalise(core, name, block, s, tokens=None):
    nc = core.nc
    mv, rstd, half, xn, stats = s["mv"], s["rstd"], s["half"], s["xn"], s["stats"]
    stats_done, mv_done, eps_done, rstd_done = s["stats_done"], s["mv_done"], s["eps_done"], s["rstd_done"]
    xn_done, turned, xnT_done = s["xn_done"], s["turned"], s["xnT_done"]

    def vector(dve):
        nc.vector.memset(half, -0.5)
        dve.wait_ge(core.x_loaded, 16)

        def statistics(g):
            of_group = range(g * G, (g + 1) * G)
            for b in of_group:
                nc.vector.bn_stats(stats[:, b, :], core.x[:, b, :]).then_inc(stats_done, 1)
            for b in of_group:
                dve.wait_ge(stats_done, b + 1)
                last = nc.vector.bn_aggr(mv[:, b, :], stats[:, b, :])
            last.then_inc(mv_done, 1)
            dve.wait_ge(mv_done, g + 1)
            nc.vector.tensor_scalar(rstd[:, g * G:(g + 1) * G], mv[:, g * G:(g + 1) * G, 1], LN_EPS, None,
                                    ALU.add).then_inc(eps_done, 1)

        def normalised(g):
            dve.wait_ge(rstd_done, g + 1)
            for b in range(g * G, (g + 1) * G):
                if tokens is None and b >= 4:
                    dve.wait_ge(turned, (b - 4) // 2 + 1)
                out = xn[:, b % 4, :] if tokens is None else tokens[:, b, :]
                nc.vector.tensor_scalar(out, core.x[:, b, :], mv[:, b, 0:1], rstd[:, b:b + 1],
                                        ALU.subtract, ALU.mult).then_inc(xn_done, 1)

        statistics(0)
        for g in range(GROUPS):
            if g + 1 < GROUPS:
                statistics(g + 1)
            normalised(g)

    def gpsimd(pool):
        for g in range(GROUPS):
            of_group = rstd[:, g * G:(g + 1) * G]
            pool.wait_ge(eps_done, g + 1)
            nc.gpsimd.tensor_tensor(of_group, of_group, half[:, g * G:(g + 1) * G], ALU.pow).then_inc(rstd_done, 1)

    def tensor(pe, with_pair=None):
        pe.wait_ge(core.const_loaded, 16)
        for i in range(B // 2):
            pe.wait_ge(xn_done, 2 * i + 2)
            if i >= 2:
                pe.wait_ge(xnT_done, i - 1)
            for k in range(KD):
                for b in (2 * i, 2 * i + 1):
                    last = nc.tensor.transpose(
                        core.bank[i % 2][:, k * 256 + (b % 2) * P:k * 256 + (b % 2) * P + P],
                        xn[:, b % 4, k * P:(k + 1) * P], core.ident)
            last.then_inc(turned, 1)
            if with_pair and i >= 1:
                pe.wait_ge(xnT_done, i)
                with_pair(i - 1)
        if with_pair:
            pe.wait_ge(xnT_done, B // 2)
            with_pair(B // 2 - 1)

    def scalar(act):
        for i in range(B // 2):
            act.wait_ge(turned, i + 1)
            nc.scalar.activation(core.xnT[:, :, 2 * i:2 * i + 2, :],
                                 core.bank[i % 2][:, :].rearrange("p (k b t) -> p k b t", k=KD, b=2),
                                 ACT.Copy).then_inc(xnT_done, 1)

    return vector, gpsimd, tensor, scalar


def norm_state(core, name, carve, ctx, turn_to_features=True):
    s = {n: core.sem(f"{name}_{n}", ctx) for n in
         ("stats_done", "mv_done", "eps_done", "rstd_done", "xn_done", "turned", "xnT_done")}
    s["stats"] = carve(B, 6)
    s["mv"] = carve(B, 2)
    s["rstd"] = carve(B)
    s["half"] = carve(B)
    s["xn"] = carve(4, D) if turn_to_features else None
    return s


def lightning_attention(core):
    nc, H, EPS = core.nc, 16, 1e-6
    w = core.weights("L0a")
    wqkv = w["qkv"].rearrange("p (k h c n) -> p k h c n", k=KD, h=H, c=3)
    wgate = w["gate"].rearrange("p (k h n) -> p k h n", k=KD, h=H)
    wout = w["out"].rearrange("p (h n) -> p h n", h=H)
    norm_w = w["norm"]
    slope = w["slope"]
    with ExitStack() as ctx:
        sem = lambda name: core.sem(f"L0a_{name}", ctx)
        carve = core.work("L0a")
        s = norm_state(core, "L0a", carve, ctx)
        decay = carve(H, P)
        xcur = carve(KD, N)
        qT, kT, v, gate, ow, sq, z = (carve(2, N) for _ in range(7))
        attn = carve(N)
        sumsq = carve(N)
        zeros = carve(N)
        msq = carve(G)
        half = s["half"][:, 0:G]
        q_bank, k_bank, v_bank, g_bank, s_bank, o_bank = core.bank[0:6]
        y_bank = core.bank[6:8]

        slope_neg, decay_exp, decay_done = sem("slope_neg"), sem("decay_exp"), sem("decay_done")
        xcur_done, xcur_used = sem("xcur_done"), sem("xcur_used")
        q_made, k_made, v_made, g_made = sem("q_made"), sem("k_made"), sem("v_made"), sem("g_made")
        qT_done, kT_done, v_done, gate_done = sem("qT_done"), sem("kT_done"), sem("v_done"), sem("gate_done")
        scores_made, attn_done, o_made = sem("scores_made"), sem("attn_done"), sem("o_made")
        ow_done, sq_done, sumsq_done, z_done = sem("ow_done"), sem("sq_done"), sem("sumsq_done"), sem("z_done")
        ssq_made, msq_done, rms_done, y_made, y_added = (
            sem("ssq_made"), sem("msq_done"), sem("rms_done"), sem("y_made"), sem("y_added"))
        block = ctx.enter_context(core.block())
        n_vector, n_gpsimd, n_tensor, n_scalar = normalise(core, "L0a", block, s)

        @block.gpsimd
        def _(pool):
            pool.wait_ge(core.x_loaded, 16)
            nc.gpsimd.memset(zeros, 0.0)
            n_gpsimd(pool)
            with pool.Fori(0, GROUPS) as t:
                pool.wait_ge(xcur_used, at(t, 1, 1))
                pool.wait_ge(s["xnT_done"], at(t, 2, 2))
                core.held(pool)
                nc.gpsimd.tensor_copy(xcur.rearrange("p k (b t) -> p k b t", b=G),
                                      core.xnT[:, :, bass.ds(t * G, G), :]).then_inc(xcur_done, 1)
                for h in range(H):
                    pool.wait_ge(sq_done, at(t, H, h + 1))
                    if h == 0:
                        nc.gpsimd.tensor_tensor(sumsq, sq[:, 0, :], zeros, ALU.add).then_inc(sumsq_done, 1)
                    else:
                        pool.wait_ge(sumsq_done, at(t, H, h))
                        nc.gpsimd.tensor_tensor(sumsq, sumsq, sq[:, h % 2, :], ALU.add).then_inc(sumsq_done, 1)
                pool.wait_ge(msq_done, at(t, 1, 1))
                nc.gpsimd.tensor_tensor(msq, msq, half, ALU.pow).then_inc(rms_done, 1)

        @block.tensor
        def _(pe):
            pe.wait_ge(core.const_loaded, 16)
            pe.sem_inc(xcur_used, 1)
            n_tensor(pe)
            pe.wait_ge(core.weights_loaded["L0a"], 16)
            pe.wait_ge(s["xnT_done"], B // 2)
            with pe.Fori(0, GROUPS) as t:
                pe.wait_ge(xcur_done, at(t, 1, 1))
                for step in range(H + 2):
                    if step < H:
                        h = step
                        if h:
                            pe.wait_ge(qT_done, at(t, H, h))
                        for k in range(KD):
                            last = nc.tensor.matmul(q_bank[:, :], wqkv[:, k, h, 0, :], xcur[:, k, :],
                                                    start=(k == 0), stop=(k == KD - 1))
                        last.then_inc(q_made, 1)
                        if h:
                            pe.wait_ge(kT_done, at(t, H, h))
                        for k in range(KD):
                            last = nc.tensor.matmul(k_bank[:, :], wqkv[:, k, h, 1, :], xcur[:, k, :],
                                                    start=(k == 0), stop=(k == KD - 1))
                        last.then_inc(k_made, 1)
                    if 1 <= step <= H:
                        h = step - 1
                        pe.wait_ge(kT_done, at(t, H, h + 1))
                        pe.wait_ge(qT_done, at(t, H, h + 1))
                        if h:
                            pe.wait_ge(attn_done, at(t, H, h))
                        else:
                            pe.wait_ge(y_added, at(t, 1, 1))
                        for j in range(G):
                            last = nc.tensor.matmul(s_bank[:, j * P:(j + 1) * P], kT[:, h % 2, j * P:(j + 1) * P],
                                                    qT[:, h % 2, j * P:(j + 1) * P], start=True, stop=True)
                        last.then_inc(scores_made, 1)
                    if step < H:
                        h = step
                        if h:
                            pe.wait_ge(v_done, at(t, H, h))
                        for j in range(G):
                            for k in range(KD):
                                last = nc.tensor.matmul(v_bank[:, j * P:(j + 1) * P], xcur[:, k, j * P:(j + 1) * P],
                                                        wqkv[:, k, h, 2, :], start=(k == 0), stop=(k == KD - 1))
                        last.then_inc(v_made, 1)
                        if h:
                            pe.wait_ge(gate_done, at(t, H, h))
                        for k in range(KD):
                            last = nc.tensor.matmul(g_bank[:, :], wgate[:, k, h, :], xcur[:, k, :],
                                                    start=(k == 0), stop=(k == KD - 1))
                        last.then_inc(g_made, 1)
                        if h == H - 1:
                            pe.wait_ge(g_made, at(t, H, H))
                            pe.sem_inc(xcur_used, 1)
                    if 1 <= step <= H:
                        h = step - 1
                        pe.wait_ge(attn_done, at(t, H, h + 1))
                        pe.wait_ge(v_done, at(t, H, h + 1))
                        if h:
                            pe.wait_ge(sq_done, at(t, H, h))
                        for j in range(G):
                            last = nc.tensor.matmul(o_bank[:, j * P:(j + 1) * P], v[:, h % 2, j * P:(j + 1) * P],
                                                    attn[:, j * P:(j + 1) * P], start=True, stop=True)
                        last.then_inc(o_made, 1)
                    if step >= 2:
                        h = step - 2
                        pe.wait_ge(z_done, at(t, H, h + 1))
                        for j in range(G):
                            last = nc.tensor.matmul(y_bank[j // 2][:, (j % 2) * D:(j % 2 + 1) * D],
                                                    z[:, h % 2, j * P:(j + 1) * P], wout[:, h, :],
                                                    start=(h == 0 and j % 2 == 0), stop=(h == H - 1),
                                                    skip_group_check=True)
                last.then_inc(y_made, 1)
                pe.wait_ge(sumsq_done, at(t, H, H))
                for j in range(G):
                    last = nc.tensor.matmul(s_bank[:, j:j + 1], sumsq[:, j * P:(j + 1) * P],
                                            core.constant("ones")[:, 0:1], start=True, stop=True)
                last.then_inc(ssq_made, 1)

        @block.scalar
        def _(act):
            n_scalar(act)
            act.wait_ge(core.weights_loaded["L0a"], 16)
            nc.scalar.mul(slope, slope, -1.0).then_inc(slope_neg, 1)
            act.wait_ge(slope_neg, 1)
            for h in range(H):
                last = nc.scalar.activation(decay[:, h, :], core.constant("dist"), ACT.Exp, scale=slope[:, h:h + 1])
            last.then_inc(decay_exp, 1)
            with act.Fori(0, GROUPS) as t:
                for step in range(H + 1):
                    if step < H:
                        h = step
                        act.wait_ge(q_made, at(t, H, h + 1))
                        nc.scalar.activation(qT[:, h % 2, :], q_bank[:, :], ACT.Silu).then_inc(qT_done, 1)
                        act.wait_ge(k_made, at(t, H, h + 1))
                        nc.scalar.activation(kT[:, h % 2, :], k_bank[:, :], ACT.Silu).then_inc(kT_done, 1)
                        act.wait_ge(v_made, at(t, H, h + 1))
                        nc.scalar.activation(v[:, h % 2, :], v_bank[:, :], ACT.Silu).then_inc(v_done, 1)
                        act.wait_ge(g_made, at(t, H, h + 1))
                        if h >= 2:
                            act.wait_ge(z_done, at(t, H, h - 1))
                        nc.scalar.activation(gate[:, h % 2, :], g_bank[:, :], ACT.Tanh, scale=0.5).then_inc(gate_done, 1)
                    if step >= 1:
                        h = step - 1
                        act.wait_ge(o_made, at(t, H, h + 1))
                        if h >= 2:
                            act.wait_ge(sumsq_done, at(t, H, h - 1))
                            act.wait_ge(z_done, at(t, H, h - 1))
                        nc.scalar.activation(ow[:, h % 2, :], o_bank[:, :], ACT.Copy, scale=norm_w[:, h:h + 1]).then_inc(ow_done, 1)
                        nc.scalar.activation(sq[:, h % 2, :], o_bank[:, :], ACT.Square).then_inc(sq_done, 1)

        @block.vector
        def _(dve):
            dve.wait_ge(core.x_loaded, 16)
            n_vector(dve)
            dve.wait_ge(core.const_loaded, 16)
            dve.wait_ge(decay_exp, 1)
            nc.vector.tensor_tensor(decay, decay, core.constant("causalT").unsqueeze(1).to_broadcast([P, H, P]),
                                    ALU.mult).then_inc(decay_done, 1)
            dve.wait_ge(decay_done, 1)
            dve.sem_inc(y_added, 1)
            with dve.Fori(0, GROUPS) as t:
                for h in range(H):
                    dve.wait_ge(scores_made, at(t, H, h + 1))
                    nc.vector.tensor_tensor(attn.rearrange("p (j t) -> p j t", j=G),
                                            s_bank[:, :].rearrange("p (j t) -> p j t", j=G),
                                            decay[:, h, :].unsqueeze(1).to_broadcast([P, G, P]),
                                            ALU.mult).then_inc(attn_done, 1)
                    dve.wait_ge(ow_done, at(t, H, h + 1))
                    dve.wait_ge(gate_done, at(t, H, h + 1))
                    nc.vector.scalar_tensor_tensor(out=z[:, h % 2, :], in0=gate[:, h % 2, :], scalar=1.0,
                                                   in1=ow[:, h % 2, :], op0=ALU.add, op1=ALU.mult).then_inc(z_done, 1)
                dve.wait_ge(ssq_made, at(t, 1, 1))
                nc.vector.tensor_scalar(msq, s_bank[:, 0:G], 4.0 / (H * P), 4.0 * EPS, ALU.mult, ALU.add).then_inc(msq_done, 1)
                dve.wait_ge(rms_done, at(t, 1, 1))
                dve.wait_ge(y_made, at(t, 1, 1))
                for j in range(G):
                    xj = core.x[:, bass.ds(t * G + j, 1), :].squeeze(1)
                    last = nc.vector.scalar_tensor_tensor(out=xj, in0=y_bank[j // 2][:, (j % 2) * D:(j % 2 + 1) * D],
                                                          scalar=msq[:, j:j + 1], in1=xj, op0=ALU.mult, op1=ALU.add)
                last.then_inc(y_added, 1)


def channel_cross_attention(core):
    nc, H, C = core.nc, 16, 8
    SEQS = 4
    UNITS, BATCHES = SEQS * H, SEQS * 4
    SM, PT = 4, 12
    T_LAG = 4
    PT_LAG = T_LAG - 1
    O_LAG = T_LAG + 5
    made_at = lambda i: H * (i + 1) - 2 + O_LAG
    SCALE = 1.0 / float(np.sqrt(np.float32(C)))
    w = core.weights("L0x")
    with ExitStack() as ctx:
        sem = lambda name: core.sem(f"L0x_{name}", ctx)
        carve = core.work("L0x")
        s = norm_state(core, "L0x", carve, ctx, turn_to_features=False)
        q_all = core.xnT.rearrange("p k b t -> p (k b t)").rearrange("p (b d) -> p b d", b=B)
        v_all = core.ctxT.rearrange("p k b t -> p (k b t)").rearrange("p (b d) -> p b d", b=B)
        k_all = carve(B, D)
        q_cur = carve(2, D)
        k_one = carve(2, 4, D)
        v_one = carve(2, 2, P)
        sm, probs, pT = carve(SM, 2 * D), carve(SM, 2 * D), carve(PT, 2 * D)
        biased, sin_part = pT, sm
        mask_in, chanmask = carve(2 * D), carve(P)
        keep, fill = carve(2 * D), carve(2 * D)
        peak_neg = carve(SM, 2)
        total_inv, oT = carve(2, D), carve(2, D)
        bank = core.bank
        t_bank, o_bank, s_bank, y_bank = bank[0:2], bank[2:4], bank[4:7], bank[7]
        k_mask = lambda n: core.constant("headmask")[:, 4 * n:4 * n + 4]
        v_mask = lambda n: chanmask[:, 32 * n:32 * n + 32]

        chanmask_loaded = sem("chanmask_loaded")
        mask_loaded, fill_done, keep_done = sem("mask_loaded"), sem("fill_done"), sem("keep_done")
        proj_made, biased_done, turn_made = sem("proj_made"), sem("biased_done"), sem("turn_made")
        cos_done, sin_done, roped = sem("cos_done"), sem("sin_done"), sem("roped")
        v_made, v_done = sem("v_made"), sem("v_done")
        k_staged, v_staged = sem("k_staged"), sem("v_staged")
        scores_made, masked, peak_done = sem("scores_made"), sem("masked"), sem("peak_done")
        exp_done, p_turned, pT_done, o_made = sem("exp_done"), sem("p_turned"), sem("pT_done"), sem("o_made")
        inverted, oT_done, y_made, y_added = sem("inverted"), sem("oT_done"), sem("y_made"), sem("y_added")
        block = ctx.enter_context(core.block())
        n_vector, n_gpsimd, _, _ = normalise(core, "L0x", block, s, tokens=q_all)

        @block.sync
        def _(sp):
            sp.dma_start(mask_in.bitcast(I32), core.dram["attn_mask"]).then_inc(mask_loaded, 16)
            sp.dma_start(chanmask, core.dram["chanmask"]).then_inc(chanmask_loaded, 16)
            core.load(sp, "L0f")

        @block.gpsimd
        def _(pool):
            n_gpsimd(pool)
            for i in range(B):
                dst, b = (q_all, 2 * i) if i < B // 2 else (k_all, 2 * i - B)
                pool.wait_ge(sin_done, i + 1)
                pool.wait_ge(cos_done, i + 1)
                nc.gpsimd.tensor_tensor(dst[:, b:b + 2, :], dst[:, b:b + 2, :],
                                        sin_part[:, i % 2, :].rearrange("p (b d) -> p b d", b=2), ALU.add).then_inc(roped, 1)
            pool.wait_ge(roped, B)
            pool.wait_ge(v_done, B // 2)
            pool.wait_ge(chanmask_loaded, 16)
            with pool.Fori(0, B // SEQS) as t:
                for m in range(BATCHES + 1):
                    if m < BATCHES:
                        i, n = m // 4, m % 4
                        pool.wait_ge(scores_made, at(t, UNITS, 4 * (m - 1) + 8))
                        core.held(pool)
                        if n == 0:
                            nc.gpsimd.tensor_copy(q_cur[:, i % 2, :], q_all[:, bass.ds(SEQS * t + i, 1), :].squeeze(1))
                        nc.gpsimd.tensor_tensor(k_one[:, m % 2, :, :], k_all[:, bass.ds(SEQS * t + i, 1), :].to_broadcast([P, 4, D]),
                                                k_mask(n).unsqueeze(2).to_broadcast([P, 4, D]), ALU.mult).then_inc(k_staged, 1)
                    if m >= 1:
                        i, n = (m - 1) // 4, (m - 1) % 4
                        pool.wait_ge(o_made, at(t, BATCHES, m))
                        core.held(pool)
                        nc.gpsimd.tensor_tensor(v_one[:, (m - 1) % 2, :, :].rearrange("p a (g c) -> p (a g) c", g=4),
                                                v_all[:, bass.ds(SEQS * t + i, 1), :].squeeze(1).rearrange("p (a c) -> p a c", c=32),
                                                v_mask(n).unsqueeze(1).to_broadcast([P, 8, 32]), ALU.mult).then_inc(v_staged, 1)

        @block.tensor
        def _(pe):
            pe.wait_ge(core.weights_loaded["L0x"], 16)
            pe.wait_ge(core.const_loaded, 16)
            pe.wait_ge(core.ctx_loaded, 16)
            for i in range(B + 1):
                if i < B:
                    src, wt, b = (q_all, w["q"], 2 * i) if i < B // 2 else (core.ctx_sb, w["k"], 2 * i - B)
                    if i < B // 2:
                        pe.wait_ge(s["xn_done"], b + 2)
                    if i >= 2:
                        pe.wait_ge(biased_done, i - 1)
                    nc.tensor.matmul(bank[i % 2][:, :], wt, src[:, b:b + 2, :].rearrange("p b d -> p (b d)"),
                                     start=True, stop=True).then_inc(proj_made, 1)
                if i >= 1:
                    pe.wait_ge(biased_done, i)
                    if i >= 3:
                        pe.wait_ge(sin_done, i - 2)
                    nc.tensor.matmul(bank[2 + (i - 1) % 2][:, :], core.constant("turn0"), biased[:, (i - 1) % 2, :],
                                     start=True, stop=True).then_inc(turn_made, 1)
            for i in range(B // 2):
                if i >= 2:
                    pe.wait_ge(v_done, i - 1)
                for j in range(4):
                    b, half = 2 * i + j // 2, j % 2
                    last = nc.tensor.matmul(bank[4 + i % 2][:, j * P:(j + 1) * P],
                                            core.ctx_sb[:, b, half * P:(half + 1) * P], w["v"], start=True, stop=True)
                last.then_inc(v_made, 1)
            pe.wait_ge(chanmask_loaded, 16)
            pe.sem_inc(scores_made, 8)
            pe.sem_inc(o_made, 2)
            with pe.Fori(0, B // SEQS) as t:
                for step in range(made_at(SEQS - 1) + 6):
                    if step < UNITS:
                        u, m, g = step, step // 4, step % 4
                        if g == 0:
                            pe.wait_ge(k_staged, at(t, BATCHES, m + 1))
                        if u >= 3:
                            pe.wait_ge(masked, at(t, UNITS, u - 2))
                        for half in range(2):
                            last = nc.tensor.matmul(s_bank[u % 3][:, half * D:(half + 1) * D],
                                                    q_cur[:, m // 4 % 2, half * P:(half + 1) * P],
                                                    k_one[:, m % 2, g, :], start=True, stop=True)
                        last.then_inc(scores_made, 1)
                    if T_LAG <= step < UNITS + T_LAG:
                        u = step - T_LAG
                        pe.wait_ge(exp_done, at(t, UNITS, u + 1))
                        if u >= 2:
                            pe.wait_ge(pT_done, at(t, UNITS, u - 1))
                        for kh in range(2):
                            for qh in range(2):
                                last = nc.tensor.transpose(t_bank[u % 2][:, kh * D + qh * P:kh * D + (qh + 1) * P],
                                                           probs[:, u % SM, qh * D + kh * P:qh * D + (kh + 1) * P], core.ident)
                        last.then_inc(p_turned, 1)
                    if step >= O_LAG and (step - O_LAG) % 2 == 0 and step <= made_at(SEQS - 1):
                        m, part = (step - O_LAG) // 4, (step - O_LAG) % 4 // 2
                        i, n = m // 4, m % 4
                        if part == 0:
                            pe.wait_ge(v_staged, at(t, BATCHES, m + 1))
                            pe.wait_ge(pT_done, at(t, UNITS, 4 * m + 4))
                            if n == 0:
                                pe.wait_ge(oT_done, at(t, SEQS, i + 1))
                        for kh in range(2):
                            for g in range(4):
                                left = v_one[:, m % 2, kh, 32 * g:32 * g + 32] if part == 0 else v_mask(n)
                                last = nc.tensor.matmul(o_bank[i % 2][32 * g:32 * g + 32, part * D:(part + 1) * D], left,
                                                        pT[:, (4 * m + g) % PT, kh * D:(kh + 1) * D],
                                                        start=(n == 0 and part == 0 and kh == 0),
                                                        stop=(n == 3 and kh == 1), skip_group_check=True)
                        if part == 1:
                            last.then_inc(o_made, 1)
                    for i in range(SEQS):
                        if step == made_at(i) + 5:
                            pe.wait_ge(oT_done, at(t, SEQS, i + 3))
                            pe.wait_ge(y_added, at(t, SEQS, i + 1))
                            nc.tensor.matmul(y_bank[:, 0:D], w["o"], oT[:, i % 2, :], start=True, stop=True).then_inc(y_made, 1)

        @block.scalar
        def _(act):
            act.wait_ge(core.weights_loaded["L0x"], 16)
            for i in range(B):
                act.wait_ge(proj_made, i + 1)
                if i >= 2:
                    act.wait_ge(cos_done, i - 1)
                    act.wait_ge(turn_made, i - 1)
                bias = w["bq"] if i < B // 2 else w["bk"]
                nc.scalar.activation(biased[:, i % 2, :], bank[i % 2][:, :], ACT.Identity, bias=bias).then_inc(biased_done, 1)
            with act.Fori(0, B // SEQS) as t:
                act.wait_ge(o_made, at(t, BATCHES, 2))
                for step in range(UNITS + PT_LAG):
                    if PT_LAG <= step < UNITS + PT_LAG:
                        u = step - PT_LAG
                        act.wait_ge(p_turned, at(t, UNITS, u + 1))
                        if u >= PT and u % 4 == 0:
                            act.wait_ge(o_made, at(t, BATCHES, (u - PT) // 4 + 3))
                        nc.scalar.copy(pT[:, u % PT, :], t_bank[u % 2][:, :]).then_inc(pT_done, 1)
                    if step < UNITS:
                        u = step
                        act.wait_ge(peak_done, at(t, UNITS, u + 1))
                        if u >= SM:
                            act.wait_ge(p_turned, at(t, UNITS, u - SM + 1))
                        for half in range(2):
                            last = nc.scalar.activation(probs[:, u % SM, half * D:(half + 1) * D],
                                                        sm[:, u % SM, half * D:(half + 1) * D], ACT.Exp,
                                                        bias=peak_neg[:, u % SM, half:half + 1], scale=-1.0)
                        last.then_inc(exp_done, 1)

        @block.vector
        def _(dve):
            n_vector(dve)
            dve.wait_ge(mask_loaded, 16)
            nc.vector.tensor_scalar(fill, mask_in.bitcast(I32), 0.0, 10000.0, ALU.is_equal, ALU.mult).then_inc(fill_done, 1)
            nc.vector.tensor_scalar(keep, mask_in.bitcast(I32), 0.0, -SCALE, ALU.not_equal, ALU.mult).then_inc(keep_done, 1)
            dve.wait_ge(keep_done, 1)
            dve.wait_ge(fill_done, 1)
            cos = core.constant("cos0").unsqueeze(1).to_broadcast([P, 2, D])
            sin = core.constant("sin0").unsqueeze(1).to_broadcast([P, 2, D])
            pair = lambda a: a.rearrange("p (b d) -> p b d", b=2)
            for i in range(B):
                dst, b = (q_all, 2 * i) if i < B // 2 else (k_all, 2 * i - B)
                dve.wait_ge(biased_done, i + 1)
                nc.vector.tensor_tensor(dst[:, b:b + 2, :], pair(biased[:, i % 2, :]), cos, ALU.mult).then_inc(cos_done, 1)
                dve.wait_ge(turn_made, i + 1)
                if i >= 2:
                    dve.wait_ge(roped, i - 1)
                nc.vector.tensor_tensor(pair(sin_part[:, i % 2, :]), pair(bank[2 + i % 2][:, :]), sin, ALU.mult).then_inc(sin_done, 1)
            bv = w["bv"].unsqueeze(1).to_broadcast([P, 4, P])
            for i in range(B // 2):
                dve.wait_ge(v_made, i + 1)
                nc.vector.tensor_tensor(v_all[:, 2 * i:2 * i + 2, :].rearrange("p b (h c) -> p (b h) c", h=2),
                                        bank[4 + i % 2][:, :].rearrange("p (a c) -> p a c", a=4), bv, ALU.add).then_inc(v_done, 1)
            dve.wait_ge(v_done, B // 2)
            dve.wait_ge(roped, B)
            dve.sem_inc(oT_done, 2)
            dve.sem_inc(y_added, 1)

            def invert_sums(t, i, half):
                if half == 0:
                    dve.wait_ge(o_made, at(t, BATCHES, 4 * i + 4 + 2))
                nc.vector.reciprocal(total_inv[:, i % 2, half * P:(half + 1) * P],
                                     o_bank[i % 2][:, D + half * P:D + (half + 1) * P]).then_inc(inverted, 1)

            def normalise_heads(t, i):
                dve.wait_ge(inverted, at(t, 2 * SEQS, 2 * i + 2))
                nc.vector.tensor_tensor(oT[:, i % 2, :], o_bank[i % 2][:, 0:D], total_inv[:, i % 2, :], ALU.mult).then_inc(oT_done, 1)

            def add_to_x(t, i):
                dve.wait_ge(y_made, at(t, SEQS, i + 1))
                xb = core.x[:, bass.ds(SEQS * t + i, 1), :].squeeze(1)
                nc.vector.scalar_tensor_tensor(out=xb, in0=y_bank[:, 0:D], scalar=w["bo"], in1=xb,
                                               op0=ALU.add, op1=ALU.add).then_inc(y_added, 1)

            with dve.Fori(0, B // SEQS) as t:
                for step in range(made_at(SEQS - 1) + 8):
                    if step < UNITS:
                        u = step
                        dve.wait_ge(scores_made, at(t, UNITS, u + 1 + 8))
                        if u >= SM:
                            dve.wait_ge(exp_done, at(t, UNITS, u - SM + 1))
                        nc.vector.tensor_tensor(sm[:, u % SM, :], s_bank[u % 3][:, :], keep, ALU.mult).then_inc(masked, 1)
                    if 1 <= step <= UNITS:
                        u = step - 1
                        dve.wait_ge(masked, at(t, UNITS, u + 1))
                        core.held(dve)
                        for half in range(2):
                            part = sm[:, u % SM, half * D:(half + 1) * D]
                            last = nc.vector.tensor_tensor_reduce(out=part, in0=part, in1=fill[:, half * D:(half + 1) * D],
                                                                  scale=1.0, scalar=3e38, op0=ALU.add, op1=ALU.min,
                                                                  accum_out=peak_neg[:, u % SM, half:half + 1])
                        last.then_inc(peak_done, 1)
                    for i in range(SEQS):
                        if step in (made_at(i) + 1, made_at(i) + 2):
                            invert_sums(t, i, step - made_at(i) - 1)
                        if step == made_at(i) + 3:
                            normalise_heads(t, i)
                        if step == made_at(i) + 7:
                            add_to_x(t, i)


def router(core, name, E, top, kind, s, gate, carve, scratch, ctx, bias=None, scale=1.0, floor=0.0, ones=0):
    nc = core.nc
    logits_bank, turn_bank = core.bank[2], core.bank[3:5]
    R = E + ones
    score, chosen_by, rank, total = carve(B, E), carve(B, E), carve(B, E), carve(B)
    share = carve(B, R)
    shareT = carve(B * P)
    ahead = scratch[:, 0:B * E * E].rearrange("p (b e f) -> p b e f", b=B, e=E)
    spare = carve(1)
    sem = lambda n: core.sem(f"{name}_{n}", ctx)
    logits_made, scored, step_done, share_done, share_turned, shareT_done = (
        sem("logits_made"), sem("scored"), sem("route_step"), sem("share_done"), sem("share_turned"), sem("shareT_done"))
    logits = logits_bank[:, 0:B * E].rearrange("p (b e) -> p b e", b=B)

    def tensor(pe, n_tensor):
        def logits_of_pair(i):
            for b in (2 * i, 2 * i + 1):
                for k in range(KD):
                    last = nc.tensor.matmul(logits_bank[:, b * E:(b + 1) * E], core.xnT[:, k, b, :],
                                            gate[:, k * E:(k + 1) * E], start=(k == 0), stop=(k == KD - 1))
            if i == B // 2 - 1:
                last.then_inc(logits_made, 1)

        pe.wait_ge(core.weights_loaded[name], 16)
        n_tensor(pe, logits_of_pair)
        pe.wait_ge(share_done, 1)
        for i in range(B // 4):
            if i >= 2:
                pe.wait_ge(shareT_done, i - 1)
            for b in range(4 * i, 4 * i + 4):
                last = nc.tensor.matmul(turn_bank[i % 2][0:R, (b % 4) * P:(b % 4 + 1) * P], share[:, b, :],
                                        core.ident, start=True, stop=True)
            last.then_inc(share_turned, 1)

    def scalar(act):
        if kind == "sigmoid":
            act.wait_ge(logits_made, 1)
            nc.scalar.activation(score, logits, ACT.Sigmoid).then_inc(scored, 1)
        else:
            act.wait_ge(step_done, 2)
            nc.scalar.activation(score, score, ACT.Exp).then_inc(scored, 1)
        for i in range(B // 4):
            act.wait_ge(share_turned, i + 1)
            nc.scalar.copy(shareT[0:R, i * N:(i + 1) * N], turn_bank[i % 2][0:R, :]).then_inc(shareT_done, 1)

    def vector(dve):
        done = [0]

        def step(instruction):
            done[0] += 1
            instruction.then_inc(step_done, 1)
            dve.wait_ge(step_done, done[0])

        each = lambda a: a.unsqueeze(2).to_broadcast([P, B, E])
        if kind == "softmax":
            dve.wait_ge(logits_made, 1)
            step(nc.vector.tensor_reduce(total, logits, AX, ALU.max))
            step(nc.vector.tensor_tensor(score, logits, each(total), ALU.subtract))
            dve.wait_ge(scored, 1)
            step(nc.vector.tensor_reduce(total, score, AX, ALU.add))
            step(nc.vector.reciprocal(total, total))
            step(nc.vector.tensor_tensor(score, score, each(total), ALU.mult))
        dve.wait_ge(scored, 1)
        by = score
        if bias is not None:
            step(nc.vector.tensor_tensor(chosen_by, score, bias.unsqueeze(1).to_broadcast([P, B, E]), ALU.add))
            by = chosen_by
        for e in range(E):
            if e:
                nc.vector.tensor_tensor(ahead[:, :, e, 0:e], by[:, :, 0:e], by[:, :, e:e + 1].to_broadcast([P, B, e]), ALU.is_ge)
            last = nc.vector.tensor_tensor(ahead[:, :, e, e:E], by[:, :, e:E], by[:, :, e:e + 1].to_broadcast([P, B, E - e]), ALU.is_gt)
        step(last)
        step(nc.vector.tensor_reduce(rank, ahead, AX, ALU.add))
        step(nc.vector.tensor_scalar(rank, rank, float(top), None, ALU.is_lt))
        if kind == "sigmoid":
            step(nc.vector.tensor_tensor(score, score, rank, ALU.mult))
            step(nc.vector.tensor_reduce(total, score, AX, ALU.add))
            step(nc.vector.tensor_scalar(total, total, floor, None, ALU.add))
            step(nc.vector.reciprocal(total, total))
            step(nc.vector.tensor_tensor(score, score, each(total), ALU.mult))
            step(nc.vector.tensor_scalar(share[:, :, 0:E], score, scale, None, ALU.mult))
        else:
            step(nc.vector.scalar_tensor_tensor(out=share[:, :, 0:E], in0=score, scalar=scale, in1=rank,
                                                op0=ALU.mult, op1=ALU.mult))
        nc.vector.memset(share[:, :, E:R] if ones else spare, scale if ones else 0.0).then_inc(share_done, 1)

    return shareT, shareT_done, (vector, tensor, scalar)


def experts(core, name, E, top, kind, chunks, routed, gated=True, **how):
    nc = core.nc
    w = core.weights(name)
    F = chunks * P
    wg = w["gate"].rearrange("p (k f) -> p k f", k=KD)
    wu = w["up"].rearrange("p (k f) -> p k f", k=KD) if gated else None
    wd = w["down"].rearrange("p (c d) -> p c d", c=chunks)
    select = (w["select"] if "select" in w else core.weights("L3sel")["select"])[0:E, :]
    with ExitStack() as ctx:
        sem = lambda n: core.sem(f"{name}_{n}", ctx)
        carve = core.work(name)
        s = norm_state(core, name, carve, ctx)
        scratch = carve(2 * B * E * E) if E == 16 else carve(max(2 * B * E * E, 3 * 2 * N))
        first, partly, h = (scratch[:, 2 * i * N:2 * (i + 1) * N].rearrange("p (a n) -> p a n", a=2) for i in range(3))
        shareT, shareT_done, (r_vector, r_tensor, r_scalar) = router(
            core, name, E, top, kind, s, w["router"], carve, scratch, ctx, **how)
        g_bank, u_bank, c_bank, y_bank = core.bank[0:2], core.bank[2:4], core.bank[4:6], core.bank[6:8]
        g_made, u_made, c_made = sem("g_made"), sem("u_made"), sem("c_made")
        first_done, partly_done, h_done = sem("first_done"), sem("partly_done"), sem("h_done")
        y_made, y_added = sem("y_made"), sem("y_added")
        block = ctx.enter_context(core.block())
        n_vector, n_gpsimd, n_tensor, n_scalar = normalise(core, name, block, s)
        parts = ([(wg, g_bank, g_made), (wu, u_bank, u_made)] if gated else [(wg, g_bank, g_made)])

        @block.sync
        def _(sp):
            for what in LOADS[name]:
                core.load(sp, what)

        @block.gpsimd
        def _(pool):
            n_gpsimd(pool)

        @block.tensor
        def _(pe):
            r_tensor(pe, n_tensor)
            if "select" not in w:
                pe.wait_ge(core.weights_loaded["L3sel"], 16)
            pe.wait_ge(shareT_done, B // 4)
            with pe.Fori(0, GROUPS) as t:
                for step in range(chunks + 1):
                    if step < chunks:
                        c = step
                        if c >= 2:
                            pe.wait_ge(h_done, at(t, chunks, c - 1))
                        elif c == 0:
                            pe.wait_ge(y_added, at(t, 1, 1))
                        for wt, bank, made in parts:
                            for k in range(KD):
                                last = nc.tensor.matmul(
                                    bank[c % 2][:, :], wt[:, k, c * P:(c + 1) * P],
                                    core.xnT[:, k, bass.ds(t * G, G), :], start=(k == 0), stop=(k == KD - 1))
                            last.then_inc(made, 1)
                        if c < routed:
                            nc.tensor.matmul(c_bank[c % 2][:, :], select[:, c * P:(c + 1) * P],
                                             shareT[0:E, bass.ds(t * N, N)], start=True, stop=True).then_inc(c_made, 1)
                    if step >= 1:
                        c = step - 1
                        pe.wait_ge(h_done, at(t, chunks, c + 1))
                        for j in range(G):
                            last = nc.tensor.matmul(y_bank[j // 2][:, (j % 2) * D:(j % 2 + 1) * D],
                                                    h[:, c % 2, j * P:(j + 1) * P], wd[:, c, :],
                                                    start=(c == 0 and j % 2 == 0), stop=(c == chunks - 1),
                                                    skip_group_check=True)
                last.then_inc(y_made, 1)

        @block.scalar
        def _(act):
            n_scalar(act)
            r_scalar(act)
            act.wait_ge(shareT_done, B // 4)
            with act.Fori(0, GROUPS) as t:
                for c in range(chunks):
                    act.wait_ge(g_made, at(t, chunks, c + 1))
                    if c >= 2:
                        act.wait_ge(h_done, at(t, chunks, c - 1))
                    nc.scalar.activation(first[:, c % 2, :], g_bank[c % 2][:, :],
                                         ACT.Silu if gated else ACT.Copy).then_inc(first_done, 1)

        @block.vector
        def _(dve):
            n_vector(dve)
            r_vector(dve)
            dve.sem_inc(y_added, 1)
            with dve.Fori(0, GROUPS) as t:
                for c in range(chunks):
                    dve.wait_ge(first_done, at(t, chunks, c + 1))
                    source = first
                    if gated:
                        dve.wait_ge(u_made, at(t, chunks, c + 1))
                        out = partly if c < routed else h
                        last = nc.vector.tensor_tensor(out[:, c % 2, :], u_bank[c % 2][:, :], first[:, c % 2, :], ALU.mult)
                        source = partly
                    if c < routed:
                        dve.wait_ge(c_made, at(t, routed, c + 1))
                        if gated:
                            last.then_inc(partly_done, 1)
                            dve.wait_ge(partly_done, at(t, routed, c + 1))
                        last = nc.vector.tensor_tensor(h[:, c % 2, :], c_bank[c % 2][:, :], source[:, c % 2, :], ALU.mult)
                    last.then_inc(h_done, 1)
                dve.wait_ge(y_made, at(t, 1, 1))
                for j in range(G):
                    xj = core.x[:, bass.ds(t * G + j, 1), :].squeeze(1)
                    last = nc.vector.tensor_tensor(xj, y_bank[j // 2][:, (j % 2) * D:(j % 2 + 1) * D], xj, ALU.add)
                last.then_inc(y_added, 1)


def experts_0(core):
    experts(core, "L0f", 8, 2, "sigmoid", 14, 11, scale=2.5, floor=1e-20)


def experts_2(core):
    experts(core, "L2f", 8, 1, "softmax", 4, 4, gated=False, scale=4.0)


def experts_3(core):
    experts(core, "L3f", 16, 6, "softmax", 25, 22)


LOADS = {"L0f": ["L1a"], "L1f": ["L1f", "L2a"], "L2a": [], "L2x": ["L2f", "L3a", "L3f"], "L2f": [], "L3a": [],
         "L3x": ["L3sel"], "L3f": []}


def power_attention(core):
    nc, HQ, HK, OFFSET, EPS = core.nc, 16, 8, 6.906768, 1e-6
    SCALE = 1.0 / 128 ** 0.5
    w = core.weights("L1a")
    wq = w["q"].rearrange("p (k h n) -> p k h n", k=KD, h=HQ)
    wk = w["k"].rearrange("p (k h n) -> p k h n", k=KD, h=HK)
    wv = w["v"].rearrange("p (k h n) -> p k h n", k=KD, h=HK)
    wc = w["c"].rearrange("p (h n) -> p h n", h=HQ)
    with ExitStack() as ctx:
        sem = lambda n: core.sem(f"L1a_{n}", ctx)
        carve = core.work("L1a")
        s = norm_state(core, "L1a", carve, ctx)
        xcur = s["xn"].rearrange("p a d -> p (a d)").rearrange("p (k n) -> p k n", k=KD)
        qT, kT, v, a, z, decay = (carve(2, N) for _ in range(6))
        sq, spread_log, norm = carve(N), carve(N), carve(N)
        log_g, soft, cum_neg = carve(B, HK), carve(B, HK), carve(B, HK)
        q_bank, kv_bank, w_bank, s_bank, o_bank, n_bank = core.bank[0:6]
        y_bank = core.bank[6:8]
        causalT, ones = core.constant("causalT"), core.constant("ones")
        over_t = lambda m: m.unsqueeze(1).to_broadcast([P, G, P])
        quads = lambda m: m.rearrange("p (j t) -> p j t", j=G)

        g_made, z_done0, exp0_done, soft_done, log_done, cum_made, cum_done = (
            sem("g_made"), sem("gate_step"), sem("exp0_done"), sem("soft_done"), sem("log_done"), sem("cum_made"), sem("cum_done"))
        xcur_done, xcur_used = sem("xcur_done"), sem("xcur_used")
        spread_done, w_made, diff_done, capped, decay_done = (
            sem("spread_done"), sem("w_made"), sem("diff_done"), sem("capped"), sem("decay_done"))
        k_made, v_made, q_made, kT_done, v_done, qT_done = (
            sem("k_made"), sem("v_made"), sem("q_made"), sem("kT_done"), sem("v_done"), sem("qT_done"))
        scores_made, sq_done, a_done, o_made, norm_step, z_done = (
            sem("scores_made"), sem("sq_done"), sem("a_done"), sem("o_made"), sem("norm_step"), sem("z_done"))
        y_made, y_added, added = sem("y_made"), sem("y_added"), sem("added")
        block = ctx.enter_context(core.block())
        n_vector, n_gpsimd, n_tensor, n_scalar = normalise(core, "L1a", block, s)

        @block.sync
        def _(sp):
            core.load(sp, "L1x")

        @block.gpsimd
        def _(pool):
            n_gpsimd(pool)
            pool.wait_ge(log_done, 1)
            with pool.Fori(0, GROUPS) as t:
                pool.wait_ge(xcur_used, at(t, 1, 1))
                core.held(pool)
                nc.gpsimd.tensor_copy(xcur.rearrange("p k (b t) -> p k b t", b=G),
                                      core.xnT[:, :, bass.ds(t * G, G), :]).then_inc(xcur_done, 1)

                def spread_logs(i):
                    if i:
                        pool.wait_ge(w_made, at(t, HK, i))
                    nc.gpsimd.tensor_tensor(quads(spread_log), over_t(causalT),
                                            log_g[:, bass.ds(t * G, G), i:i + 1].to_broadcast([P, G, P]),
                                            ALU.mult).then_inc(spread_done, 1)

                for i in range(HK):
                    spread_logs(i)

        @block.tensor
        def _(pe):
            n_tensor(pe)
            pe.sem_inc(xcur_used, 1)
            pe.wait_ge(core.weights_loaded["L1a"], 16)
            pe.wait_ge(s["xnT_done"], B // 2)
            for b in range(B):
                for k in range(KD):
                    last = nc.tensor.matmul(q_bank[:, b * HK:(b + 1) * HK], core.xnT[:, k, b, :],
                                            w["g"][:, k * HK:(k + 1) * HK], start=(k == 0), stop=(k == KD - 1))
            last.then_inc(g_made, 1)
            pe.wait_ge(log_done, 1)
            nc.tensor.matmul(q_bank[:, 0:B * HK], causalT, log_g.rearrange("p b h -> p (b h)"),
                             start=True, stop=True).then_inc(cum_made, 1)
            pe.wait_ge(cum_done, 1)
            with pe.Fori(0, GROUPS) as t:
                pe.wait_ge(xcur_done, at(t, 1, 1))
                for step in range(HQ + 4):
                    i = step // 2
                    if step < HQ and step % 2 == 0:
                        if i:
                            pe.wait_ge(v_done, at(t, HK, i))
                        for k in range(KD):
                            last = nc.tensor.matmul(kv_bank[:, :], wk[:, k, i, :], xcur[:, k, :],
                                                    start=(k == 0), stop=(k == KD - 1))
                        last.then_inc(k_made, 1)
                    if 1 <= step <= HQ:
                        u = step - 1
                        pe.wait_ge(qT_done, at(t, HQ, u + 1))
                        pe.wait_ge(kT_done, at(t, HK, u // 2 + 1))
                        if u:
                            pe.wait_ge(sq_done, at(t, HQ, u))
                        for j in range(G):
                            last = nc.tensor.matmul(s_bank[:, j * P:(j + 1) * P], kT[:, u // 2 % 2, j * P:(j + 1) * P],
                                                    qT[:, u % 2, j * P:(j + 1) * P], start=True, stop=True)
                        last.then_inc(scores_made, 1)
                    if step < HQ:
                        u = step
                        if u:
                            pe.wait_ge(qT_done, at(t, HQ, u))
                        for k in range(KD):
                            last = nc.tensor.matmul(q_bank[:, :], wq[:, k, u, :], xcur[:, k, :],
                                                    start=(k == 0), stop=(k == KD - 1))
                        last.then_inc(q_made, 1)
                    if step < HQ and step % 2 == 0:
                        pe.wait_ge(spread_done, at(t, HK, i + 1))
                        if i:
                            pe.wait_ge(diff_done, at(t, HK, i))
                        nc.tensor.matmul(w_bank[:, :], ones, spread_log, start=True, stop=True).then_inc(w_made, 1)
                    if step < HQ and step % 2 == 1:
                        pe.wait_ge(kT_done, at(t, HK, i + 1))
                        for j in range(G):
                            for k in range(KD):
                                last = nc.tensor.matmul(kv_bank[:, j * P:(j + 1) * P], xcur[:, k, j * P:(j + 1) * P],
                                                        wv[:, k, i, :], start=(k == 0), stop=(k == KD - 1))
                        last.then_inc(v_made, 1)
                    if step == HQ - 1:
                        pe.wait_ge(v_made, at(t, HK, HK))
                        pe.sem_inc(xcur_used, 1)
                    if step >= 4:
                        u = step - 4
                        pe.wait_ge(z_done, at(t, HQ, u + 1))
                        if u == 0:
                            pe.wait_ge(y_added, at(t, 1, 1))
                        for j in range(G):
                            last = nc.tensor.matmul(y_bank[j // 2][:, (j % 2) * D:(j % 2 + 1) * D],
                                                    z[:, u % 2, j * P:(j + 1) * P], wc[:, u, :],
                                                    start=(u == 0 and j % 2 == 0), stop=(u == HQ - 1),
                                                    skip_group_check=True)
                        if u == HQ - 1:
                            last.then_inc(y_made, 1)
                    if 2 <= step <= HQ + 1:
                        u = step - 2
                        pe.wait_ge(a_done, at(t, HQ, u + 1))
                        pe.wait_ge(v_done, at(t, HK, u // 2 + 1))
                        if u:
                            pe.wait_ge(z_done, at(t, HQ, u))
                        for j in range(G):
                            nc.tensor.matmul(o_bank[:, j * P:(j + 1) * P], v[:, u // 2 % 2, j * P:(j + 1) * P],
                                             a[:, u % 2, j * P:(j + 1) * P], start=True, stop=True)
                        nc.tensor.matmul(n_bank[:, :], ones, a[:, u % 2, :], start=True, stop=True).then_inc(o_made, 1)

        @block.scalar
        def _(act):
            n_scalar(act)
            act.wait_ge(z_done0, 2)
            nc.scalar.activation(soft, soft, ACT.Exp).then_inc(exp0_done, 1)
            act.wait_ge(exp0_done, 1)
            nc.scalar.activation(soft, soft, ACT.Ln, bias=1.0).then_inc(soft_done, 1)
            with act.Fori(0, GROUPS) as t:
                for step in range(HQ + 1):
                    i = step // 2
                    if step < HQ and step % 2 == 0:
                        act.wait_ge(k_made, at(t, HK, i + 1))
                        nc.scalar.copy(kT[:, i % 2, :], kv_bank[:, :]).then_inc(kT_done, 1)
                    if 1 <= step <= HQ:
                        u = step - 1
                        act.wait_ge(scores_made, at(t, HQ, u + 1))
                        if u:
                            act.wait_ge(a_done, at(t, HQ, u))
                        nc.scalar.activation(sq, s_bank[:, :], ACT.Square, scale=SCALE).then_inc(sq_done, 1)
                    if step < HQ:
                        u = step
                        act.wait_ge(q_made, at(t, HQ, u + 1))
                        nc.scalar.copy(qT[:, u % 2, :], q_bank[:, :]).then_inc(qT_done, 1)
                    if step < HQ and step % 2 == 1:
                        act.wait_ge(v_made, at(t, HK, i + 1))
                        nc.scalar.copy(v[:, i % 2, :], kv_bank[:, :]).then_inc(v_done, 1)
                    if step < HQ and step % 2 == 0:
                        act.wait_ge(capped, at(t, HK, i + 1))
                        nc.scalar.activation(decay[:, i % 2, :], decay[:, i % 2, :], ACT.Exp).then_inc(decay_done, 1)

        @block.vector
        def _(dve):
            n_vector(dve)
            gates = q_bank[:, 0:B * HK].rearrange("p (b h) -> p b h", b=B)
            dve.wait_ge(g_made, 1)
            nc.vector.tensor_scalar(log_g, gates, OFFSET, None, ALU.add).then_inc(z_done0, 1)
            dve.wait_ge(z_done0, 1)
            nc.vector.scalar_tensor_tensor(out=soft, in0=log_g, scalar=-1.0, in1=log_g,
                                           op0=ALU.mult, op1=ALU.min).then_inc(z_done0, 1)
            dve.wait_ge(z_done0, 2)
            nc.vector.tensor_scalar(log_g, log_g, 0.0, None, ALU.min).then_inc(z_done0, 1)
            dve.wait_ge(z_done0, 3)
            dve.wait_ge(soft_done, 1)
            nc.vector.tensor_tensor(log_g, log_g, soft, ALU.subtract).then_inc(log_done, 1)
            dve.wait_ge(cum_made, 1)
            nc.vector.tensor_scalar(cum_neg, gates, -1.0, None, ALU.mult).then_inc(cum_done, 1)
            dve.wait_ge(cum_done, 1)
            dve.sem_inc(y_added, 1)
            with dve.Fori(0, GROUPS) as t:

                def normalise_head(u):
                    dve.wait_ge(o_made, at(t, HQ, u + 1))
                    nc.vector.tensor_scalar(norm, n_bank[:, :], EPS, None, ALU.add).then_inc(norm_step, 1)
                    dve.wait_ge(norm_step, at(t, 2 * HQ, 2 * u + 1))
                    nc.vector.reciprocal(norm, norm).then_inc(norm_step, 1)
                    dve.wait_ge(norm_step, at(t, 2 * HQ, 2 * u + 2))
                    nc.vector.tensor_tensor(z[:, u % 2, :], o_bank[:, :], norm, ALU.mult).then_inc(z_done, 1)

                for step in range(HQ + 2):
                    if step < HQ and step % 2 == 0:
                        i = step // 2
                        dve.wait_ge(w_made, at(t, HK, i + 1))
                        nc.vector.tensor_tensor(quads(decay[:, i % 2, :]), quads(w_bank[:, :]),
                                                cum_neg[:, bass.ds(t * G, G), i:i + 1].to_broadcast([P, G, P]),
                                                ALU.add).then_inc(diff_done, 1)
                        dve.wait_ge(diff_done, at(t, HK, i + 1))
                        nc.vector.tensor_tensor(quads(decay[:, i % 2, :]), quads(decay[:, i % 2, :]),
                                                over_t(core.constant("causal_cap")), ALU.min).then_inc(capped, 1)
                    if 1 <= step <= HQ:
                        u = step - 1
                        if u % 2 == 0:
                            dve.wait_ge(decay_done, at(t, HK, u // 2 + 1))
                        dve.wait_ge(sq_done, at(t, HQ, u + 1))
                        nc.vector.tensor_tensor(a[:, u % 2, :], sq, decay[:, u // 2 % 2, :], ALU.mult).then_inc(a_done, 1)
                    if step >= 2:
                        normalise_head(step - 2)
                dve.wait_ge(y_made, at(t, 1, 1))
                for j in range(G):
                    xj = core.x[:, bass.ds(t * G + j, 1), :].squeeze(1)
                    nc.vector.tensor_tensor(xj, y_bank[j // 2][:, (j % 2) * D:(j % 2 + 1) * D], xj, ALU.add).then_inc(added, 1)
                dve.wait_ge(added, at(t, G, G))
                xg = core.x[:, bass.ds(t * G, G), :]
                nc.vector.tensor_tensor(xg, xg, w["bc"].unsqueeze(1).to_broadcast([P, G, D]), ALU.add).then_inc(y_added, 1)


def context_features(core, pe, act, made, done, banks):
    nc = core.nc
    if pe is not None:
        pe.wait_ge(core.const_loaded, 16)
        pe.wait_ge(core.ctx_loaded, 16)
        for i in range(B // 2):
            if i >= 2:
                pe.wait_ge(done, i - 1)
            for k in range(KD):
                for b in (2 * i, 2 * i + 1):
                    last = nc.tensor.transpose(banks[i % 2][:, k * 256 + (b % 2) * P:k * 256 + (b % 2) * P + P],
                                               core.ctx_sb[:, b, k * P:(k + 1) * P], core.ident)
            last.then_inc(made, 1)
    else:
        for i in range(B // 2):
            act.wait_ge(made, i + 1)
            nc.scalar.activation(core.ctxT[:, :, 2 * i:2 * i + 2, :],
                                 banks[i % 2][:, :].rearrange("p (k b t) -> p k b t", k=KD, b=2),
                                 ACT.Copy).then_inc(done, 1)


def rotary_cross_attention(core):
    nc, EPS, HD = core.nc, 1e-6, 128
    w = core.weights("L1x")
    proj = {n: w[n].rearrange("p (k n) -> p k n", k=KD) for n in ("q", "k", "v", "kc", "vc")}
    wo = w["o"].rearrange("p (h n) -> p h n", h=16)
    KINDS = ["k", "kc", "q0", "v", "vc", "q1", "q2", "q3"]
    NP, NU = 2 * len(KINDS), 16
    ROPES = [n for n in range(NP) if KINDS[n % 8][0] != "v"]
    VALUES = [n for n in range(NP) if KINDS[n % 8][0] == "v"]
    NR, NV = len(ROPES), len(VALUES)
    LEAD, LAG_T, LAG_O, LAG_Y, LAG_X = 8, 2, 3, 4, 3
    STEPS = LEAD + NU + LAG_Y
    ready = {}
    for r, n in enumerate(ROPES):
        ready[(n // 8, KINDS[n % 8])] = r + 1
    with ExitStack() as ctx:
        sem = lambda n: core.sem(f"L1x_{n}", ctx)
        carve = core.work("L1x")
        s = norm_state(core, "L1x", carve, ctx)
        xcur = carve(KD, 2 * P)
        ccur = carve(KD, 2 * P)
        raw, cos_part, sin_part, turned_in = carve(2, 512), carve(2, 512), carve(2, 512), carve(2, 512)
        square = carve(512)
        sums = carve(2, 24)
        qT, kT, v = carve(2, 16, P), carve(2, 4, 2 * P), carve(2, 2, 512)
        sm, probs, pT, oT = s["xn"].rearrange("p (a b) d -> p a (b d)", a=2), carve(2, 512), carve(2, 512), carve(2, 256)
        peak, peak_neg, total = carve(2, 2), carve(2, 2), carve(2, 2)
        minus_one = carve(2)
        visible = carve(2, P)
        tables = {c: (carve(HD), carve(HD)) for c in "qk"}
        half = s["half"]
        p_bank, x_bank, s_bank, t_bank, o_bank, y_bank = (
            core.bank[0:2], core.bank[2], core.bank[3], core.bank[4], core.bank[5], core.bank[6:8])

        ctx_turned, ctxT_done = sem("ctx_turned"), sem("ctxT_done")
        tables_done, staged, staged_used = sem("tables_done"), sem("staged"), sem("staged_used")
        piece_made, raw_done, square_done, sums_done, factor_done = (
            sem("piece_made"), sem("raw_done"), sem("square_done"), sem("sums_done"), sem("factor_done"))
        reduced, parts_done, roped, rope_turned, rope_done, v_done = (
            sem("reduced"), sem("parts_done"), sem("roped"), sem("rope_turned"), sem("rope_done"), sem("v_done"))
        added = sem("pool_added")
        scores_made, masked, peak_done, exp_done, total_inv, p_done = (
            sem("scores_made"), sem("masked"), sem("peak_done"), sem("exp_done"), sem("total_inv"), sem("p_done"))
        p_turned, pT_done, o_made, oT_done, y_made, y_added = (
            sem("p_turned"), sem("pT_done"), sem("o_made"), sem("oT_done"), sem("y_made"), sem("y_added"))
        block = ctx.enter_context(core.block())
        n_vector, n_gpsimd, n_tensor, n_scalar = normalise(core, "L1x", block, s)
        heads = lambda a: a.rearrange("p (h d) -> p h d", h=4)
        over = lambda a: a.unsqueeze(1).to_broadcast([P, 4, a.shape[1]])

        @block.gpsimd
        def _(pool):
            nc.gpsimd.memset(minus_one, -1.0)
            n_gpsimd(pool)
            pool.wait_ge(ctxT_done, B // 2)
            with pool.Fori(0, B // 2) as t:
                pool.wait_ge(staged_used, at(t, 1, 1))
                core.held(pool)
                nc.gpsimd.tensor_copy(ccur.rearrange("p k (b t) -> p k b t", b=2), core.ctxT[:, :, bass.ds(t * 2, 2), :])
                pool.wait_ge(s["xnT_done"], at(t, 1, 1))
                core.held(pool)
                nc.gpsimd.tensor_copy(xcur.rearrange("p k (b t) -> p k b t", b=2),
                                      core.xnT[:, :, bass.ds(t * 2, 2), :]).then_inc(staged, 1)
                for step in range(LEAD + NU):
                    if step in ROPES:
                        r, i, kind, n = ROPES.index(step), step // 8, KINDS[step % 8], step
                        col = {"k": 0, "kc": 4}.get(kind, 8 + 4 * int(kind[1]) if kind[0] == "q" else 0)
                        factor = sums[:, i, col:col + 4]
                        pool.wait_ge(sums_done, at(t, NR, r + 1))
                        nc.gpsimd.tensor_tensor(factor, factor, half[:, 0:4], ALU.pow).then_inc(factor_done, 1)
                        pool.wait_ge(parts_done, at(t, NR, r + 1))
                        if r >= 2:
                            pool.wait_ge(rope_turned, at(t, NR, r - 1))
                        out, by = heads(turned_in[:, r % 2, :]), factor.unsqueeze(2).to_broadcast([P, 4, HD])
                        if kind == "kc":
                            pool.wait_ge(factor_done, at(t, NR, r + 1))
                            nc.gpsimd.tensor_tensor(out, heads(cos_part[:, r % 2, :]), by, ALU.mult).then_inc(roped, 1)
                        else:
                            last = nc.gpsimd.tensor_tensor(turned_in[:, r % 2, :], cos_part[:, r % 2, :],
                                                           sin_part[:, r % 2, :], ALU.add)
                            if kind == "k":
                                last.then_inc(added, 1)
                                pool.wait_ge(added, at(t, 2, i + 1))
                                pool.wait_ge(factor_done, at(t, NR, r + 1))
                                last = nc.gpsimd.tensor_tensor(out, out, by, ALU.mult)
                            last.then_inc(roped, 1)
                    if step >= LEAD:
                        u = step - LEAD
                        pool.wait_ge(exp_done, at(t, NU, u + 1))
                        nc.gpsimd.tensor_tensor(total[:, u % 2, :], total[:, u % 2, :], minus_one, ALU.pow).then_inc(total_inv, 1)
                        pool.wait_ge(total_inv, at(t, NU, u + 1))
                        p2 = probs[:, u % 2, :].rearrange("p (h d) -> p h d", h=2)
                        nc.gpsimd.tensor_tensor(p2, p2, total[:, u % 2, :].unsqueeze(2).to_broadcast([P, 2, 256]),
                                                ALU.mult).then_inc(p_done, 1)

        @block.tensor
        def _(pe):
            pe.sem_inc(staged_used, 1)
            context_features(core, pe, None, ctx_turned, ctxT_done, core.bank[2:4])
            n_tensor(pe)
            pe.wait_ge(s["xnT_done"], B // 2)
            pe.wait_ge(ctxT_done, B // 2)
            pe.wait_ge(core.weights_loaded["L1x"], 16)
            with pe.Fori(0, B // 2) as t:
                pe.wait_ge(staged, at(t, 1, 1))
                for step in range(STEPS):
                    if step < NP:
                        n, i, kind = step, step // 8, KINDS[step % 8]
                        src = ccur if kind[-1] == "c" else xcur
                        rhs = proj["q"][:, :, 512 * int(kind[1]):512 * int(kind[1]) + 512] if kind[0] == "q" else proj[kind]
                        if n >= 2:
                            pe.wait_ge(raw_done, at(t, NR, sum(m < n - 1 for m in ROPES)))
                            if any(m < n - 1 for m in VALUES):
                                pe.wait_ge(v_done, at(t, NV, sum(m < n - 1 for m in VALUES)))
                        for k in range(KD):
                            last = nc.tensor.matmul(p_bank[n % 2][:, :], src[:, k, i * P:(i + 1) * P], rhs[:, k, :],
                                                    start=(k == 0), stop=(k == KD - 1))
                        last.then_inc(piece_made, 1)
                        if n == NP - 1:
                            pe.wait_ge(piece_made, at(t, NP, NP))
                            pe.sem_inc(staged_used, 1)
                    if step - LAG_X in ROPES:
                        r = ROPES.index(step - LAG_X)
                        pe.wait_ge(roped, at(t, NR, r + 1))
                        if r:
                            pe.wait_ge(rope_done, at(t, NR, r))
                        for h in range(4):
                            last = nc.tensor.transpose(x_bank[:, h * P:(h + 1) * P],
                                                       turned_in[:, r % 2, h * P:(h + 1) * P], core.ident)
                        last.then_inc(rope_turned, 1)
                    if LEAD <= step < LEAD + NU:
                        u = step - LEAD
                        i, m = u // 8, u % 8
                        need = max(ready[(i, "k")], ready[(i, "kc")], ready[(i, f"q{m // 2}")])
                        pe.wait_ge(rope_done, at(t, NR, need))
                        if u:
                            pe.wait_ge(masked, at(t, NU, u))
                        for hh in range(2):
                            last = nc.tensor.matmul(s_bank[:, hh * 256:(hh + 1) * 256], qT[:, i, 2 * m + hh, :],
                                                    kT[:, i, m // 2, :], start=True, stop=True)
                        last.then_inc(scores_made, 1)
                    if LEAD + LAG_T <= step < LEAD + LAG_T + NU:
                        u = step - LEAD - LAG_T
                        pe.wait_ge(p_done, at(t, NU, u + 1))
                        if u:
                            pe.wait_ge(pT_done, at(t, NU, u))
                        for c in range(4):
                            last = nc.tensor.transpose(t_bank[:, c * P:(c + 1) * P], probs[:, u % 2, c * P:(c + 1) * P], core.ident)
                        last.then_inc(p_turned, 1)
                    if LEAD + LAG_O <= step < LEAD + LAG_O + NU:
                        u = step - LEAD - LAG_O
                        i, m = u // 8, u % 8
                        pe.wait_ge(pT_done, at(t, NU, u + 1))
                        pe.wait_ge(v_done, at(t, NV, 2 * i + 2))
                        if u:
                            pe.wait_ge(oT_done, at(t, NU, u))
                        for hh in range(2):
                            for c in range(2):
                                kv = m // 2
                                last = nc.tensor.matmul(o_bank[:, hh * P:(hh + 1) * P],
                                                        v[:, i, c, kv * HD:(kv + 1) * HD],
                                                        pT[:, u % 2, (2 * hh + c) * P:(2 * hh + c + 1) * P],
                                                        start=(c == 0), stop=(c == 1))
                        last.then_inc(o_made, 1)
                    if LEAD + LAG_Y <= step:
                        u = step - LEAD - LAG_Y
                        i, m = u // 8, u % 8
                        pe.wait_ge(oT_done, at(t, NU, u + 1))
                        if m == 0:
                            pe.wait_ge(y_added, at(t, 2, i + 1))
                        for hh in range(2):
                            last = nc.tensor.matmul(y_bank[i][:, 0:D], oT[:, u % 2, hh * P:(hh + 1) * P],
                                                    wo[:, 2 * m + hh, :], start=(m == 0 and hh == 0), stop=(m == 7 and hh == 1))
                        if m == 7:
                            last.then_inc(y_made, 1)

        @block.scalar
        def _(act):
            context_features(core, None, act, ctx_turned, ctxT_done, core.bank[2:4])
            n_scalar(act)
            with act.Fori(0, B // 2) as t:
                for step in range(LEAD + NU + LAG_O):
                    if step in ROPES:
                        n, r = step, ROPES.index(step)
                        act.wait_ge(piece_made, at(t, NP, n + 1))
                        if r >= 2:
                            act.wait_ge(parts_done, at(t, NR, r - 1))
                        nc.scalar.copy(raw[:, r % 2, :], p_bank[n % 2][:, :]).then_inc(raw_done, 1)
                        act.wait_ge(raw_done, at(t, NR, r + 1))
                        if r:
                            act.wait_ge(reduced, at(t, NR, r))
                        nc.scalar.activation(square, raw[:, r % 2, :], ACT.Square).then_inc(square_done, 1)
                    if step in VALUES:
                        n, i = step, step // 8
                        act.wait_ge(piece_made, at(t, NP, n + 1))
                        nc.scalar.copy(v[:, i, 0 if KINDS[n % 8] == "vc" else 1, :], p_bank[n % 2][:, :]).then_inc(v_done, 1)
                    if LEAD + LAG_T <= step < LEAD + LAG_T + NU:
                        u = step - LEAD - LAG_T
                        act.wait_ge(p_turned, at(t, NU, u + 1))
                        nc.scalar.copy(pT[:, u % 2, :], t_bank[:, :]).then_inc(pT_done, 1)
                    if LEAD <= step < LEAD + NU:
                        u = step - LEAD
                        i, m = u // 8, u % 8
                        act.wait_ge(peak_done, at(t, NU, u + 1))
                        if u >= 2:
                            act.wait_ge(p_turned, at(t, NU, u - 1))
                        for hh in range(2):
                            h = 2 * m + hh
                            last = nc.scalar.activation(probs[:, u % 2, hh * 256:(hh + 1) * 256], sm[:, u % 2, hh * 256:(hh + 1) * 256],
                                                        ACT.Exp, bias=peak_neg[:, u % 2, hh:hh + 1],
                                                        scale=sums[:, i, 8 + h:9 + h], accum_out=total[:, u % 2, hh:hh + 1])
                        last.then_inc(exp_done, 1)
                    if LEAD + LAG_O <= step:
                        u = step - LEAD - LAG_O
                        act.wait_ge(o_made, at(t, NU, u + 1))
                        nc.scalar.copy(oT[:, u % 2, :], o_bank[:, 0:256]).then_inc(oT_done, 1)

        @block.vector
        def _(dve):
            n_vector(dve)
            dve.wait_ge(core.weights_loaded["L1x"], 16)
            cos, sin = core.constant("cos1"), core.constant("sin1")
            for c, wn in (("q", w["qn"]), ("k", w["kn"])):
                cw, sw = tables[c]
                for lo in (0, 64):
                    nc.vector.tensor_tensor(cw[:, lo:lo + 64], cos, wn[:, lo:lo + 64], ALU.mult)
                nc.vector.scalar_tensor_tensor(out=sw[:, 0:64], in0=sin, scalar=-1.0, in1=wn[:, 64:128], op0=ALU.mult, op1=ALU.mult)
                nc.vector.tensor_tensor(sw[:, 64:128], sin, wn[:, 0:64], ALU.mult)
            nc.vector.memset(visible[:, 0, :], 0.0)
            nc.vector.tensor_copy(visible[:, 1, :], core.constant("causal_bias")).then_inc(tables_done, 1)
            dve.wait_ge(tables_done, 1)
            dve.sem_inc(y_added, 2)
            with dve.Fori(0, B // 2) as t:

                def add_to_x(i):
                    dve.wait_ge(y_made, at(t, 2, i + 1))
                    xb = core.x[:, bass.ds(2 * t + i, 1), :].squeeze(1)
                    nc.vector.tensor_tensor(xb, y_bank[i][:, 0:D], xb, ALU.add).then_inc(y_added, 1)

                for step in range(LEAD + NU):
                    if step - LAG_X in ROPES:
                        n = step - LAG_X
                        r, i, kind = ROPES.index(n), n // 8, KINDS[n % 8]
                        dve.wait_ge(rope_turned, at(t, NR, r + 1))
                        if kind[0] == "q":
                            out = qT[:, i, 4 * int(kind[1]):4 * int(kind[1]) + 4, :]
                        else:
                            own = 0 if kind == "kc" else P
                            out = kT[:, i, :, own:own + P]
                        nc.vector.tensor_copy(out, heads(x_bank[:, :])).then_inc(rope_done, 1)
                    if LEAD <= step:
                        u = step - LEAD
                        i, m = u // 8, u % 8
                        dve.wait_ge(scores_made, at(t, NU, u + 1))
                        if u >= 2:
                            dve.wait_ge(exp_done, at(t, NU, u - 1))
                        dve.wait_ge(factor_done, at(t, NR, ready[(i, f"q{m // 2}")]))
                        core.held(dve)
                        for hh in range(2):
                            last = nc.vector.tensor_tensor_reduce(
                                out=sm[:, u % 2, hh * 256:(hh + 1) * 256], in0=s_bank[:, hh * 256:(hh + 1) * 256],
                                in1=visible.rearrange("p a b -> p (a b)"), scale=1.0, scalar=-3e38, op0=ALU.add, op1=ALU.max,
                                accum_out=peak[:, u % 2, hh:hh + 1])
                        last.then_inc(masked, 1)
                        dve.wait_ge(masked, at(t, NU, u + 1))
                        nc.vector.scalar_tensor_tensor(out=peak_neg[:, u % 2, :], in0=peak[:, u % 2, :], scalar=-1.0,
                                                       in1=sums[:, i, 8 + 2 * m:10 + 2 * m], op0=ALU.mult,
                                                       op1=ALU.mult).then_inc(peak_done, 1)
                    if step in ROPES:
                        r, i, kind = ROPES.index(step), step // 8, KINDS[step % 8]
                        col = {"k": 0, "kc": 4}.get(kind, 8 + 4 * int(kind[1]) if kind[0] == "q" else 0)
                        into = sums[:, i, col:col + 4]
                        cw, sw = tables[kind[0]]
                        dve.wait_ge(raw_done, at(t, NR, r + 1))
                        if r >= 2:
                            dve.wait_ge(roped, at(t, NR, r - 1))
                        part, src = heads(cos_part[:, r % 2, :]), heads(raw[:, r % 2, :])
                        if kind == "kc":
                            last = nc.vector.tensor_tensor(part, src, over(w["kn"]), ALU.mult)
                        else:
                            nc.vector.tensor_tensor(part, src, over(cw), ALU.mult)
                            part = heads(sin_part[:, r % 2, :])
                            nc.vector.tensor_tensor(part[:, :, 0:64], src[:, :, 64:128], over(sw[:, 0:64]), ALU.mult)
                            last = nc.vector.tensor_tensor(part[:, :, 64:128], src[:, :, 0:64], over(sw[:, 64:128]), ALU.mult)
                        last.then_inc(parts_done, 1)
                        dve.wait_ge(square_done, at(t, NR, r + 1))
                        nc.vector.tensor_reduce(into, heads(square), AX, ALU.add).then_inc(reduced, 1)
                        dve.wait_ge(reduced, at(t, NR, r + 1))
                        if kind[0] == "k":
                            nc.vector.tensor_scalar(into, into, 1.0 / HD, EPS, ALU.mult, ALU.add).then_inc(sums_done, 1)
                        else:
                            nc.vector.tensor_scalar(into, into, HD * EPS, None, ALU.add).then_inc(sums_done, 1)
                    if step == LEAD + 8 + LAG_Y:
                        add_to_x(0)
                add_to_x(1)


def sink_attention(core):
    nc, HD = core.nc, 64
    w = core.weights("L2a")
    proj = {n: w[n].rearrange("p (k n) -> p k n", k=KD) for n in "qkv"}
    wo = w["o"].rearrange("p (m n) -> p m n", m=16)
    KINDS = ["k", "v", "q0", "q1", "q2", "q3"]
    NK = len(KINDS)
    NP, NU = 2 * NK, 8
    ROPES = [n for n in range(NP) if KINDS[n % NK] != "v"]
    NR = len(ROPES)
    LAG_X = 3
    SLOT = [6, 7, 9, 10, 12, 13, 14, 15, 16, 17, 18, 19]
    LAG_T, LAG_O, LAG_Y = 2, 3, 4
    STEPS = 20
    SM = 3
    with ExitStack() as ctx:
        sem = lambda n: core.sem(f"L2a_{n}", ctx)
        carve = core.work("L2a")
        s = norm_state(core, "L2a", carve, ctx)
        xcur = s["xn"].rearrange("p a d -> p (a d)").rearrange("p (k t) -> p k t", k=KD)[:, :, 0:2 * P]
        xcur = carve(KD, 2 * P)
        raw, cos_part, sin_part, turned_in = (carve(2, 512) for _ in range(4))
        qT, kT, v = carve(2, 16, P), carve(2, 4, P), carve(2, 512)
        sm, pT, oT = carve(SM, 2, 512), carve(2, 512), carve(2, 512)
        peak, sinks, sink_part, total = carve(2, 8), carve(32), carve(2, 8), carve(2, 8)
        p_bank, x_bank, s_bank, t_bank, o_bank, y_bank = (
            core.bank[0], core.bank[1], core.bank[2:4], core.bank[4:6], core.bank[6], core.bank[7])

        piece_bank = lambda n: t_bank[1] if n % 2 == 1 and n < SLOT[LAG_T] else p_bank

        staged, staged_used, sinks_done = sem("staged"), sem("staged_used"), sem("sinks_done")
        piece_made, piece_done, parts_done, roped = sem("piece_made"), sem("piece_done"), sem("parts_done"), sem("roped")
        rope_turned, rope_done = sem("rope_turned"), sem("rope_done")
        scores_made, peaks, peak_done, moved = sem("scores_made"), sem("peaks"), sem("peak_done"), sem("moved")
        exp_done, summed, total_done, total_inv, p_done = (
            sem("exp_done"), sem("summed"), sem("total_done"), sem("total_inv"), sem("p_done"))
        p_turned, pT_done, o_made, oT_done, y_made, y_read, y_added = (
            sem("p_turned"), sem("pT_done"), sem("o_made"), sem("oT_done"), sem("y_made"), sem("y_read"), sem("y_added"))
        block = ctx.enter_context(core.block())
        n_vector, n_gpsimd, n_tensor, n_scalar = normalise(core, "L2a", block, s)
        fours = lambda a: a.rearrange("p (m d) -> p m d", m=4)

        @block.sync
        def _(sp):
            for what in LOADS["L2a"]:
                core.load(sp, what)

        @block.gpsimd
        def _(pool):
            n_gpsimd(pool)
            with pool.Fori(0, B // 2) as t:
                pool.wait_ge(staged_used, at(t, 1, 1))
                pool.wait_ge(s["xnT_done"], at(t, 1, 1))
                core.held(pool)
                nc.gpsimd.tensor_copy(xcur.rearrange("p k (b t) -> p k b t", b=2),
                                      core.xnT[:, :, bass.ds(t * 2, 2), :]).then_inc(staged, 1)
                for step in range(STEPS):
                    if step in ROPES:
                        r = ROPES.index(step)
                        pool.wait_ge(parts_done, at(t, NR, r + 1))
                        if r >= 2:
                            pool.wait_ge(rope_turned, at(t, NR, r - 1))
                        nc.gpsimd.tensor_tensor(turned_in[:, r % 2, :], cos_part[:, r % 2, :], sin_part[:, r % 2, :],
                                                ALU.add).then_inc(roped, 1)
                    if step in SLOT[:NU]:
                        u = SLOT.index(step)
                        pool.wait_ge(total_inv, at(t, NU, u + 1))
                        p8 = sm[:, u % SM, :, :].rearrange("p e (m d) -> p (e m) d", m=4)
                        nc.gpsimd.tensor_tensor(p8, p8, total[:, u % 2, :].unsqueeze(2).to_broadcast([P, 8, P]),
                                                ALU.mult).then_inc(p_done, 1)

        @block.tensor
        def _(pe):
            pe.sem_inc(staged_used, 1)
            n_tensor(pe)
            pe.wait_ge(s["xnT_done"], B // 2)
            pe.wait_ge(core.weights_loaded["L2a"], 16)
            with pe.Fori(0, B // 2) as t:
                pe.wait_ge(staged, at(t, 1, 1))
                for step in range(STEPS):
                    if step < NP:
                        n, i, kind = step, step // NK, KINDS[step % NK]
                        rhs = proj["q"][:, :, 512 * int(kind[1]):512 * int(kind[1]) + 512] if kind[0] == "q" else proj[kind]
                        if n >= SLOT[LAG_T]:
                            pe.wait_ge(piece_done, at(t, NP, n))
                        elif n >= 2:
                            pe.wait_ge(piece_done, at(t, NP, n - 1))
                        for k in range(KD):
                            last = nc.tensor.matmul(piece_bank(n)[:, :], xcur[:, k, i * P:(i + 1) * P], rhs[:, k, :],
                                                    start=(k == 0), stop=(k == KD - 1))
                        last.then_inc(piece_made, 1)
                        if n == NP - 1:
                            pe.wait_ge(piece_made, at(t, NP, NP))
                            pe.sem_inc(staged_used, 1)
                    if step - LAG_X in ROPES:
                        r = ROPES.index(step - LAG_X)
                        pe.wait_ge(roped, at(t, NR, r + 1))
                        if r:
                            pe.wait_ge(rope_done, at(t, NR, r))
                        for h in range(4):
                            last = nc.tensor.transpose(x_bank[:, h * P:(h + 1) * P],
                                                       turned_in[:, r % 2, h * P:(h + 1) * P], core.ident)
                        last.then_inc(rope_turned, 1)
                    if step in SLOT[:NU]:
                        u = SLOT.index(step)
                        i, a = u // 4, u % 4
                        pe.wait_ge(rope_done, at(t, NR, ROPES.index(NK * i + 2 + a) + 1))
                        if u:
                            pe.wait_ge(moved, at(t, NU, u))
                        for m in range(4):
                            for e in range(2):
                                last = nc.tensor.matmul(s_bank[e][:, m * P:(m + 1) * P],
                                                        qT[e * HD:(e + 1) * HD, i, 4 * a + m, :],
                                                        kT[e * HD:(e + 1) * HD, i, a, :], start=True, stop=True)
                        last.then_inc(scores_made, 1)
                    if step in SLOT[LAG_T:LAG_T + NU]:
                        u = SLOT.index(step) - LAG_T
                        pe.wait_ge(p_done, at(t, NU, u + 1))
                        if u:
                            pe.wait_ge(pT_done, at(t, NU, u))
                        for e in range(2):
                            for m in range(4):
                                last = nc.tensor.transpose(t_bank[e][:, m * P:(m + 1) * P],
                                                           sm[:, u % SM, e, m * P:(m + 1) * P], core.ident)
                        last.then_inc(p_turned, 1)
                    if step in SLOT[LAG_O:LAG_O + NU]:
                        u = SLOT.index(step) - LAG_O
                        i, a = u // 4, u % 4
                        pe.wait_ge(pT_done, at(t, NU, u + 1))
                        if u:
                            pe.wait_ge(oT_done, at(t, NU, u))
                        for e in range(2):
                            kv = 2 * a + e
                            last = nc.tensor.matmul(o_bank[e * HD:(e + 1) * HD, :], v[:, i, kv * HD:(kv + 1) * HD],
                                                    pT[:, e, :], start=True, stop=True)
                        last.then_inc(o_made, 1)
                    if step in SLOT[LAG_Y:]:
                        u = SLOT.index(step) - LAG_Y
                        i, a = u // 4, u % 4
                        pe.wait_ge(oT_done, at(t, NU, u + 1))
                        if a == 0:
                            pe.wait_ge(y_read, at(t, 2, i + 1))
                        for m in range(4):
                            last = nc.tensor.matmul(y_bank[:, 0:D], oT[:, u % 2, m * P:(m + 1) * P], wo[:, 4 * a + m, :],
                                                    start=(a == 0 and m == 0), stop=(a == 3 and m == 3))
                        if a == 3:
                            last.then_inc(y_made, 1)

        @block.scalar
        def _(act):
            n_scalar(act)
            with act.Fori(0, B // 2) as t:
                for step in range(STEPS):
                    if step in SLOT[LAG_T:LAG_T + NU]:
                        u = SLOT.index(step) - LAG_T
                        act.wait_ge(p_turned, at(t, NU, u + 1))
                        if u:
                            act.wait_ge(o_made, at(t, NU, u))
                        for e in range(2):
                            last = nc.scalar.copy(pT[:, e, :], t_bank[e][:, :])
                        last.then_inc(pT_done, 1)
                    if step - LAG_X in ROPES:
                        n = step - LAG_X
                        r, i, kind = ROPES.index(n), n // NK, KINDS[n % NK]
                        act.wait_ge(rope_turned, at(t, NR, r + 1))
                        out = qT[:, i, 4 * int(kind[1]):4 * int(kind[1]) + 4, :] if kind[0] == "q" else kT[:, i, :, :]
                        nc.scalar.copy(out, fours(x_bank[:, :])).then_inc(rope_done, 1)
                    if step in SLOT[:NU]:
                        u = SLOT.index(step)
                        act.wait_ge(moved, at(t, NU, u + 1))
                        nc.scalar.activation(sink_part[:, u % 2, :], sink_part[:, u % 2, :], ACT.Exp, scale=0.125)
                        nc.scalar.activation(sm[:, u % SM, :, :], sm[:, u % SM, :, :], ACT.Exp, scale=0.125).then_inc(exp_done, 1)
                    if step in SLOT[LAG_O:LAG_O + NU]:
                        u = SLOT.index(step) - LAG_O
                        act.wait_ge(o_made, at(t, NU, u + 1))
                        nc.scalar.copy(oT[:, u % 2, :], o_bank[:, :]).then_inc(oT_done, 1)

        @block.vector
        def _(dve):
            n_vector(dve)
            dve.wait_ge(core.weights_loaded["L2a"], 16)
            nc.vector.tensor_scalar(sinks, w["sinks"], 8.0, None, ALU.mult).then_inc(sinks_done, 1)
            dve.wait_ge(sinks_done, 1)
            dve.sem_inc(y_read, 1)
            eights = lambda a: a.rearrange("p (h d) -> p h d", h=8)
            with dve.Fori(0, B // 2) as t:

                def add_to_x(i):
                    dve.wait_ge(y_made, at(t, 2, i + 1))
                    xb = core.x[:, bass.ds(2 * t + i, 1), :].squeeze(1)
                    nc.vector.tensor_tensor(xb, y_bank[:, 0:D], xb, ALU.add).then_inc(y_read, 1)
                    dve.wait_ge(y_read, at(t, 2, i + 2))
                    nc.vector.tensor_tensor(xb, xb, w["bo"], ALU.add).then_inc(y_added, 1)

                def invert_total(t, u):
                    dve.wait_ge(exp_done, at(t, NU, u + 1))
                    nc.vector.tensor_reduce(total[:, u % 2, :], sm[:, u % SM, :, :].rearrange("p e (m d) -> p (e m) d", m=4),
                                            AX, ALU.add).then_inc(summed, 1)
                    dve.wait_ge(summed, at(t, NU, u + 1))
                    nc.vector.tensor_tensor(total[:, u % 2, :], total[:, u % 2, :], sink_part[:, u % 2, :],
                                            ALU.add).then_inc(total_done, 1)
                    dve.wait_ge(total_done, at(t, NU, u + 1))
                    nc.vector.reciprocal(total[:, u % 2, :], total[:, u % 2, :]).then_inc(total_inv, 1)

                for step in range(STEPS):
                    if step < NP:
                        n, i, kind = step, step // NK, KINDS[step % NK]
                        dve.wait_ge(piece_made, at(t, NP, n + 1))
                        if kind == "v":
                            nc.vector.tensor_tensor(v[:, i, :], piece_bank(n)[:, :], w["bv"], ALU.add).then_inc(piece_done, 1)
                        else:
                            r = ROPES.index(n)
                            bias = w["bk"] if kind == "k" else w["bq"][:, 512 * int(kind[1]):512 * int(kind[1]) + 512]
                            nc.vector.tensor_tensor(raw[:, r % 2, :], piece_bank(n)[:, :], bias, ALU.add).then_inc(piece_done, 1)
                            dve.wait_ge(piece_done, at(t, NP, n + 1))
                            if r >= 2:
                                dve.wait_ge(roped, at(t, NR, r - 1))
                            cos = core.constant("cos2").unsqueeze(1)
                            sin = core.constant("sin2").unsqueeze(1)
                            halves = raw[:, r % 2, :].rearrange("p (a d) -> p a d", a=16)
                            nc.vector.tensor_tensor(cos_part[:, r % 2, :].rearrange("p (a d) -> p a d", a=16), halves,
                                                    cos.to_broadcast([P, 16, 32]), ALU.mult)
                            out, src = eights(sin_part[:, r % 2, :]), eights(raw[:, r % 2, :])
                            nc.vector.scalar_tensor_tensor(out=out[:, :, 0:32], in0=src[:, :, 32:64], scalar=-1.0,
                                                           in1=sin.to_broadcast([P, 8, 32]), op0=ALU.mult, op1=ALU.mult)
                            nc.vector.tensor_tensor(out[:, :, 32:64], src[:, :, 0:32], sin.to_broadcast([P, 8, 32]),
                                                    ALU.mult).then_inc(parts_done, 1)
                    if step in SLOT[1:NU + 1]:
                        invert_total(t, SLOT.index(step) - 1)
                    if step in SLOT[:NU]:
                        u = SLOT.index(step)
                        a = u % 4
                        dve.wait_ge(scores_made, at(t, NU, u + 1))
                        for e in range(2):
                            last = nc.vector.tensor_reduce(peak[:, u % 2, 4 * e:4 * e + 4], fours(s_bank[e][:, :]), AX, ALU.max)
                        last.then_inc(peaks, 1)
                        dve.wait_ge(peaks, at(t, NU, u + 1))
                        sink = sinks[:, 8 * a:8 * a + 8]
                        nc.vector.tensor_tensor(peak[:, u % 2, :], peak[:, u % 2, :], sink, ALU.max).then_inc(peak_done, 1)
                        dve.wait_ge(peak_done, at(t, NU, u + 1))
                        if u >= SM:
                            dve.wait_ge(p_turned, at(t, NU, u - SM + 1))
                        nc.vector.tensor_tensor(sink_part[:, u % 2, :], sink, peak[:, u % 2, :], ALU.subtract)
                        for e in range(2):
                            last = nc.vector.tensor_tensor(fours(sm[:, u % SM, e, :]), fours(s_bank[e][:, :]),
                                                           peak[:, u % 2, 4 * e:4 * e + 4].unsqueeze(2).to_broadcast([P, 4, P]),
                                                           ALU.subtract)
                        last.then_inc(moved, 1)
                    if step == SLOT[3 + LAG_Y]:
                        add_to_x(0)
                add_to_x(1)


def lora_experts(core):
    nc, CH, R = core.nc, 6, 72
    w = core.weights("L1f")
    wg, wu = (w[n].rearrange("p (k f) -> p k f", k=KD) for n in ("gate", "up"))
    ag, au = (w[n].rearrange("p (k f) -> p k f", k=KD) for n in ("a_gate", "a_up"))
    wd = w["down"].rearrange("p (c d) -> p c d", c=CH)
    ad = w["a_down"].rearrange("p (c r) -> p c r", c=CH)
    with ExitStack() as ctx:
        sem = lambda n: core.sem(f"L1f_{n}", ctx)
        carve = core.work("L1f")
        s = norm_state(core, "L1f", carve, ctx)
        scratch = carve(2 * B * 64)
        shareT, shareT_done, (r_vector, r_tensor, r_scalar) = router(
            core, "L1f", 8, 2, "sigmoid", s, w["router"], carve, scratch, ctx, bias=w["bias"], scale=0.125,
            floor=1e-8, ones=1)
        factor, low_gate, low_up, low_down = carve(N), carve(N), carve(N), carve(N)
        silu, h = carve(2, N), carve(CH, N)
        g_bank, u_bank, a_bank, b_bank, y_bank = core.bank[0:2], core.bank[2:4], core.bank[4], core.bank[5], core.bank[6:8]
        low_made, factor_made, down_made = sem("low_made"), sem("factor_made"), sem("down_made")
        factor_done, low_done, low_down_done = sem("factor_done"), sem("low_done"), sem("low_down_done")
        g_made, u_made, silu_done, h_done = sem("g_made"), sem("u_made"), sem("silu_done"), sem("h_done")
        y_made, y_added = sem("y_made"), sem("y_added")
        block = ctx.enter_context(core.block())
        n_vector, n_gpsimd, n_tensor, n_scalar = normalise(core, "L1f", block, s)

        @block.sync
        def _(sp):
            for what in LOADS["L1f"]:
                core.load(sp, what)

        @block.gpsimd
        def _(pool):
            n_gpsimd(pool)

        @block.tensor
        def _(pe):
            r_tensor(pe, n_tensor)
            pe.wait_ge(shareT_done, B // 4)
            with pe.Fori(0, GROUPS) as t:
                xg = core.xnT[:, :, bass.ds(t * G, G), :]
                pe.wait_ge(y_added, at(t, 1, 1))
                nc.tensor.matmul(g_bank[1][0:R, :], w["select"][0:9, :], shareT[0:9, bass.ds(t * N, N)],
                                 start=True, stop=True).then_inc(factor_made, 1)
                for wa, bank in ((ag, a_bank), (au, b_bank)):
                    for k in range(KD):
                        last = nc.tensor.matmul(bank[0:R, :], wa[:, k, :], core.xnT[:, k, bass.ds(t * G, G), :],
                                                start=(k == 0), stop=(k == KD - 1))
                last.then_inc(low_made, 1)
                for step in range(CH + 1):
                    if step < CH:
                        c = step
                        if c == 1:
                            pe.wait_ge(factor_done, at(t, 1, 1))
                        if c >= 2:
                            pe.wait_ge(h_done, at(t, CH, c - 1))
                        for wt, bank in ((wg, g_bank), (wu, u_bank)):
                            for k in range(KD):
                                nc.tensor.matmul(bank[c % 2][:, :], wt[:, k, c * P:(c + 1) * P],
                                                 core.xnT[:, k, bass.ds(t * G, G), :], start=(k == 0), stop=False)
                        pe.wait_ge(low_done, at(t, 1, 1))
                        nc.tensor.matmul(g_bank[c % 2][:, :], w["b_gate"][0:R, c * P:(c + 1) * P], low_gate[0:R, :],
                                         start=False, stop=True).then_inc(g_made, 1)
                        nc.tensor.matmul(u_bank[c % 2][:, :], w["b_up"][0:R, c * P:(c + 1) * P], low_up[0:R, :],
                                         start=False, stop=True).then_inc(u_made, 1)
                    if step >= 1:
                        c = step - 1
                        pe.wait_ge(h_done, at(t, CH, c + 1))
                        last = nc.tensor.matmul(a_bank[0:R, :], ad[:, c, :], h[:, c, :], start=(c == 0), stop=(c == CH - 1))
                        if c == CH - 1:
                            last.then_inc(down_made, 1)
                        for j in range(G):
                            nc.tensor.matmul(y_bank[j // 2][:, (j % 2) * D:(j % 2 + 1) * D], h[:, c, j * P:(j + 1) * P],
                                             wd[:, c, :], start=(c == 0 and j % 2 == 0), stop=False, skip_group_check=True)
                pe.wait_ge(low_down_done, at(t, 1, 1))
                for j in range(G):
                    last = nc.tensor.matmul(y_bank[j // 2][:, (j % 2) * D:(j % 2 + 1) * D], low_down[0:R, j * P:(j + 1) * P],
                                            w["b_down"][0:R, :], start=False, stop=True, skip_group_check=True)
                last.then_inc(y_made, 1)

        @block.scalar
        def _(act):
            n_scalar(act)
            r_scalar(act)
            act.wait_ge(shareT_done, B // 4)
            with act.Fori(0, GROUPS) as t:
                act.wait_ge(factor_made, at(t, 1, 1))
                nc.scalar.copy(factor[0:R, :], g_bank[1][0:R, :]).then_inc(factor_done, 1)
                for c in range(CH):
                    act.wait_ge(g_made, at(t, CH, c + 1))
                    nc.scalar.activation(silu[:, c % 2, :], g_bank[c % 2][:, :], ACT.Silu).then_inc(silu_done, 1)

        @block.vector
        def _(dve):
            n_vector(dve)
            r_vector(dve)
            dve.sem_inc(y_added, 1)
            with dve.Fori(0, GROUPS) as t:
                dve.wait_ge(factor_done, at(t, 1, 1))
                dve.wait_ge(low_made, at(t, 1, 1))
                nc.vector.tensor_tensor(low_gate[0:R, :], a_bank[0:R, :], factor[0:R, :], ALU.mult)
                nc.vector.tensor_tensor(low_up[0:R, :], b_bank[0:R, :], factor[0:R, :], ALU.mult).then_inc(low_done, 1)
                for c in range(CH):
                    dve.wait_ge(silu_done, at(t, CH, c + 1))
                    dve.wait_ge(u_made, at(t, CH, c + 1))
                    nc.vector.tensor_tensor(h[:, c, :], u_bank[c % 2][:, :], silu[:, c % 2, :], ALU.mult).then_inc(h_done, 1)
                dve.wait_ge(down_made, at(t, 1, 1))
                nc.vector.tensor_tensor(low_down[0:R, :], a_bank[0:R, :], factor[0:R, :], ALU.mult).then_inc(low_down_done, 1)
                dve.wait_ge(y_made, at(t, 1, 1))
                for j in range(G):
                    xj = core.x[:, bass.ds(t * G + j, 1), :].squeeze(1)
                    last = nc.vector.tensor_tensor(xj, y_bank[j // 2][:, (j % 2) * D:(j % 2 + 1) * D], xj, ALU.add)
                last.then_inc(y_added, 1)



def token_attention(core, name):
    nc = core.nc
    own = name == "L3a"
    SCALE = 1.0 / float(np.sqrt(32)) if own else 1.0 / 16
    w = core.weights(name)
    with ExitStack() as ctx:
        sem = lambda n: core.sem(f"{name}_{n}", ctx)
        carve = core.work(name)
        s = norm_state(core, name, carve, ctx)
        xcur = carve(2, KD, N) if not own else carve(2, KD, N)
        sm, pT = carve(2, N), carve(2, N)
        peak, total = carve(2, G), carve(2, G)
        s_bank, v_bank, t_bank, y_bank = core.bank[0:2], core.bank[2:4], core.bank[4:6], core.bank[6:8]
        if own:
            state, action, values = carve(2, N), carve(2, N), carve(2, G * D)
        else:
            mask = carve(B * P // 4)
            keep, fill, valid = carve(B, P), carve(B, P), carve(B)
        mask_loaded, keep_done, staged, staged_used = sem("mask_loaded"), sem("keep_done"), sem("staged"), sem("staged_used")
        sa_made, sa_done, v_made, v_done = sem("sa_made"), sem("sa_done"), sem("v_made"), sem("v_done")
        scores_made, masked, filled, peak_done, moved, exp_done = (
            sem("scores_made"), sem("masked"), sem("filled"), sem("peak_done"), sem("moved"), sem("exp_done"))
        total_step, p_done, p_turned, pT_done, y_made, y_added, b_added = (
            sem("total_step"), sem("p_done"), sem("p_turned"), sem("pT_done"), sem("y_made"), sem("y_added"), sem("b_added"))
        block = ctx.enter_context(core.block())
        n_vector, n_gpsimd, n_tensor, n_scalar = normalise(core, name, block, s)
        quads = lambda a: a.rearrange("p (j d) -> p j d", j=G)
        TURNS = GROUPS // 2

        @block.sync
        def _(sp):
            if not own:
                sp.dma_start(mask.bitcast(U8), core.dram["memory_mask"].to_broadcast([P, B * P])).then_inc(mask_loaded, 16)
            for what in LOADS[name]:
                core.load(sp, what)

        @block.gpsimd
        def _(pool):
            n_gpsimd(pool)
            with pool.Fori(0, TURNS) as t:
                for g in range(2):
                    pool.wait_ge(staged_used, at(t, 2, g + 1))
                    pool.wait_ge(s["xnT_done"], at(t, 4, 2 * g + 2))
                    core.held(pool)
                    nc.gpsimd.tensor_copy(xcur[:, g, :, :].rearrange("p k (b t) -> p k b t", b=G),
                                          core.xnT[:, :, bass.ds(t * 2 * G + g * G, G), :]).then_inc(staged, 1)

        @block.tensor
        def _(pe):
            pe.sem_inc(staged_used, 2)
            n_tensor(pe)
            pe.wait_ge(s["xnT_done"], B // 2)
            if own:
                pe.wait_ge(core.weights_loaded[name], 16)
            with pe.Fori(0, TURNS) as t:
                for g in range(2):
                    pe.wait_ge(staged, at(t, 2, g + 1))
                    pe.wait_ge(y_added, at(t, 2, g + 1))
                    if own:
                        for wn, bank in (("s", t_bank[g]), ("a", y_bank[g])):
                            for k in range(KD):
                                last = nc.tensor.matmul(bank[0:32, :], w[wn][:, k * 32:(k + 1) * 32], xcur[:, g, k, :],
                                                        start=(k == 0), stop=(k == KD - 1))
                        last.then_inc(sa_made, 1)
                for g in range(2):
                    if own:
                        for j in range(G):
                            if j == 2 or (j == 0 and g):
                                pe.wait_ge(v_done, at(t, 4, 2 * g + j // 2))
                            for k in range(KD):
                                last = nc.tensor.matmul(v_bank[j // 2][:, (j % 2) * D:(j % 2 + 1) * D],
                                                        xcur[:, g, k, j * P:(j + 1) * P], w["o"][:, k * D:(k + 1) * D],
                                                        start=(k == 0), stop=(k == KD - 1))
                            if j % 2:
                                last.then_inc(v_made, 1)
                        pe.wait_ge(sa_done, at(t, 2, g + 1))
                    for j in range(G):
                        if own:
                            last = nc.tensor.matmul(s_bank[g][:, j * P:(j + 1) * P], state[0:32, g, j * P:(j + 1) * P],
                                                    action[0:32, g, j * P:(j + 1) * P], start=True, stop=True)
                        else:
                            for k in range(KD):
                                last = nc.tensor.matmul(s_bank[g][:, j * P:(j + 1) * P], xcur[:, g, k, j * P:(j + 1) * P],
                                                        core.ctxT[:, k, bass.ds(t * 2 * G + g * G + j, 1), :].squeeze(1),
                                                        start=(k == 0), stop=(k == KD - 1))
                    last.then_inc(scores_made, 1)
                    pe.wait_ge(scores_made, at(t, 2, g + 1))
                    pe.sem_inc(staged_used, 1)
                for g in range(2):
                    pe.wait_ge(p_done, at(t, 2, g + 1))
                    for j in range(G):
                        last = nc.tensor.transpose(t_bank[g][:, j * P:(j + 1) * P], sm[:, g, j * P:(j + 1) * P], core.ident)
                    last.then_inc(p_turned, 1)
                for g in range(2):
                    pe.wait_ge(pT_done, at(t, 2, g + 1))
                    if own:
                        pe.wait_ge(v_done, at(t, 4, 2 * g + 2))
                    for half in range(2):
                        bank = (y_bank[g], s_bank[g])[half]
                        for jj in range(2):
                            j = 2 * half + jj
                            rhs = (values[:, g, j * D:(j + 1) * D] if own else
                                   core.ctx_sb[:, bass.ds(t * 2 * G + g * G + j, 1), :].squeeze(1))
                            last = nc.tensor.matmul(bank[:, jj * D:(jj + 1) * D], pT[:, g, j * P:(j + 1) * P], rhs,
                                                    start=True, stop=True)
                    last.then_inc(y_made, 1)

        @block.scalar
        def _(act):
            n_scalar(act)
            with act.Fori(0, TURNS) as t:
                if own:
                    for g in range(2):
                        act.wait_ge(sa_made, at(t, 2, g + 1))
                        nc.scalar.copy(state[0:32, g, :], t_bank[g][0:32, :])
                        nc.scalar.copy(action[0:32, g, :], y_bank[g][0:32, :]).then_inc(sa_done, 1)
                    for g in range(2):
                        for half in range(2):
                            act.wait_ge(v_made, at(t, 4, 2 * g + half + 1))
                            nc.scalar.copy(values[:, g, half * 2 * D:(half + 1) * 2 * D], v_bank[half][:, :]).then_inc(v_done, 1)
                for g in range(2):
                    act.wait_ge(moved, at(t, 2, g + 1))
                    nc.scalar.activation(sm[:, g, :], sm[:, g, :], ACT.Exp, scale=SCALE).then_inc(exp_done, 1)
                for g in range(2):
                    act.wait_ge(p_turned, at(t, 2, g + 1))
                    nc.scalar.copy(pT[:, g, :], t_bank[g][:, :]).then_inc(pT_done, 1)

        @block.vector
        def _(dve):
            n_vector(dve)
            if own:
                dve.wait_ge(core.weights_loaded[name], 16)
                bias = core.constant("causal_bias").unsqueeze(1).to_broadcast([P, G, P])
            else:
                dve.wait_ge(mask_loaded, 16)
                m8 = mask.bitcast(U8).rearrange("p (b t) -> p b t", b=B)
                nc.vector.tensor_scalar(keep, m8, 0.0, None, ALU.not_equal).then_inc(keep_done, 1)
                nc.vector.tensor_scalar(fill, m8, 0.0, -1e30 / SCALE, ALU.is_equal, ALU.mult).then_inc(keep_done, 1)
                dve.wait_ge(keep_done, 2)
                nc.vector.tensor_reduce(valid, keep, AX, ALU.max).then_inc(keep_done, 1)
                dve.wait_ge(keep_done, 3)
            dve.sem_inc(y_added, 2)
            with dve.Fori(0, TURNS) as t:
                for g in range(2):
                    group = bass.ds(t * 2 * G + g * G, G)
                    dve.wait_ge(scores_made, at(t, 2, g + 1))
                    if own:
                        nc.vector.tensor_tensor(quads(sm[:, g, :]), quads(s_bank[g][:, :]), bias, ALU.add).then_inc(filled, 1)
                    else:
                        nc.vector.tensor_tensor(quads(sm[:, g, :]), quads(s_bank[g][:, :]), keep[:, group, :], ALU.mult).then_inc(masked, 1)
                        dve.wait_ge(masked, at(t, 2, g + 1))
                        nc.vector.tensor_tensor(quads(sm[:, g, :]), quads(sm[:, g, :]), fill[:, group, :], ALU.add).then_inc(filled, 1)
                    dve.wait_ge(filled, at(t, 2, g + 1))
                    nc.vector.tensor_reduce(peak[:, g, :], quads(sm[:, g, :]), AX, ALU.max).then_inc(peak_done, 1)
                    dve.wait_ge(peak_done, at(t, 2, g + 1))
                    nc.vector.tensor_tensor(quads(sm[:, g, :]), quads(sm[:, g, :]),
                                            peak[:, g, :].unsqueeze(2).to_broadcast([P, G, P]), ALU.subtract).then_inc(moved, 1)
                for g in range(2):
                    group = bass.ds(t * 2 * G + g * G, G)
                    dve.wait_ge(exp_done, at(t, 2, g + 1))
                    nc.vector.tensor_reduce(total[:, g, :], quads(sm[:, g, :]), AX, ALU.add).then_inc(total_step, 1)
                    steps = 2 if own else 3
                    dve.wait_ge(total_step, at(t, 2 * steps, steps * g + 1))
                    nc.vector.reciprocal(total[:, g, :], total[:, g, :]).then_inc(total_step, 1)
                    dve.wait_ge(total_step, at(t, 2 * steps, steps * g + 2))
                    if not own:
                        nc.vector.tensor_tensor(total[:, g, :], total[:, g, :], valid[:, group], ALU.mult).then_inc(total_step, 1)
                        dve.wait_ge(total_step, at(t, 2 * steps, steps * g + 3))
                    nc.vector.tensor_tensor(quads(sm[:, g, :]), quads(sm[:, g, :]),
                                            total[:, g, :].unsqueeze(2).to_broadcast([P, G, P]), ALU.mult).then_inc(p_done, 1)
                for g in range(2):
                    group = bass.ds(t * 2 * G + g * G, G)
                    dve.wait_ge(y_made, at(t, 2, g + 1))
                    for half in range(2):
                        pair = core.x[:, bass.ds(t * 2 * G + g * G + 2 * half, 2), :]
                        bank = (y_bank[g], s_bank[g])[half]
                        last = nc.vector.tensor_tensor(pair, bank[:, :].rearrange("p (j d) -> p j d", j=2), pair, ALU.add)
                    if own:
                        last.then_inc(b_added, 1)
                        dve.wait_ge(b_added, at(t, 2, g + 1))
                        xg = core.x[:, group, :]
                        last = nc.vector.tensor_tensor(xg, xg, w["bo"].unsqueeze(1).to_broadcast([P, G, D]), ALU.add)
                    last.then_inc(y_added, 1)


def context_attention(core):
    token_attention(core, "L2x")


def state_action_attention(core):
    token_attention(core, "L3a")


def column_cross_attention(core):
    nc = core.nc
    SCALE = 1.0 / 16
    SM = 3
    with ExitStack() as ctx:
        sem = lambda n: core.sem(f"L3x_{n}", ctx)
        carve = core.work("L3x")
        s = norm_state(core, "L3x", carve, ctx, turn_to_features=False)
        xn = core.xnT.rearrange("p k b t -> p (k b t)").rearrange("p (b d) -> p b d", b=B)
        sm = carve(SM, 2 * D)
        peak, total = carve(2, 2), carve(2, 2)
        s_bank, y_bank = core.bank[0:2], core.bank[2:4]
        scores_made, peak_done, moved, exp_done = sem("scores_made"), sem("peak_done"), sem("moved"), sem("exp_done")
        summed, inverted, p_done, y_made, y_added = sem("summed"), sem("inverted"), sem("p_done"), sem("y_made"), sem("y_added")
        block = ctx.enter_context(core.block())
        n_vector, n_gpsimd, _, _ = normalise(core, "L3x", block, s, tokens=xn)
        halves = lambda a: a.rearrange("p (h d) -> p h d", h=2)

        @block.sync
        def _(sp):
            for what in LOADS["L3x"]:
                core.load(sp, what)

        @block.gpsimd
        def _(pool):
            n_gpsimd(pool)

        @block.tensor
        def _(pe):
            for step in range(B + 2):
                if step < B:
                    pe.wait_ge(s["xn_done"], step + 1)
                    if step >= 2:
                        pe.wait_ge(moved, step - 1)
                    for half in range(2):
                        last = nc.tensor.matmul(s_bank[step % 2][:, half * D:(half + 1) * D],
                                                core.ctx_sb[:, step, half * P:(half + 1) * P],
                                                xn[:, step, :], start=True, stop=True)
                    last.then_inc(scores_made, 1)
                if step >= 2:
                    b = step - 2
                    pe.wait_ge(p_done, b + 1)
                    if b >= 2:
                        pe.wait_ge(y_added, b - 1)
                    for half in range(2):
                        last = nc.tensor.matmul(y_bank[b % 2][:, 0:D], core.ctxT[:, half, b, :],
                                                sm[:, b % SM, half * D:(half + 1) * D], start=(half == 0), stop=(half == 1))
                    last.then_inc(y_made, 1)

        @block.scalar
        def _(act):
            for b in range(B):
                act.wait_ge(moved, b + 1)
                nc.scalar.activation(sm[:, b % SM, :], sm[:, b % SM, :], ACT.Exp, scale=SCALE).then_inc(exp_done, 1)

        @block.vector
        def _(dve):
            n_vector(dve)
            for step in range(B + 3):
                if step < B:
                    b = step
                    dve.wait_ge(scores_made, b + 1)
                    nc.vector.tensor_reduce(peak[:, b % 2, :], halves(s_bank[b % 2][:, :]), AX, ALU.max).then_inc(peak_done, 1)
                if step >= 3:
                    b = step - 3
                    dve.wait_ge(y_made, b + 1)
                    nc.vector.tensor_tensor(core.x[:, b, :], y_bank[b % 2][:, 0:D], core.x[:, b, :], ALU.add).then_inc(y_added, 1)
                if step < B:
                    b = step
                    dve.wait_ge(peak_done, b + 1)
                    nc.vector.tensor_tensor(halves(sm[:, b % SM, :]), halves(s_bank[b % 2][:, :]),
                                            peak[:, b % 2, :].unsqueeze(2).to_broadcast([P, 2, D]), ALU.subtract).then_inc(moved, 1)
                if 1 <= step <= B:
                    b = step - 1
                    dve.wait_ge(exp_done, b + 1)
                    nc.vector.tensor_reduce(total[:, b % 2, :], halves(sm[:, b % SM, :]), AX, ALU.add).then_inc(summed, 1)
                    dve.wait_ge(summed, b + 1)
                    nc.vector.reciprocal(total[:, b % 2, :], total[:, b % 2, :]).then_inc(inverted, 1)
                    dve.wait_ge(inverted, b + 1)
                    nc.vector.tensor_tensor(halves(sm[:, b % SM, :]), halves(sm[:, b % SM, :]),
                                            total[:, b % 2, :].unsqueeze(2).to_broadcast([P, 2, D]), ALU.mult).then_inc(p_done, 1)


def start(core):
    nc = core.nc
    with nc.Block() as block:
        @block.sync
        def _(sp):
            sp.dma_start(core.x.rearrange("p b d -> p (b d)"), core.dram["x"]).then_inc(core.x_loaded, 16)
            sp.dma_start(core.const[:, :], core.dram["const"]).then_inc(core.const_loaded, 16)
            for name in FIRST_LOADS:
                core.load(sp, name)
            sp.dma_start(core.ctx_sb.rearrange("p b d -> p (b d)"), core.dram["ctx"]).then_inc(core.ctx_loaded, 16)


def finish(core, out):
    nc = core.nc
    with ExitStack() as ctx:
        stored = core.sem("stored", ctx)
        block = ctx.enter_context(nc.Block())

        @block.sync
        def _(sp):
            sp.dma_start(out, core.x.rearrange("p b d -> p (b d)")).then_inc(stored, 16)
            sp.wait_ge(stored, 16)


FIRST_LOADS = ["L0a", "L0x"]
PHASES = [lightning_attention, channel_cross_attention, experts_0,
          power_attention, rotary_cross_attention, lora_experts,
          sink_attention, context_attention, experts_2,
          state_action_attention, column_cross_attention, experts_3]


CONST_AT = {}
WEIGHT_PARTS = {"L0a": [], "L0x": [], "L0f": [], "L1a": [], "L1x": [], "L1f": [], "L2a": [], "L2f": [],
                "L2x": [], "L3a": [], "L3x": [], "L3f": [], "L3sel": []}


def constants():
    i = np.arange(P)
    s, t = i[:, None], i[None, :]

    def rope(half, base, dim):
        return np.outer(i.astype(np.float32),
                        (1.0 / np.float32(base) ** (np.arange(0, dim, 2, dtype=np.float32) / dim)).astype(np.float32)[:half])

    parts = {
        "ident": np.eye(P), "ones": np.ones((P, P)),
        "causalT": (s <= t) * 1.0,
        "causal_bias": np.where(t > s, -1e30, 0.0),
        "causal_cap": np.where(s <= t, 0.0, -1e30),
        "dist": np.maximum(t - s, 0),
    }
    c, pos = i % 8, np.arange(D, dtype=np.float32)
    theta = (1.0 / np.float32(10000.0) ** (np.arange(0, 4, 2, dtype=np.float32) / 4)).astype(np.float32)
    angle = pos[None, :] * theta[c % 2][:, None]
    parts["cos0"] = np.where(c[:, None] < 4, np.cos(angle), 1.0)
    parts["sin0"] = np.where(c[:, None] < 4, np.sin(angle), 0.0)
    turn = np.zeros((P, P))
    for p in range(P):
        if p % 8 < 2:
            turn[p + 2, p] = -1.0
        elif p % 8 < 4:
            turn[p - 2, p] = 1.0
    parts["turn0"] = turn
    parts["headmask"] = np.stack([(i // 8 == 4 * g + n) * 1.0 for n in range(4) for g in range(4)], 1)
    f1 = rope(64, 10000.0, 128)
    parts["cos1"], parts["sin1"] = np.cos(f1), np.sin(f1)
    f2 = i[:, None].astype(np.float32) * (1.0 / np.float32(150000.0) ** (np.arange(32, dtype=np.float32) * 2.0 / 64)).astype(np.float32)
    parts["cos2"], parts["sin2"] = np.cos(f2), np.sin(f2)
    at_col = 0
    for name, a in parts.items():
        CONST_AT[name] = (at_col, at_col + a.shape[1])
        at_col += a.shape[1]
    return np.ascontiguousarray(np.concatenate([a.astype(np.float32) for a in parts.values()], 1))


def rows(w):
    w = np.asarray(w)
    k = -(-w.shape[0] // P)
    w = np.concatenate([w, np.zeros((k * P - w.shape[0], w.shape[1]), w.dtype)]) if k * P > w.shape[0] else w
    return w.reshape(k, P, -1).transpose(1, 0, 2).reshape(P, -1)


def on_top(w):
    w = np.asarray(w)
    return np.concatenate([w, np.zeros((P - w.shape[0], w.shape[1]), w.dtype)])


def spread(v):
    v = np.asarray(v).reshape(1, -1)
    return np.broadcast_to(v, (P, v.shape[1]))


def selector(groups, width, size):
    return (np.arange(width)[None, :] // size == np.arange(groups)[:, None]).astype(np.float32)


def pack(name, parts):
    at_col, WEIGHT_PARTS[name][:] = 0, []
    for part, a in parts.items():
        WEIGHT_PARTS[name].append((part, at_col, at_col + a.shape[1]))
        at_col += a.shape[1]
    return np.ascontiguousarray(np.concatenate(list(parts.values()), 1))


def arrays_of(i):
    T = np.transpose
    i = {k: np.asarray(v) for k, v in i.items()}
    out = {"const": constants()}
    out["x"] = np.ascontiguousarray(i["x"].transpose(1, 0, 2)).reshape(P, B * D)
    out["ctx"] = np.ascontiguousarray(i["ctx_2048"].transpose(1, 0, 2)).reshape(P, B * D)
    out["chanmask"] = spread(np.concatenate([np.arange(32) // 8 == n for n in range(4)])).astype(np.float32)
    out["attn_mask"] = np.ascontiguousarray(i["mask_1x1x2048x2048_if1"].reshape(2, P, D).transpose(1, 0, 2)).reshape(P, 2 * D)
    out["memory_mask"] = np.ascontiguousarray(i["mask_BxS2_bk0"].reshape(1, B * P))
    out["w_L0a"] = pack("L0a", {
        "qkv": rows(T(i["L0_attn_w_qkv"])), "gate": rows(T(i["L0_attn_w_gate"])), "out": rows(T(i["L0_attn_w_out"])),
        "norm": rows(i["L0_attn_norm_w"].reshape(-1, 1)), "slope": spread(i["L0_attn_slope_rate"])})
    col = lambda v: rows(np.asarray(v).reshape(-1, 1))
    out["w_L0x"] = pack("L0x", {
        "q": T(i["L0_xattn_wq"]), "k": T(i["L0_xattn_wk"]), "v": T(i["L0_xattn_wv"]), "o": T(i["L0_xattn_wo"]),
        "bq": col(i["L0_xattn_bq"]), "bk": col(i["L0_xattn_bk"]), "bo": col(i["L0_xattn_bo"]), "bv": spread(i["L0_xattn_bv"])})
    wide = lambda w, f: np.concatenate([w, np.zeros((w.shape[0], f - w.shape[1]), w.dtype)], 1)
    hidden = lambda e, sh, f: rows(wide(np.concatenate([T(e.reshape(-1, D)), T(sh)], 1), f))
    down = lambda e, sh: rows(np.concatenate([e.transpose(0, 2, 1).reshape(-1, D), T(sh)], 0))
    out["w_L0f"] = pack("L0f", {
        "router": rows(T(i["L0_ffn_gate_w"])),
        "gate": hidden(i["L0_ffn_exp_wg"], i["L0_ffn_shared_wg"], 14 * P),
        "up": hidden(i["L0_ffn_exp_wu"], i["L0_ffn_shared_wu"], 14 * P),
        "down": down(i["L0_ffn_exp_wd"], i["L0_ffn_shared_wd"]), "select": on_top(selector(8, 11 * P, 176))})
    w1, s1 = i["L3_ffn_w1"], i["L3_ffn_shared_w1"]
    out["w_L3f"] = pack("L3f", {
        "router": rows(T(i["L3_ffn_gate_w"])),
        "gate": hidden(w1[:, :176], s1[:352], 25 * P), "up": hidden(w1[:, 176:], s1[352:], 25 * P),
        "down": down(i["L3_ffn_w2"], i["L3_ffn_shared_w2"])})
    out["w_L3sel"] = pack("L3sel", {"select": on_top(selector(16, 22 * P, 176))})
    out["w_L2f"] = pack("L2f", {
        "router": rows(T(i["L2_ffn_Wg"])), "gate": rows(T(i["L2_ffn_A"].reshape(-1, D))),
        "down": rows(i["L2_ffn_Bw"].transpose(0, 2, 1).reshape(-1, D)), "select": on_top(selector(8, 4 * P, 64))})
    out["w_L1a"] = pack("L1a", {
        "q": rows(i["L1_attn_Wq"]), "k": rows(i["L1_attn_Wk"]), "v": rows(i["L1_attn_Wv"]), "g": rows(i["L1_attn_Wg"]),
        "c": rows(i["L1_attn_Wc"]), "bc": spread(i["L1_attn_bc"])})
    out["w_L1x"] = pack("L1x", {
        **{n: rows(i["L1_xattn_" + m]) for n, m in (("q", "wq"), ("k", "wk"), ("v", "wv"), ("kc", "wk_ctx"), ("vc", "wv_ctx"), ("o", "wo"))},
        "qn": spread(i["L1_xattn_q_norm_w"]), "kn": spread(i["L1_xattn_k_norm_w"])})
    def paired(q):
        q = q.reshape(*q.shape[:-2], 4, 2, 4, 64)
        q = np.swapaxes(q, -3, -2)
        return evens_first(q).reshape(*q.shape[:-4], 2048)

    def evens_first(q):
        q = q.reshape(*q.shape[:-1], 32, 2)
        return np.swapaxes(q, -1, -2).reshape(*q.shape[:-2], 64)

    kvs = lambda k: evens_first(k).reshape(*k.shape[:-2], 512)
    o = i["L2_attn_Wo"].reshape(4, 2, 4, 64, D).transpose(0, 2, 1, 3, 4).reshape(2048, D)
    out["w_L2a"] = pack("L2a", {
        "q": rows(paired(i["L2_attn_Wq"])), "k": rows(kvs(i["L2_attn_Wk"])), "v": rows(i["L2_attn_Wv"].reshape(D, 512)),
        "o": rows(o), "bq": spread(paired(i["L2_attn_bq"])), "bk": spread(kvs(i["L2_attn_bk"])),
        "bv": spread(i["L2_attn_bv"]), "bo": spread(i["L2_attn_bo"]), "sinks": spread(i["L2_attn_sinks"])})
    f = 6 * P
    rank = lambda a, sh: np.concatenate([a.transpose(1, 0, 2).reshape(a.shape[1], -1), sh], 1)
    back = lambda b, sh: np.concatenate([b.reshape(-1, b.shape[2]), sh], 0)
    g = {n[7:]: v for n, v in i.items() if n.startswith("L1_ffn_")}
    out["w_L1f"] = pack("L1f", {
        "router": rows(g["W_router"]), "bias": spread(g["expert_bias"]),
        "gate": rows(wide(g["W_gate"], f)), "up": rows(wide(g["W_up"], f)), "down": rows(g["W_down"]),
        "a_gate": rows(rank(g["A_gate"], g["sA_gate"])), "a_up": rows(rank(g["A_up"], g["sA_up"])),
        "a_down": rows(rank(g["A_down"], g["sA_down"])),
        "b_gate": on_top(wide(back(g["B_gate"], g["sB_gate"]), f)), "b_up": on_top(wide(back(g["B_up"], g["sB_up"]), f)),
        "b_down": on_top(back(g["B_down"], g["sB_down"])), "select": on_top(selector(9, 72, 8))})
    out["w_L3a"] = pack("L3a", {
        "s": rows(i["L3_attn_Ws"]), "a": rows(i["L3_attn_Wa"]), "o": rows(T(i["L3_attn_Wo"])), "bo": spread(i["L3_attn_bo"])})
    return out


def program(nc, arrays, out, phases):
    dram = {name: nc.dram_tensor(f"in_{name}", a.shape, mybir.dt.from_np(a.dtype), kind="ExternalInput").ap()
            for name, a in arrays.items()}
    with ExitStack() as ctx:
        core = Core(nc, ctx, dram)
        start(core)
        for phase in phases:
            phase(core)
        finish(core, out)


def kernel(**inputs):
    import concourse.bacc as _bacc
    from concourse.bass_utils import run_bass_kernel_spmd as _run

    nc = _bacc.Bacc("TRN2", target_bir_lowering=False, num_devices=1)
    arrays = arrays_of(inputs)
    out = nc.dram_tensor("out_x", (P, B * D), F32, kind="ExternalOutput").ap()
    program(nc, arrays, out, PHASES)
    r = _run(nc, [{f"in_{k}": v for k, v in arrays.items()}], core_ids=[0])
    return r.results[0]["out_x"].reshape(P, B, D).transpose(1, 0, 2)
```
